# Optimizing a Trainium2 kernel written in Bass

```python
import numpy as np
import jax
import jax.numpy as jnp

def _softmax(x, axis=-1):
    return jax.nn.softmax(x, axis=axis)

def _gelu(x):
    return jax.nn.gelu(x, approximate=True)

def _silu(x):
    return jax.nn.silu(x)

def _sigmoid(x):
    return jax.nn.sigmoid(x)

def _layernorm(x, axis=-1, eps=1e-05):
    m = jnp.mean(x, axis=axis, keepdims=True)
    v = jnp.var(x, axis=axis, keepdims=True)
    return (x - m) / jnp.sqrt(v + eps)

def _scatter_add(tgt, idx, src, axis=0):
    return tgt.at[idx].add(src)

def _segment_sum(src, seg, n):
    return jax.ops.segment_sum(src, seg, n)
kernel_name = 'mk_recurrent_d4_jaxref_r8_f1b6e8'

def setup_inputs(seed: int=0):
    np.random.seed(seed)
    _w = jnp.asarray

    def _L0_attn_setup():
        import jax, jax.numpy as jnp
        import numpy as np
        B, S, HID, NH = (8, 512, 128, 16)
        D = HID // NH
        LN_EPS = 1e-05

        def _l2norm(a):
            n = jnp.sqrt(jnp.sum(a * a, axis=-1, keepdims=True))
            return a / jnp.maximum(n, 1e-12)
        key = jax.random.key(seed)
        ks = jax.random.split(key, 8)
        s = 0.02
        x = jax.random.normal(ks[0], (B, S, HID), jnp.float32)
        Wq = jax.random.normal(ks[1], (HID, NH * D), jnp.float32) * s
        Wk = jax.random.normal(ks[2], (HID, NH * D), jnp.float32) * s
        Wv = jax.random.normal(ks[3], (HID, NH * D), jnp.float32) * s
        Wbeta = jax.random.normal(ks[4], (HID, NH), jnp.float32) * s
        Wg = jax.random.normal(ks[5], (HID, NH * D), jnp.float32) * s
        Wout = jax.random.normal(ks[6], (NH * D, HID), jnp.float32) * s
        ln_g = jnp.ones((NH * D,), jnp.float32)
        ln_b = jnp.zeros((NH * D,), jnp.float32)
        return {'x': x, 'Wq': Wq, 'Wk': Wk, 'Wv': Wv, 'Wbeta': Wbeta, 'Wg': Wg, 'Wout': Wout, 'ln_g': ln_g, 'ln_b': ln_b}
    _L0_attn_in = _L0_attn_setup()

    def _L0_ffn_setup():
        import jax, jax.numpy as jnp
        import numpy as np
        B, S, DIM = (4, 512, 128)
        BASE_COUPLING = 0.1
        NUM_CYCLES = 3

        def _gelu(x):
            return jax.nn.gelu(x, approximate=False)

        def _coupling_net(h, w1, b1, w2, b2, w3, b3, w4, b4):
            h = _gelu(h @ w1 + b1)
            h = _gelu(h @ w2 + b2)
            h = _gelu(h @ w3 + b3)
            return jax.nn.sigmoid(h @ w4 + b4)

        def _global_net(h, w1, b1, w2, b2, w3, b3):
            h = _gelu(h @ w1 + b1)
            h = _gelu(h @ w2 + b2)
            return jax.nn.sigmoid(h @ w3 + b3)

        def _twist(x):
            o_r, o_i, p_r, p_i = jnp.split(x, 4, axis=-1)
            return jnp.concatenate([p_r, -p_i, -o_r, o_i], axis=-1)
        key = jax.random.key(seed)
        ks = jax.random.split(key, 9)
        d = DIM

        def w(k, fan_in, fan_out):
            return jax.random.normal(k, (fan_in, fan_out), dtype=jnp.float32) / np.sqrt(fan_in).astype(np.float32)
        inp = {'x': jax.random.normal(ks[0], (B, S, d), dtype=jnp.float32)}
        cn_dims = [(d, d), (d, d // 2), (d // 2, d // 4), (d // 4, 1)]
        for i, (a, b) in enumerate(cn_dims):
            inp[f'cn_w{i + 1}'] = w(ks[1 + i], a, b)
            inp[f'cn_b{i + 1}'] = jnp.zeros((b,), dtype=jnp.float32)
        gc_dims = [(d, d // 2), (d // 2, d // 4), (d // 4, 1)]
        for i, (a, b) in enumerate(gc_dims):
            inp[f'gc_w{i + 1}'] = w(ks[5 + i], a, b)
            inp[f'gc_b{i + 1}'] = jnp.zeros((b,), dtype=jnp.float32)
        inp['adaptive_range'] = jnp.full((1,), 0.2, dtype=jnp.float32)
        return inp
    _L0_ffn_in = _L0_ffn_setup()

    def _L1_attn_setup():
        import jax, jax.numpy as jnp
        import numpy as np
        DECAY = 0.95
        EPS = 1e-05
        B, T, D, L = (4, 512, 128, 2)

        def _layer_norm(x, w, b):
            mu = jnp.mean(x, axis=-1, keepdims=True)
            var = jnp.mean(jnp.square(x - mu), axis=-1, keepdims=True)
            return (x - mu) * jax.lax.rsqrt(var + EPS) * w + b

        def _time_mix_layer(x, ln_w, ln_b, Wk, Wv, Wr, Wo):
            normed = _layer_norm(x, ln_w, ln_b)
            k = jnp.einsum('btd,ed->bte', normed, Wk)
            v = jnp.einsum('btd,ed->bte', normed, Wv)
            r = jax.nn.sigmoid(jnp.einsum('btd,ed->bte', normed, Wr))
            kv = k * v

            def step(state, kv_t):
                state = DECAY * state + (1.0 - DECAY) * kv_t
                return (state, state)
            init = jnp.zeros((x.shape[0], x.shape[2]), dtype=x.dtype)
            _, states = jax.lax.scan(step, init, jnp.swapaxes(kv, 0, 1))
            y = r * jnp.swapaxes(states, 0, 1)
            y = jnp.einsum('btd,ed->bte', y, Wo)
            return x + y
        key = jax.random.key(seed)
        ks = jax.random.split(key, 7)
        scale = 1.0 / np.sqrt(D)
        return {'h': jax.random.normal(ks[0], (B, T, D), dtype=jnp.float32), 'ln_w': jnp.ones((L, D), dtype=jnp.float32), 'ln_b': jnp.zeros((L, D), dtype=jnp.float32), 'Wk': jax.random.normal(ks[1], (L, D, D), dtype=jnp.float32) * scale, 'Wv': jax.random.normal(ks[2], (L, D, D), dtype=jnp.float32) * scale, 'Wr': jax.random.normal(ks[3], (L, D, D), dtype=jnp.float32) * scale, 'Wo': jax.random.normal(ks[4], (L, D, D), dtype=jnp.float32) * scale}
    _L1_attn_in = _L1_attn_setup()

    def _L1_ffn_setup():
        import jax, jax.numpy as jnp
        import numpy as np
        DIM = 128
        DEPTH = 2
        HEADS = 8
        DIM_HEAD = 64
        WINDOW = 64
        INNER = HEADS * DIM_HEAD
        HID = int(DIM * 4 * 2 / 3)
        B, N = (2, 1024)
        QK_SCALE = 8.0

        def shift_token(t):
            t1, t2 = jnp.split(t, 2, axis=-1)
            t2 = jnp.pad(t2, ((0, 0), (1, 0), (0, 0)))[:, :-1]
            return jnp.concatenate([t1, t2], axis=-1)

        def l2norm(t):
            return t / jnp.clip(jnp.linalg.norm(t, axis=-1, keepdims=True), 1e-12)

        def rotate_half(x):
            x1, x2 = jnp.split(x, 2, axis=-1)
            return jnp.concatenate([-x2, x1], axis=-1)

        def rotary_xpos(q, k):
            n = q.shape[-2]
            half_idx = jnp.arange(0, DIM_HEAD, 2, dtype=jnp.float32)
            inv_freq = 1.0 / 10000.0 ** (half_idx / DIM_HEAD)
            t = jnp.arange(n, dtype=jnp.float32)
            freqs = t[:, None] * inv_freq[None, :]
            freqs = jnp.concatenate([freqs, freqs], axis=-1)
            base = (half_idx + 0.4 * DIM_HEAD) / (1.4 * DIM_HEAD)
            power = (t - n // 2) / float(WINDOW // 2)
            scale = base[None, :] ** power[:, None]
            scale = jnp.concatenate([scale, scale], axis=-1)
            cos, sin = (jnp.cos(freqs), jnp.sin(freqs))
            q = q * cos * scale + rotate_half(q) * sin * scale
            k = k * cos / scale + rotate_half(k) * sin / scale
            return (q, k)

        def local_attention(q, k, v):
            b, h, n, d = q.shape
            w = n // WINDOW
            bq = q.reshape(b, h, w, WINDOW, d) * QK_SCALE
            bk = k.reshape(b, h, w, WINDOW, d)
            bv = v.reshape(b, h, w, WINDOW, d)

            def look_around(t):
                p = jnp.pad(t, ((0, 0), (0, 0), (1, 0), (0, 0), (0, 0)))
                return jnp.concatenate([p[:, :, :w], p[:, :, 1:]], axis=3)
            bk, bv = (look_around(bk), look_around(bv))
            bt = jnp.arange(n).reshape(w, WINDOW)
            btp = jnp.pad(bt, ((1, 0), (0, 0)), constant_values=-1)
            btk = jnp.concatenate([btp[:w], btp[1:]], axis=1)
            sim = jnp.einsum('bhwid,bhwjd->bhwij', bq, bk)
            i = bt[:, :, None]
            j = btk[:, None, :]
            mask = (i < j) | (i > j + WINDOW) | (j == -1)
            sim = jnp.where(mask, -jnp.finfo(sim.dtype).max, sim)
            attn = jax.nn.softmax(sim, axis=-1)
            out = jnp.einsum('bhwij,bhwjd->bhwid', attn, bv)
            return out.reshape(b, h, n, d)

        def _layer(x, wqkv, qs, ksc, wo, lg, lb, w1, b1, w2, b2):
            b, n, _ = x.shape
            h = shift_token(x)
            qkv = h @ wqkv
            q, k, v = jnp.split(qkv, 3, axis=-1)
            to_heads = lambda t: t.reshape(b, n, HEADS, DIM_HEAD).transpose(0, 2, 1, 3)
            q, k, v = (to_heads(q), to_heads(k), to_heads(v))
            q = l2norm(q) * qs
            k = l2norm(k) * ksc
            q, k = rotary_xpos(q, k)
            o = local_attention(q, k, v)
            o = o.transpose(0, 2, 1, 3).reshape(b, n, INNER)
            x = x + o @ wo
            h = shift_token(x)
            mu = h.mean(-1, keepdims=True)
            var = h.var(-1, keepdims=True)
            h = (h - mu) / jnp.sqrt(var + 1e-05) * lg + lb
            h = h @ w1 + b1
            a, g = jnp.split(h, 2, axis=-1)
            h = a * jax.nn.gelu(g, approximate=False)
            x = x + h @ w2 + b2
            return x
        key = jax.random.key(seed)
        ks = jax.random.split(key, 6)
        return {'x': jax.random.normal(ks[0], (B, N, DIM), jnp.float32), 'wqkv': jax.random.normal(ks[1], (DEPTH, DIM, 3 * INNER), jnp.float32) * 0.02, 'q_scale': jnp.ones((DEPTH, DIM_HEAD), jnp.float32), 'k_scale': jnp.ones((DEPTH, DIM_HEAD), jnp.float32), 'wo': jax.random.normal(ks[2], (DEPTH, INNER, DIM), jnp.float32) * 0.02, 'ln_g': jnp.ones((DEPTH, DIM), jnp.float32), 'ln_b': jnp.zeros((DEPTH, DIM), jnp.float32), 'w1': jax.random.normal(ks[3], (DEPTH, DIM, 2 * HID), jnp.float32) * 0.02, 'b1': jnp.zeros((DEPTH, 2 * HID), jnp.float32), 'w2': jax.random.normal(ks[4], (DEPTH, HID, DIM), jnp.float32) * 0.02, 'b2': jnp.zeros((DEPTH, DIM), jnp.float32)}
    _L1_ffn_in = _L1_ffn_setup()

    def _L2_attn_setup():
        import jax, jax.numpy as jnp
        import numpy as np
        from jax import lax
        H = 128
        EXPAND = 2
        I = EXPAND * H
        N = 16
        K = 4
        R = 64
        EPS = 1e-06
        B_SZ, L = (2, 128)

        def rmsnorm(x, w):
            v = jnp.mean(x.astype(jnp.float32) ** 2, axis=-1, keepdims=True)
            return w * (x * jax.lax.rsqrt(v + EPS)).astype(x.dtype)
        key = jax.random.key(seed)
        ks = jax.random.split(key, 10)
        s = 0.02
        inp = {'hidden_states': jax.random.normal(ks[0], (B_SZ, L, H), jnp.float32), 'in_proj_w': jax.random.normal(ks[1], (2 * I, H), jnp.float32) * s, 'conv_w': jax.random.normal(ks[2], (I, 1, K), jnp.float32) * s, 'conv_b': jnp.zeros((I,), jnp.float32), 'x_proj_w': jax.random.normal(ks[3], (R + 2 * N, I), jnp.float32) * s, 'dt_proj_w': jax.random.normal(ks[4], (I, R), jnp.float32) * s, 'dt_proj_b': jax.random.normal(ks[5], (I,), jnp.float32) * 0.1, 'dt_ln_w': jnp.ones((R,), jnp.float32), 'b_ln_w': jnp.ones((N,), jnp.float32), 'c_ln_w': jnp.ones((N,), jnp.float32), 'A_log': jnp.log(jnp.broadcast_to(jnp.arange(1, N + 1, dtype=jnp.float32)[None, :], (I, N))), 'D': jnp.ones((I,), jnp.float32), 'out_proj_w': jax.random.normal(ks[6], (H, I), jnp.float32) * s}
        return inp
    _L2_attn_in = _L2_attn_setup()

    def _L2_ffn_setup():
        import jax, jax.numpy as jnp
        import numpy as np
        B, S, D, F, E, K = (4, 256, 128, 512, 4, 2)
        key = jax.random.key(seed)
        k = jax.random.split(key, 6)
        x = jax.random.normal(k[0], (B, S, D), jnp.float32)
        router_w = jax.random.normal(k[1], (D, E), jnp.float32) * D ** (-0.5)
        router_b = jnp.zeros((E,), jnp.float32)
        w1 = jax.random.normal(k[2], (E, D, F), jnp.float32) * 0.02
        w3 = jax.random.normal(k[3], (E, D, F), jnp.float32) * 0.02
        w2 = jax.random.normal(k[4], (E, F, D), jnp.float32) * 0.02
        return {'x': x, 'router_w': router_w, 'router_b': router_b, 'w1': w1, 'w3': w3, 'w2': w2}
    _L2_ffn_in = _L2_ffn_setup()

    def _L3_attn_setup():
        import jax, jax.numpy as jnp
        import numpy as np
        H = 16
        TOPK_RATIO = 0.05
        LN_EPS = 1e-05

        def _layernorm(t, gamma, beta):
            mu = t.mean(-1, keepdims=True)
            var = t.var(-1, keepdims=True)
            return (t - mu) * jax.lax.rsqrt(var + LN_EPS) * gamma + beta
        key = jax.random.key(seed)
        ks = jax.random.split(key, 4)
        B, N, C = (2, 256, 128)
        x = jax.random.normal(ks[0], (B, N, C), dtype=jnp.float32)
        Wqkv = jax.random.normal(ks[1], (3 * C, C), dtype=jnp.float32) * (1.0 / np.sqrt(C))
        Wproj = jax.random.normal(ks[2], (C, C), dtype=jnp.float32) * (1.0 / np.sqrt(C))
        return {'x': x, 'Wqkv': Wqkv, 'bqkv': jnp.zeros((3 * C,), jnp.float32), 'q_gamma': jnp.ones((C // H,), jnp.float32), 'q_beta': jnp.zeros((C // H,), jnp.float32), 'k_gamma': jnp.ones((C // H,), jnp.float32), 'k_beta': jnp.zeros((C // H,), jnp.float32), 'alpha': jnp.full((H,), 0.5, jnp.float32), 'Wproj': Wproj, 'bproj': jnp.zeros((C,), jnp.float32)}
    _L3_attn_in = _L3_attn_setup()

    def _L3_ffn_setup():
        import jax, jax.numpy as jnp
        import numpy as np
        B, S, DIM = (4, 512, 128)
        BASE_COUPLING = 0.1
        NUM_CYCLES = 3

        def _gelu(x):
            return jax.nn.gelu(x, approximate=False)

        def _coupling_net(h, w1, b1, w2, b2, w3, b3, w4, b4):
            h = _gelu(h @ w1 + b1)
            h = _gelu(h @ w2 + b2)
            h = _gelu(h @ w3 + b3)
            return jax.nn.sigmoid(h @ w4 + b4)

        def _global_net(h, w1, b1, w2, b2, w3, b3):
            h = _gelu(h @ w1 + b1)
            h = _gelu(h @ w2 + b2)
            return jax.nn.sigmoid(h @ w3 + b3)

        def _twist(x):
            o_r, o_i, p_r, p_i = jnp.split(x, 4, axis=-1)
            return jnp.concatenate([p_r, -p_i, -o_r, o_i], axis=-1)
        key = jax.random.key(seed)
        ks = jax.random.split(key, 9)
        d = DIM

        def w(k, fan_in, fan_out):
            return jax.random.normal(k, (fan_in, fan_out), dtype=jnp.float32) / np.sqrt(fan_in).astype(np.float32)
        inp = {'x': jax.random.normal(ks[0], (B, S, d), dtype=jnp.float32)}
        cn_dims = [(d, d), (d, d // 2), (d // 2, d // 4), (d // 4, 1)]
        for i, (a, b) in enumerate(cn_dims):
            inp[f'cn_w{i + 1}'] = w(ks[1 + i], a, b)
            inp[f'cn_b{i + 1}'] = jnp.zeros((b,), dtype=jnp.float32)
        gc_dims = [(d, d // 2), (d // 2, d // 4), (d // 4, 1)]
        for i, (a, b) in enumerate(gc_dims):
            inp[f'gc_w{i + 1}'] = w(ks[5 + i], a, b)
            inp[f'gc_b{i + 1}'] = jnp.zeros((b,), dtype=jnp.float32)
        inp['adaptive_range'] = jnp.full((1,), 0.2, dtype=jnp.float32)
        return inp
    _L3_ffn_in = _L3_ffn_setup()
    _d = {'L0_attn_x': _L0_attn_in['x'], 'L0_attn_Wq': _L0_attn_in['Wq'], 'L0_attn_Wk': _L0_attn_in['Wk'], 'L0_attn_Wv': _L0_attn_in['Wv'], 'L0_attn_Wbeta': _L0_attn_in['Wbeta'], 'L0_attn_Wg': _L0_attn_in['Wg'], 'L0_attn_Wout': _L0_attn_in['Wout'], 'L0_attn_ln_g': _L0_attn_in['ln_g'], 'L0_attn_ln_b': _L0_attn_in['ln_b'], 'L0_ffn_cn_w1': _L0_ffn_in['cn_w1'], 'L0_ffn_cn_b1': _L0_ffn_in['cn_b1'], 'L0_ffn_cn_w2': _L0_ffn_in['cn_w2'], 'L0_ffn_cn_b2': _L0_ffn_in['cn_b2'], 'L0_ffn_cn_w3': _L0_ffn_in['cn_w3'], 'L0_ffn_cn_b3': _L0_ffn_in['cn_b3'], 'L0_ffn_cn_w4': _L0_ffn_in['cn_w4'], 'L0_ffn_cn_b4': _L0_ffn_in['cn_b4'], 'L0_ffn_gc_w1': _L0_ffn_in['gc_w1'], 'L0_ffn_gc_b1': _L0_ffn_in['gc_b1'], 'L0_ffn_gc_w2': _L0_ffn_in['gc_w2'], 'L0_ffn_gc_b2': _L0_ffn_in['gc_b2'], 'L0_ffn_gc_w3': _L0_ffn_in['gc_w3'], 'L0_ffn_gc_b3': _L0_ffn_in['gc_b3'], 'L0_ffn_adaptive_range': _L0_ffn_in['adaptive_range'], 'L1_attn_ln_w': _L1_attn_in['ln_w'], 'L1_attn_ln_b': _L1_attn_in['ln_b'], 'L1_attn_Wk': _L1_attn_in['Wk'], 'L1_attn_Wv': _L1_attn_in['Wv'], 'L1_attn_Wr': _L1_attn_in['Wr'], 'L1_attn_Wo': _L1_attn_in['Wo'], 'L1_ffn_wqkv': _L1_ffn_in['wqkv'], 'L1_ffn_q_scale': _L1_ffn_in['q_scale'], 'L1_ffn_k_scale': _L1_ffn_in['k_scale'], 'L1_ffn_wo': _L1_ffn_in['wo'], 'L1_ffn_ln_g': _L1_ffn_in['ln_g'], 'L1_ffn_ln_b': _L1_ffn_in['ln_b'], 'L1_ffn_w1': _L1_ffn_in['w1'], 'L1_ffn_b1': _L1_ffn_in['b1'], 'L1_ffn_w2': _L1_ffn_in['w2'], 'L1_ffn_b2': _L1_ffn_in['b2'], 'L2_attn_in_proj_w': _L2_attn_in['in_proj_w'], 'L2_attn_conv_w': _L2_attn_in['conv_w'], 'L2_attn_conv_b': _L2_attn_in['conv_b'], 'L2_attn_x_proj_w': _L2_attn_in['x_proj_w'], 'L2_attn_dt_proj_w': _L2_attn_in['dt_proj_w'], 'L2_attn_dt_proj_b': _L2_attn_in['dt_proj_b'], 'L2_attn_dt_ln_w': _L2_attn_in['dt_ln_w'], 'L2_attn_b_ln_w': _L2_attn_in['b_ln_w'], 'L2_attn_c_ln_w': _L2_attn_in['c_ln_w'], 'L2_attn_A_log': _L2_attn_in['A_log'], 'L2_attn_D': _L2_attn_in['D'], 'L2_attn_out_proj_w': _L2_attn_in['out_proj_w'], 'L2_ffn_router_w': _L2_ffn_in['router_w'], 'L2_ffn_router_b': _L2_ffn_in['router_b'], 'L2_ffn_w1': _L2_ffn_in['w1'], 'L2_ffn_w3': _L2_ffn_in['w3'], 'L2_ffn_w2': _L2_ffn_in['w2'], 'L3_attn_Wqkv': _L3_attn_in['Wqkv'], 'L3_attn_bqkv': _L3_attn_in['bqkv'], 'L3_attn_q_gamma': _L3_attn_in['q_gamma'], 'L3_attn_q_beta': _L3_attn_in['q_beta'], 'L3_attn_k_gamma': _L3_attn_in['k_gamma'], 'L3_attn_k_beta': _L3_attn_in['k_beta'], 'L3_attn_alpha': _L3_attn_in['alpha'], 'L3_attn_Wproj': _L3_attn_in['Wproj'], 'L3_attn_bproj': _L3_attn_in['bproj'], 'L3_ffn_cn_w1': _L3_ffn_in['cn_w1'], 'L3_ffn_cn_b1': _L3_ffn_in['cn_b1'], 'L3_ffn_cn_w2': _L3_ffn_in['cn_w2'], 'L3_ffn_cn_b2': _L3_ffn_in['cn_b2'], 'L3_ffn_cn_w3': _L3_ffn_in['cn_w3'], 'L3_ffn_cn_b3': _L3_ffn_in['cn_b3'], 'L3_ffn_cn_w4': _L3_ffn_in['cn_w4'], 'L3_ffn_cn_b4': _L3_ffn_in['cn_b4'], 'L3_ffn_gc_w1': _L3_ffn_in['gc_w1'], 'L3_ffn_gc_b1': _L3_ffn_in['gc_b1'], 'L3_ffn_gc_w2': _L3_ffn_in['gc_w2'], 'L3_ffn_gc_b2': _L3_ffn_in['gc_b2'], 'L3_ffn_gc_w3': _L3_ffn_in['gc_w3'], 'L3_ffn_gc_b3': _L3_ffn_in['gc_b3'], 'L3_ffn_adaptive_range': _L3_ffn_in['adaptive_range']}
    _x0 = _d['L0_attn_x']
    _d['L0_attn_x'] = jax.random.normal(jax.random.fold_in(jax.random.key(seed), 1), (8, 512, 128), dtype=_x0.dtype)
    del _x0
    return _d

def reference(L0_attn_x, L0_attn_Wq, L0_attn_Wk, L0_attn_Wv, L0_attn_Wbeta, L0_attn_Wg, L0_attn_Wout, L0_attn_ln_g, L0_attn_ln_b, L0_ffn_cn_w1, L0_ffn_cn_b1, L0_ffn_cn_w2, L0_ffn_cn_b2, L0_ffn_cn_w3, L0_ffn_cn_b3, L0_ffn_cn_w4, L0_ffn_cn_b4, L0_ffn_gc_w1, L0_ffn_gc_b1, L0_ffn_gc_w2, L0_ffn_gc_b2, L0_ffn_gc_w3, L0_ffn_gc_b3, L0_ffn_adaptive_range, L1_attn_ln_w, L1_attn_ln_b, L1_attn_Wk, L1_attn_Wv, L1_attn_Wr, L1_attn_Wo, L1_ffn_wqkv, L1_ffn_q_scale, L1_ffn_k_scale, L1_ffn_wo, L1_ffn_ln_g, L1_ffn_ln_b, L1_ffn_w1, L1_ffn_b1, L1_ffn_w2, L1_ffn_b2, L2_attn_in_proj_w, L2_attn_conv_w, L2_attn_conv_b, L2_attn_x_proj_w, L2_attn_dt_proj_w, L2_attn_dt_proj_b, L2_attn_dt_ln_w, L2_attn_b_ln_w, L2_attn_c_ln_w, L2_attn_A_log, L2_attn_D, L2_attn_out_proj_w, L2_ffn_router_w, L2_ffn_router_b, L2_ffn_w1, L2_ffn_w3, L2_ffn_w2, L3_attn_Wqkv, L3_attn_bqkv, L3_attn_q_gamma, L3_attn_q_beta, L3_attn_k_gamma, L3_attn_k_beta, L3_attn_alpha, L3_attn_Wproj, L3_attn_bproj, L3_ffn_cn_w1, L3_ffn_cn_b1, L3_ffn_cn_w2, L3_ffn_cn_b2, L3_ffn_cn_w3, L3_ffn_cn_b3, L3_ffn_cn_w4, L3_ffn_cn_b4, L3_ffn_gc_w1, L3_ffn_gc_b1, L3_ffn_gc_w2, L3_ffn_gc_b2, L3_ffn_gc_w3, L3_ffn_gc_b3, L3_ffn_adaptive_range):

    def _L0_attn_ref(x, Wq, Wk, Wv, Wbeta, Wg, Wout, ln_g, ln_b):
        import jax, jax.numpy as jnp
        import numpy as np
        B, S, HID, NH = (8, 512, 128, 16)
        D = HID // NH
        LN_EPS = 1e-05

        def _l2norm(a):
            n = jnp.sqrt(jnp.sum(a * a, axis=-1, keepdims=True))
            return a / jnp.maximum(n, 1e-12)
        b, s, _ = x.shape
        nh = Wbeta.shape[1]
        d = Wq.shape[1] // nh
        q = _l2norm((x @ Wq).reshape(b, s, nh, d))
        k = _l2norm((x @ Wk).reshape(b, s, nh, d))
        v = (x @ Wv).reshape(b, s, nh, d)
        beta = jax.nn.sigmoid(x @ Wbeta)
        qT = jnp.moveaxis(q, 1, 0)
        kT = jnp.moveaxis(k, 1, 0)
        vT = jnp.moveaxis(v, 1, 0)
        bT = jnp.moveaxis(beta, 1, 0)
        state0 = jnp.zeros((b, nh, d, d), x.dtype)

        def step(state, inp):
            qt, kt, vt, bt = inp
            kk = kt[..., :, None] * kt[..., None, :]
            bb = bt[..., None, None]
            state = state * (1.0 - bb * kk) + bb * (vt[..., :, None] * kt[..., None, :])
            out_t = jnp.einsum('bhij,bhj->bhi', state, qt)
            return (state, out_t)
        _, outs = jax.lax.scan(step, state0, (qT, kT, vT, bT))
        out = jnp.moveaxis(outs, 0, 1).reshape(b, s, nh * d)
        mu = jnp.mean(out, axis=-1, keepdims=True)
        var = jnp.mean((out - mu) ** 2, axis=-1, keepdims=True)
        out = (out - mu) / jnp.sqrt(var + LN_EPS) * ln_g + ln_b
        out = out * jax.nn.silu(x @ Wg)
        return out @ Wout

    def _L0_ffn_ref(x, cn_w1, cn_b1, cn_w2, cn_b2, cn_w3, cn_b3, cn_w4, cn_b4, gc_w1, gc_b1, gc_w2, gc_b2, gc_w3, gc_b3, adaptive_range):
        import jax, jax.numpy as jnp
        import numpy as np
        B, S, DIM = (4, 512, 128)
        BASE_COUPLING = 0.1
        NUM_CYCLES = 3

        def _gelu(x):
            return jax.nn.gelu(x, approximate=False)

        def _coupling_net(h, w1, b1, w2, b2, w3, b3, w4, b4):
            h = _gelu(h @ w1 + b1)
            h = _gelu(h @ w2 + b2)
            h = _gelu(h @ w3 + b3)
            return jax.nn.sigmoid(h @ w4 + b4)

        def _global_net(h, w1, b1, w2, b2, w3, b3):
            h = _gelu(h @ w1 + b1)
            h = _gelu(h @ w2 + b2)
            return jax.nn.sigmoid(h @ w3 + b3)

        def _twist(x):
            o_r, o_i, p_r, p_i = jnp.split(x, 4, axis=-1)
            return jnp.concatenate([p_r, -p_i, -o_r, o_i], axis=-1)
        global_context = x.mean(axis=1, keepdims=True)
        gf = _global_net(global_context, gc_w1, gc_b1, gc_w2, gc_b2, gc_w3, gc_b3)
        out = x
        for _ in range(NUM_CYCLES):
            tf = _coupling_net(out, cn_w1, cn_b1, cn_w2, cn_b2, cn_w3, cn_b3, cn_w4, cn_b4)
            combined = 0.7 * gf + 0.3 * tf
            coupling = BASE_COUPLING + adaptive_range * (combined - 0.5) * 2.0
            out = out + coupling * _twist(out)
        return out

    def _L1_attn_ref(h, ln_w, ln_b, Wk, Wv, Wr, Wo):
        import jax, jax.numpy as jnp
        import numpy as np
        DECAY = 0.95
        EPS = 1e-05
        B, T, D, L = (4, 512, 128, 2)

        def _layer_norm(x, w, b):
            mu = jnp.mean(x, axis=-1, keepdims=True)
            var = jnp.mean(jnp.square(x - mu), axis=-1, keepdims=True)
            return (x - mu) * jax.lax.rsqrt(var + EPS) * w + b

        def _time_mix_layer(x, ln_w, ln_b, Wk, Wv, Wr, Wo):
            normed = _layer_norm(x, ln_w, ln_b)
            k = jnp.einsum('btd,ed->bte', normed, Wk)
            v = jnp.einsum('btd,ed->bte', normed, Wv)
            r = jax.nn.sigmoid(jnp.einsum('btd,ed->bte', normed, Wr))
            kv = k * v

            def step(state, kv_t):
                state = DECAY * state + (1.0 - DECAY) * kv_t
                return (state, state)
            init = jnp.zeros((x.shape[0], x.shape[2]), dtype=x.dtype)
            _, states = jax.lax.scan(step, init, jnp.swapaxes(kv, 0, 1))
            y = r * jnp.swapaxes(states, 0, 1)
            y = jnp.einsum('btd,ed->bte', y, Wo)
            return x + y
        out = h
        for i in range(Wk.shape[0]):
            out = _time_mix_layer(out, ln_w[i], ln_b[i], Wk[i], Wv[i], Wr[i], Wo[i])
        return out

    def _L1_ffn_ref(x, wqkv, q_scale, k_scale, wo, ln_g, ln_b, w1, b1, w2, b2):
        import jax, jax.numpy as jnp
        import numpy as np
        DIM = 128
        DEPTH = 2
        HEADS = 8
        DIM_HEAD = 64
        WINDOW = 64
        INNER = HEADS * DIM_HEAD
        HID = int(DIM * 4 * 2 / 3)
        B, N = (2, 1024)
        QK_SCALE = 8.0

        def shift_token(t):
            t1, t2 = jnp.split(t, 2, axis=-1)
            t2 = jnp.pad(t2, ((0, 0), (1, 0), (0, 0)))[:, :-1]
            return jnp.concatenate([t1, t2], axis=-1)

        def l2norm(t):
            return t / jnp.clip(jnp.linalg.norm(t, axis=-1, keepdims=True), 1e-12)

        def rotate_half(x):
            x1, x2 = jnp.split(x, 2, axis=-1)
            return jnp.concatenate([-x2, x1], axis=-1)

        def rotary_xpos(q, k):
            n = q.shape[-2]
            half_idx = jnp.arange(0, DIM_HEAD, 2, dtype=jnp.float32)
            inv_freq = 1.0 / 10000.0 ** (half_idx / DIM_HEAD)
            t = jnp.arange(n, dtype=jnp.float32)
            freqs = t[:, None] * inv_freq[None, :]
            freqs = jnp.concatenate([freqs, freqs], axis=-1)
            base = (half_idx + 0.4 * DIM_HEAD) / (1.4 * DIM_HEAD)
            power = (t - n // 2) / float(WINDOW // 2)
            scale = base[None, :] ** power[:, None]
            scale = jnp.concatenate([scale, scale], axis=-1)
            cos, sin = (jnp.cos(freqs), jnp.sin(freqs))
            q = q * cos * scale + rotate_half(q) * sin * scale
            k = k * cos / scale + rotate_half(k) * sin / scale
            return (q, k)

        def local_attention(q, k, v):
            b, h, n, d = q.shape
            w = n // WINDOW
            bq = q.reshape(b, h, w, WINDOW, d) * QK_SCALE
            bk = k.reshape(b, h, w, WINDOW, d)
            bv = v.reshape(b, h, w, WINDOW, d)

            def look_around(t):
                p = jnp.pad(t, ((0, 0), (0, 0), (1, 0), (0, 0), (0, 0)))
                return jnp.concatenate([p[:, :, :w], p[:, :, 1:]], axis=3)
            bk, bv = (look_around(bk), look_around(bv))
            bt = jnp.arange(n).reshape(w, WINDOW)
            btp = jnp.pad(bt, ((1, 0), (0, 0)), constant_values=-1)
            btk = jnp.concatenate([btp[:w], btp[1:]], axis=1)
            sim = jnp.einsum('bhwid,bhwjd->bhwij', bq, bk)
            i = bt[:, :, None]
            j = btk[:, None, :]
            mask = (i < j) | (i > j + WINDOW) | (j == -1)
            sim = jnp.where(mask, -jnp.finfo(sim.dtype).max, sim)
            attn = jax.nn.softmax(sim, axis=-1)
            out = jnp.einsum('bhwij,bhwjd->bhwid', attn, bv)
            return out.reshape(b, h, n, d)

        def _layer(x, wqkv, qs, ksc, wo, lg, lb, w1, b1, w2, b2):
            b, n, _ = x.shape
            h = shift_token(x)
            qkv = h @ wqkv
            q, k, v = jnp.split(qkv, 3, axis=-1)
            to_heads = lambda t: t.reshape(b, n, HEADS, DIM_HEAD).transpose(0, 2, 1, 3)
            q, k, v = (to_heads(q), to_heads(k), to_heads(v))
            q = l2norm(q) * qs
            k = l2norm(k) * ksc
            q, k = rotary_xpos(q, k)
            o = local_attention(q, k, v)
            o = o.transpose(0, 2, 1, 3).reshape(b, n, INNER)
            x = x + o @ wo
            h = shift_token(x)
            mu = h.mean(-1, keepdims=True)
            var = h.var(-1, keepdims=True)
            h = (h - mu) / jnp.sqrt(var + 1e-05) * lg + lb
            h = h @ w1 + b1
            a, g = jnp.split(h, 2, axis=-1)
            h = a * jax.nn.gelu(g, approximate=False)
            x = x + h @ w2 + b2
            return x
        for l in range(DEPTH):
            x = _layer(x, wqkv[l], q_scale[l], k_scale[l], wo[l], ln_g[l], ln_b[l], w1[l], b1[l], w2[l], b2[l])
        return x

    def _L2_attn_ref(hidden_states, in_proj_w, conv_w, conv_b, x_proj_w, dt_proj_w, dt_proj_b, dt_ln_w, b_ln_w, c_ln_w, A_log, D, out_proj_w):
        import jax, jax.numpy as jnp
        import numpy as np
        from jax import lax
        H = 128
        EXPAND = 2
        I = EXPAND * H
        N = 16
        K = 4
        R = 64
        EPS = 1e-06
        B_SZ, L = (2, 128)

        def rmsnorm(x, w):
            v = jnp.mean(x.astype(jnp.float32) ** 2, axis=-1, keepdims=True)
            return w * (x * jax.lax.rsqrt(v + EPS)).astype(x.dtype)
        b, l, _ = hidden_states.shape
        proj = hidden_states @ in_proj_w.T
        hs, gate = (proj[..., :I], proj[..., I:])
        x = jnp.transpose(hs, (0, 2, 1))
        x = lax.conv_general_dilated(x, conv_w, (1,), [(1, 2)], feature_group_count=I, dimension_numbers=('NCH', 'OIH', 'NCH'))
        x = x + conv_b[None, :, None]
        u = jax.nn.silu(jnp.transpose(x, (0, 2, 1)))
        x_dbl = u @ x_proj_w.T
        dt = rmsnorm(x_dbl[..., :R], dt_ln_w)
        Bm = rmsnorm(x_dbl[..., R:R + N], b_ln_w)
        Cm = rmsnorm(x_dbl[..., R + N:], c_ln_w)
        dt = jax.nn.softplus(dt @ dt_proj_w.T + dt_proj_b)
        A = -jnp.exp(A_log)
        dA = jnp.exp(dt[..., None] * A)
        dBu = (dt * u)[..., None] * Bm[:, :, None, :]

        def step(h, inp):
            dA_t, dBu_t = inp
            h = dA_t * h + dBu_t
            return (h, h)
        h0 = jnp.zeros((b, I, N), jnp.float32)
        _, h_seq = lax.scan(step, h0, (jnp.transpose(dA, (1, 0, 2, 3)), jnp.transpose(dBu, (1, 0, 2, 3))))
        y = jnp.einsum('lbin,bln->bli', h_seq, Cm)
        y = y + u * D
        y = y * jax.nn.silu(gate)
        return y @ out_proj_w.T

    def _L2_ffn_ref(x, router_w, router_b, w1, w3, w2):
        import jax, jax.numpy as jnp
        import numpy as np
        B, S, D, F, E, K = (4, 256, 128, 512, 4, 2)
        b, s, d = x.shape
        T = b * s
        e = router_w.shape[1]
        xf = x.reshape(T, d)
        logits = xf @ router_w + router_b
        probs = jax.nn.softmax(logits, axis=-1)
        top_p, top_i = jax.lax.top_k(probs, K)
        top_p = top_p / jnp.sum(top_p, axis=-1, keepdims=True)
        gates = jnp.zeros((T, e), xf.dtype).at[jnp.arange(T)[:, None], top_i].add(top_p)
        h = jax.nn.silu(jnp.einsum('td,edf->etf', xf, w1)) * jnp.einsum('td,edf->etf', xf, w3)
        expert_out = jnp.einsum('etf,efd->etd', h, w2)
        out = jnp.einsum('te,etd->td', gates, expert_out)
        return out.reshape(b, s, d)

    def _L3_attn_ref(x, Wqkv, bqkv, q_gamma, q_beta, k_gamma, k_beta, alpha, Wproj, bproj):
        import jax, jax.numpy as jnp
        import numpy as np
        H = 16
        TOPK_RATIO = 0.05
        LN_EPS = 1e-05

        def _layernorm(t, gamma, beta):
            mu = t.mean(-1, keepdims=True)
            var = t.var(-1, keepdims=True)
            return (t - mu) * jax.lax.rsqrt(var + LN_EPS) * gamma + beta
        B, N, C = x.shape
        D = C // H
        qkv = (x @ Wqkv.T + bqkv).reshape(B, N, 3, H, D).transpose(2, 0, 3, 1, 4)
        q, k, v = (qkv[0], qkv[1], qkv[2])
        q = _layernorm(q, q_gamma, q_beta)
        k = _layernorm(k, k_gamma, k_beta)
        scores = jnp.einsum('bhnd,bhmd->bhnm', q, k) / jnp.sqrt(jnp.float32(D))
        aw = jax.nn.softmax(scores, axis=-1)
        topk = max(1, int(N * TOPK_RATIO))
        kth = jax.lax.top_k(aw, topk)[0][..., -1:]
        mask = (aw >= kth).astype(aw.dtype)
        aws = aw * mask
        aws = aws / (aws.sum(-1, keepdims=True) + 1e-08)
        o_s = jnp.einsum('bhnm,bhmd->bhnd', aws, v)
        qf = jax.nn.softmax(q, axis=-1)
        kf = jax.nn.softmax(k, axis=-1)
        kv = jnp.einsum('bhnd,bhne->bhde', kf, v)
        z = jnp.einsum('bhnd,bhd->bhn', qf, kf.sum(axis=2))
        o_l = jnp.einsum('bhnd,bhde->bhne', qf, kv) / (z[..., None] + 1e-06)
        a = jax.nn.sigmoid(alpha).reshape(1, H, 1, 1)
        o = (a * o_s + (1.0 - a) * o_l).transpose(0, 2, 1, 3).reshape(B, N, C)
        return o @ Wproj.T + bproj

    def _L3_ffn_ref(x, cn_w1, cn_b1, cn_w2, cn_b2, cn_w3, cn_b3, cn_w4, cn_b4, gc_w1, gc_b1, gc_w2, gc_b2, gc_w3, gc_b3, adaptive_range):
        import jax, jax.numpy as jnp
        import numpy as np
        B, S, DIM = (4, 512, 128)
        BASE_COUPLING = 0.1
        NUM_CYCLES = 3

        def _gelu(x):
            return jax.nn.gelu(x, approximate=False)

        def _coupling_net(h, w1, b1, w2, b2, w3, b3, w4, b4):
            h = _gelu(h @ w1 + b1)
            h = _gelu(h @ w2 + b2)
            h = _gelu(h @ w3 + b3)
            return jax.nn.sigmoid(h @ w4 + b4)

        def _global_net(h, w1, b1, w2, b2, w3, b3):
            h = _gelu(h @ w1 + b1)
            h = _gelu(h @ w2 + b2)
            return jax.nn.sigmoid(h @ w3 + b3)

        def _twist(x):
            o_r, o_i, p_r, p_i = jnp.split(x, 4, axis=-1)
            return jnp.concatenate([p_r, -p_i, -o_r, o_i], axis=-1)
        global_context = x.mean(axis=1, keepdims=True)
        gf = _global_net(global_context, gc_w1, gc_b1, gc_w2, gc_b2, gc_w3, gc_b3)
        out = x
        for _ in range(NUM_CYCLES):
            tf = _coupling_net(out, cn_w1, cn_b1, cn_w2, cn_b2, cn_w3, cn_b3, cn_w4, cn_b4)
            combined = 0.7 * gf + 0.3 * tf
            coupling = BASE_COUPLING + adaptive_range * (combined - 0.5) * 2.0
            out = out + coupling * _twist(out)
        return out
    x = L0_attn_x
    xn = _layernorm(x, axis=-1)
    s = _L0_attn_ref(xn, L0_attn_Wq, L0_attn_Wk, L0_attn_Wv, L0_attn_Wbeta, L0_attn_Wg, L0_attn_Wout, L0_attn_ln_g, L0_attn_ln_b)
    g = _silu(_L0_ffn_ref(xn, L0_ffn_cn_w1, L0_ffn_cn_b1, L0_ffn_cn_w2, L0_ffn_cn_b2, L0_ffn_cn_w3, L0_ffn_cn_b3, L0_ffn_cn_w4, L0_ffn_cn_b4, L0_ffn_gc_w1, L0_ffn_gc_b1, L0_ffn_gc_w2, L0_ffn_gc_b2, L0_ffn_gc_w3, L0_ffn_gc_b3, L0_ffn_adaptive_range))
    x = x + s * g
    xn = _layernorm(x, axis=-1)
    s = _L1_attn_ref(xn, L1_attn_ln_w, L1_attn_ln_b, L1_attn_Wk, L1_attn_Wv, L1_attn_Wr, L1_attn_Wo)
    g = _silu(_L1_ffn_ref(xn, L1_ffn_wqkv, L1_ffn_q_scale, L1_ffn_k_scale, L1_ffn_wo, L1_ffn_ln_g, L1_ffn_ln_b, L1_ffn_w1, L1_ffn_b1, L1_ffn_w2, L1_ffn_b2))
    x = x + s * g
    xn = _layernorm(x, axis=-1)
    s = _L2_attn_ref(xn, L2_attn_in_proj_w, L2_attn_conv_w, L2_attn_conv_b, L2_attn_x_proj_w, L2_attn_dt_proj_w, L2_attn_dt_proj_b, L2_attn_dt_ln_w, L2_attn_b_ln_w, L2_attn_c_ln_w, L2_attn_A_log, L2_attn_D, L2_attn_out_proj_w)
    g = _silu(_L2_ffn_ref(xn, L2_ffn_router_w, L2_ffn_router_b, L2_ffn_w1, L2_ffn_w3, L2_ffn_w2))
    x = x + s * g
    xn = _layernorm(x, axis=-1)
    s = _L3_attn_ref(xn, L3_attn_Wqkv, L3_attn_bqkv, L3_attn_q_gamma, L3_attn_q_beta, L3_attn_k_gamma, L3_attn_k_beta, L3_attn_alpha, L3_attn_Wproj, L3_attn_bproj)
    g = _silu(_L3_ffn_ref(xn, L3_ffn_cn_w1, L3_ffn_cn_b1, L3_ffn_cn_w2, L3_ffn_cn_b2, L3_ffn_cn_w3, L3_ffn_cn_b3, L3_ffn_cn_w4, L3_ffn_cn_b4, L3_ffn_gc_w1, L3_ffn_gc_b1, L3_ffn_gc_w2, L3_ffn_gc_b2, L3_ffn_gc_w3, L3_ffn_gc_b3, L3_ffn_adaptive_range))
    x = x + s * g
    return x

_drawn_inputs = setup_inputs


def setup_inputs(seed=0):
    import zlib

    import numpy as np

    out = dict(_drawn_inputs(seed))
    spreads = {'L0_attn_ln_g': (1.0, 0.6),
     'L0_attn_ln_b': (0.0, 0.8),
     'L0_ffn_cn_b1': (0.0, 2.0),
     'L0_ffn_cn_b2': (0.0, 2.0),
     'L0_ffn_cn_b3': (0.0, 2.0),
     'L0_ffn_gc_b1': (0.0, 0.8),
     'L0_ffn_gc_b2': (0.0, 2.0),
     'L1_attn_ln_w': (1.0, 0.6),
     'L1_attn_ln_b': (0.0, 0.8),
     'L1_ffn_q_scale': (1.0, 0.6),
     'L1_ffn_k_scale': (1.0, 0.6),
     'L1_ffn_ln_g': (1.0, 0.6),
     'L1_ffn_ln_b': (0.0, 0.8),
     'L1_ffn_b1': (0.0, 0.8),
     'L1_ffn_b2': (0.0, 0.1),
     'L2_attn_conv_b': (0.0, 0.8),
     'L2_attn_dt_ln_w': (1.0, 0.6),
     'L2_attn_b_ln_w': (1.0, 0.6),
     'L2_attn_c_ln_w': (1.0, 0.6),
     'L2_attn_D': (1.0, 0.6),
     'L2_ffn_router_b': (0.0, 0.8),
     'L3_attn_bqkv': (0.0, 0.8),
     'L3_attn_q_gamma': (1.0, 0.6),
     'L3_attn_q_beta': (0.0, 2.0),
     'L3_attn_k_gamma': (1.0, 0.6),
     'L3_attn_k_beta': (0.0, 2.0),
     'L3_attn_alpha': (0.5, 0.6),
     'L3_attn_bproj': (0.0, 2.0),
     'L3_ffn_cn_b1': (0.0, 2.0),
     'L3_ffn_cn_b2': (0.0, 2.0),
     'L3_ffn_cn_b3': (0.0, 2.0),
     'L3_ffn_gc_b1': (0.0, 0.8),
     'L3_ffn_gc_b2': (0.0, 0.8)}
    factors = {'L0_attn_Wbeta': 8.0,
     'L0_ffn_cn_w1': 8.0,
     'L0_ffn_cn_w2': 8.0,
     'L0_ffn_cn_w3': 8.0,
     'L0_ffn_cn_w4': 8.0,
     'L0_ffn_gc_w1': 64.0,
     'L0_ffn_gc_w2': 64.0,
     'L0_ffn_gc_w3': 8.0,
     'L1_ffn_wqkv': 3.954,
     'L1_ffn_wo': 3.955,
     'L1_ffn_w1': 6.449,
     'L1_ffn_w2': 6.349,
     'L2_attn_in_proj_w': 8.0,
     'L2_attn_conv_w': 8.0,
     'L2_attn_x_proj_w': 8.0,
     'L2_attn_dt_proj_w': 8.0,
     'L2_attn_dt_proj_b': 8.0,
     'L2_attn_A_log': 8.0,
     'L2_attn_out_proj_w': 8.0,
     'L2_ffn_router_w': 8.0,
     'L2_ffn_w1': 8.0,
     'L2_ffn_w3': 8.0,
     'L2_ffn_w2': 8.0,
     'L3_ffn_cn_w1': 64.0,
     'L3_ffn_cn_w2': 64.0,
     'L3_ffn_cn_w3': 64.0,
     'L3_ffn_cn_w4': 64.0,
     'L3_ffn_gc_w1': 64.0,
     'L3_ffn_gc_w2': 8.0,
     'L3_ffn_gc_w3': 64.0,
     'L3_attn_Wqkv': 8.0,
     'L3_attn_Wproj': 8.0}
    for name, (base, spread) in spreads.items():
        noise = np.random.default_rng([zlib.crc32(name.encode()), seed]).standard_normal(out[name].shape)
        drawn = base * np.exp(spread * noise) if base else spread * noise
        out[name] = jnp.asarray(drawn.astype(out[name].dtype))
    for name, factor in factors.items():
        out[name] = (out[name] * factor).astype(out[name].dtype)
    return out
```

```python
from contextlib import ExitStack

import numpy as np
import concourse.bass as bass
from concourse import mybir

F32 = mybir.dt.float32
ALU = mybir.AluOpType
ACT = mybir.ActivationFunctionType
AX = mybir.AxisListType

B, T, D = 8, 512, 128
NT = T // 128
LN_EPS = 1e-5
NORM_SCALE = 2.0 ** 36
NORM_FLOOR = 2.0 ** -64
BIG = 1e30

H1, DH, WIN, HID = 8, 64, 64, 341
HCH = [(0, 128), (128, 128), (256, HID - 256)]
NS, R = 16, 64
NE, FCH = 4, 4
H3, D3 = 16, 8
TOPK = max(1, int(T * 0.05))
DEPTH = 2


def constants():
    p = np.arange(128)
    c = {}
    c["ident"] = np.eye(128)
    c["mean"] = np.full((128, 128), 1.0 / 128)
    c["head8"] = (p[:, None] // 8 == p[None] // 8).astype(float)
    c["head64"] = (p[:, None] // 64 == p[None] // 64).astype(float)
    for i in range(8):
        c[f"reduce{i}"] = ((p[:, None] // 8 == p[None] // 8) & (p[None] % 8 == i)).astype(float)
    tw = np.zeros((128, 128))
    r = np.arange(32)
    tw[64 + r, r] = 1
    tw[96 + r, 32 + r] = -1
    tw[r, 64 + r] = -1
    tw[32 + r, 96 + r] = 1
    c["twist"] = tw
    j = np.arange(WIN + 128)
    ok = (j[None] - WIN <= p[:, None]) & (p[:, None] <= j[None])
    c["band"] = np.where(ok, 0.0, -BIG)
    g = np.zeros((96, 96))
    for a, b in ((0, R), (R, R + NS), (R + NS, R + 2 * NS)):
        g[a:b, a:b] = 1.0 / (b - a)
    c["rms"] = g
    e = np.arange(NE)
    low = (e[None, :] < e[:, None]).astype(float).reshape(1, -1)
    c["tie"] = np.repeat(np.tile(low, (1, NT)), 128, 0)
    c["untie"] = 1.0 - c["tie"]
    c["headcol"] = (p[:, None] // 8 == np.arange(16)[None]).astype(float)
    c["quarter"] = ((p[:, None] // 8) % 4 == np.arange(4)[None]).astype(float)
    c["ones_row"] = np.ones((1, 128))
    c["decay"] = np.full((128, T), 0.95)
    for n, v in (("eps5", 1e-5), ("eps6", 1e-6), ("floor", NORM_FLOOR),
                 ("norm_back", 0.5 * np.log(NORM_SCALE)), ("one", 1.0), ("zero", 0.0)):
        c[n] = np.full((128, 1), v)
    half = np.arange(0, DH, 2, dtype=np.float32)
    inv = (1.0 / 10000.0 ** (half / np.float32(DH))).astype(np.float32)
    t = np.arange(T, dtype=np.float32)
    fr = (t[:, None] * inv[None]).astype(np.float32)
    base = (half + np.float32(0.4 * DH)) / np.float32(1.4 * DH)
    power = (t - T // 2) / np.float32(WIN // 2)
    sc = (base[None] ** power[:, None]).astype(np.float32)
    dup = lambda a: np.tile(np.concatenate([a, a], 1), (1, 2)).T
    sign = np.where(p % 64 < 32, -1.0, 1.0)[:, None]
    c["first_once"] = np.zeros((128, 0))
    c["cos_q"], c["sin_q"] = dup(np.cos(fr) * sc), dup(np.sin(fr) * sc) * sign
    c["cos_k"], c["sin_k"] = dup(np.cos(fr) / sc), dup(np.sin(fr) / sc) * sign
    return {k: np.asarray(v, np.float32) for k, v in c.items()}


def weights(a):
    w = {}
    col = lambda v: np.reshape(v, (-1, 1))
    for n in ("Wq", "Wk", "Wg", "Wout"):
        w["l0_" + n] = a["L0_attn_" + n]
    for i in range(8):
        w[f"l0_Wkr{i}"] = np.repeat(a["L0_attn_Wk"].reshape(128, 16, 8)[:, :, i], 8, 1)
        w[f"l0_Wvr{i}"] = np.repeat(a["L0_attn_Wv"].reshape(128, 16, 8)[:, :, i], 8, 1)
    w["l0_Wbeta"] = np.repeat(a["L0_attn_Wbeta"], 8, 1)
    w["l0_ln_g"], w["l0_ln_b"] = col(a["L0_attn_ln_g"]), col(a["L0_attn_ln_b"])
    for lay in ("L0", "L3"):
        for n in ("cn_w1", "cn_w2", "cn_w3", "gc_w1", "gc_w2"):
            w[f"{lay}_{n}"] = a[f"{lay}_ffn_{n}"]
        for n in ("cn_b1", "cn_b2", "cn_b3", "gc_b1", "gc_b2"):
            w[f"{lay}_{n}"] = col(a[f"{lay}_ffn_{n}"])
        for n in ("cn_w4", "gc_w3"):
            w[f"{lay}_{n}"] = np.repeat(a[f"{lay}_ffn_{n}"], 128, 1)
        for n in ("cn_b4", "gc_b3", "adaptive_range"):
            w[f"{lay}_{n}"] = np.repeat(col(a[f"{lay}_ffn_{n}"]), 128, 0)
    for i in range(DEPTH):
        w[f"l1_ln_w{i}"], w[f"l1_ln_b{i}"] = col(a["L1_attn_ln_w"][i]), col(a["L1_attn_ln_b"][i])
        for n in ("Wk", "Wv", "Wr", "Wo"):
            w[f"l1_{n}{i}"] = a["L1_attn_" + n][i].T
        qkv = a["L1_ffn_wqkv"][i]
        w[f"l1_qkv{i}"] = qkv
        w[f"l1_swap{i}"] = qkv[:, :1024].reshape(128, 16, 2, 32)[:, :, ::-1].reshape(128, 1024)
        for n, s in (("q", "q_scale"), ("k", "k_scale")):
            v = a["L1_ffn_" + s][i]
            w[f"l1_{n}s{i}"] = col(np.concatenate([v, v]))
            w[f"l1_{n}x{i}"] = col(np.concatenate([v[32:], v[:32], v[32:], v[:32]]))
        w[f"l1_wo{i}"] = a["L1_ffn_wo"][i].reshape(4, 128, 128).transpose(1, 0, 2).reshape(128, 512)
        w[f"l1_lg{i}"], w[f"l1_lb{i}"] = col(a["L1_ffn_ln_g"][i]), col(a["L1_ffn_ln_b"][i])
        w[f"l1_w1_{i}"] = a["L1_ffn_w1"][i]
        for c, (o, m) in enumerate(HCH):
            w[f"l1_b1a{c}_{i}"] = col(a["L1_ffn_b1"][i][o:o + m])
            w[f"l1_b1g{c}_{i}"] = col(a["L1_ffn_b1"][i][HID + o:HID + o + m])
            w[f"l1_w2_{c}_{i}"] = a["L1_ffn_w2"][i][o:o + m]
        w[f"l1_b2_{i}"] = col(a["L1_ffn_b2"][i])
    w["l2_in"] = a["L2_attn_in_proj_w"].T
    two = lambda v: v.reshape(2, 128, -1).transpose(1, 0, 2).reshape(128, -1)
    w["l2_conv"] = two(a["L2_attn_conv_w"].reshape(256, 4))
    w["l2_conv_b"], w["l2_D"], w["l2_dt_b"] = (two(a["L2_attn_" + n]) for n in ("conv_b", "D", "dt_proj_b"))
    w["l2_xproj"] = two(a["L2_attn_x_proj_w"].T)
    w["l2_xln"] = col(np.concatenate([a["L2_attn_dt_ln_w"], a["L2_attn_b_ln_w"], a["L2_attn_c_ln_w"]]))
    w["l2_dt"] = a["L2_attn_dt_proj_w"].T
    w["l2_alog"] = two(a["L2_attn_A_log"])
    w["l2_out"] = two(a["L2_attn_out_proj_w"].T)
    w["l2_router"] = a["L2_ffn_router_w"]
    w["l2_router_b"] = a["L2_ffn_router_b"].reshape(1, NE)
    for e in range(NE):
        w[f"l2_w1_{e}"], w[f"l2_w3_{e}"] = a["L2_ffn_w1"][e], a["L2_ffn_w3"][e]
        w[f"l2_w2_{e}"] = a["L2_ffn_w2"][e].reshape(4, 128, 128).transpose(1, 0, 2).reshape(128, 512)
    w["l3_qkv"] = a["L3_attn_Wqkv"].T
    w["l3_bqkv"] = a["L3_attn_bqkv"].reshape(1, 384)
    for n in ("gamma", "beta"):
        row = np.concatenate([np.tile(a[f"L3_attn_{p}_{n}"], H3) for p in "qk"])
        w["l3_" + n] = np.repeat(row.reshape(1, -1), 128, 0)
    w["l3_alpha"] = np.repeat(a["L3_attn_alpha"].reshape(1, 16), 128, 0)
    w["l3_proj"] = a["L3_attn_Wproj"].T
    w["l3_bproj"] = col(a["L3_attn_bproj"])
    return w


def packed(parts):
    out = np.zeros((128, sum(v.shape[1] for v in parts.values())), np.float32)
    at = 0
    for v in parts.values():
        out[:v.shape[0], at:at + v.shape[1]] = v
        at += v.shape[1]
    return out


class Steps:

    def __init__(self, nc, ctx, layer):
        self.nc, self.ctx, self.layer, self.all = nc, ctx, layer, {}

    def __getitem__(self, name):
        if name not in self.all:
            self.all[name] = self.ctx.enter_context(self.nc.semaphore(f"{self.layer}_{name}"))
        return self.all[name]

    def clear(self):
        engines = (self.nc.sync, self.nc.scalar, self.nc.vector, self.nc.gpsimd, self.nc.tensor)
        for n, s in enumerate(self.all.values()):
            engines[n % 5].sem_clear(s)
        self.nc.all_engine_barrier()


def build(nc, x_in, w_in, c_in, out, wcols, ccols, upto=99, probe=None):
    ctx = ExitStack()

    def sb(name, shape, c=None):
        return (c or ctx).enter_context(nc.sbuf_tensor(name, shape, F32))

    with ctx:
        w_sb = sb("weights", [128, w_in.shape[1]])
        once = ccols["first_once"][0]
        c_sb = sb("consts", [128, once])
        bank = [ctx.enter_context(nc.psum_tensor(f"bank{i}", [128, 512], F32)) for i in range(8)]
        x = sb("x", [128, T])
        xn = sb("xn", [128, T])
        rot = sb("rot", [128, DEPTH * 4, T])
        a_neg = sb("a_neg", [128, 2 * NS])
        alpha = sb("alpha", [128, 2, H3])
        couple = sb("couple", [128, 2, 4])

        def W(name, r=None, lo=0, n=None):
            o, rows, cols = wcols[name]
            return w_sb[0:(r or rows), o + lo:o + lo + (cols - lo if n is None else n)]

        def C(name, r=None):
            o, rows, cols = ccols[name]
            return c_sb[0:(r or rows), o:o + cols]

        def mm(o, lhsT, rhs, start=True, stop=True):
            return nc.tensor.matmul(o, lhsT, rhs, start=start, stop=stop)

        act = nc.scalar.activation
        tt, ts, stt = nc.vector.tensor_tensor, nc.vector.tensor_scalar, nc.vector.scalar_tensor_tensor

        with ExitStack() as c0:
            S = Steps(nc, c0, "setup")
            tables = sb("rotary", [128, c_in.shape[1] - once], c0)
            with nc.Block() as block:
                @block.sync
                def _(sp):
                    sp.dma_start(w_sb[:], w_in).then_inc(S["loaded"], 16)
                    sp.dma_start(c_sb[:], c_in[:, 0:once]).then_inc(S["loaded"], 16)
                    sp.dma_start(tables[:], c_in[:, once:]).then_inc(S["loaded"], 16)

                @block.scalar
                def _(a):
                    a.wait_ge(S["loaded"], 48)
                    act(a_neg[:], W("l2_alog"), ACT.Exp).then_inc(S["exp_a"], 1)
                    act(alpha[:, 0], W("l3_alpha"), ACT.Sigmoid).then_inc(S["alpha"], 1)

                @block.vector
                def _(v):
                    v.wait_ge(S["loaded"], 48)
                    for i in range(DEPTH):
                        for n, (table, scale) in enumerate((("cos_q", "qs"), ("sin_q", "qx"), ("cos_k", "ks"), ("sin_k", "kx"))):
                            o = ccols[table][0] - once
                            ts(rot[:, 4 * i + n], tables[:, o:o + T], W(f"l1_{scale}{i}"), None, ALU.mult)
                    for n, lay in enumerate(("L0", "L3")):
                        ts(couple[:, n, 0:1], W(f"{lay}_cn_b4"), 0.5, None, ALU.mult)
                        ts(couple[:, n, 1:2], W(f"{lay}_adaptive_range"), 2.0, None, ALU.mult)
                        ts(couple[:, n, 2:3], W(f"{lay}_adaptive_range"), 0.3, None, ALU.mult)
                        ts(couple[:, n, 3:4], W(f"{lay}_gc_b3"), 0.5, None, ALU.mult)
                    v.wait_ge(S["exp_a"], 1)
                    ts(a_neg[:], a_neg[:], -1.0, None, ALU.mult)
                    v.wait_ge(S["alpha"], 1)
                    ts(alpha[:, 1], alpha[:, 0], -1.0, 1.0, ALU.mult, ALU.add)
            S.clear()

        class Norm:

            def __init__(self, S, name, src, dst, xc, sq, rs, mu_bank, var_bank, gain=None, shift=None):
                self.S, self.n, self.src, self.dst, self.xc, self.sq, self.rs = S, name, src, dst, xc, sq, rs
                self.mu, self.var, self.gain, self.shift = mu_bank, var_bank, gain, shift

            def pe(self, pe):
                mm(self.mu, C("mean"), self.src).then_inc(self.S[self.n + "_mu"], 1)
                pe.wait_ge(self.S[self.n + "_sq"], 1)
                mm(self.var, C("mean"), self.sq).then_inc(self.S[self.n + "_var"], 1)

            def act(self, a):
                a.wait_ge(self.S[self.n + "_xc"], 1)
                act(self.sq, self.xc, ACT.Square).then_inc(self.S[self.n + "_sq"], 1)
                a.wait_ge(self.S[self.n + "_var"], 1)
                act(self.rs, self.var, ACT.Ln, bias=C("eps5")).then_inc(self.S[self.n + "_ln"], 1)
                a.wait_ge(self.S[self.n + "_ln"], 1)
                act(self.rs, self.rs, ACT.Exp, scale=-0.5).then_inc(self.S[self.n + "_rs"], 1)

            def dve(self, v):
                v.wait_ge(self.S[self.n + "_mu"], 1)
                tt(self.xc, self.src, self.mu, ALU.subtract).then_inc(self.S[self.n + "_xc"], 1)
                v.wait_ge(self.S[self.n + "_rs"], 1)
                if self.gain is None:
                    tt(self.dst, self.xc, self.rs, ALU.mult).then_inc(self.S[self.n], 1)
                else:
                    stt(self.dst, self.xc, self.gain, self.rs, ALU.mult, ALU.mult).then_inc(self.S[self.n + "_g"], 1)
                    v.wait_ge(self.S[self.n + "_g"], 1)
                    ts(self.dst, self.dst, self.shift, None, ALU.add).then_inc(self.S[self.n], 1)

        class Coupling:

            def __init__(self, S, lay, n, c, banks, src):
                self.S, self.lay, self.n, self.b, self.src = S, lay, n, banks, src
                self.o = [sb(f"{lay}_cyc{k}", [128, T], c) for k in range(3)]
                self.h1, self.h2, self.h3, self.th, self.m = (
                    sb(f"{lay}_ff{k}", [128, T], c) for k in range(5))
                self.sm = sb(f"{lay}_ctx", [128, 8], c)

            def pe(self, pe):
                S, lay, b, sm = self.S, self.lay, self.b, self.sm
                pe.wait_ge(S["ctx"], 1)
                mm(b[0][0:64, 0:1], W(lay + "_gc_w1"), sm[:, 0:1]).then_inc(S["gc1"], 1)
                yield
                pe.wait_ge(S["gc1_gelu"], 1)
                mm(b[0][0:32, 0:1], W(lay + "_gc_w2"), sm[0:64, 1:2]).then_inc(S["gc2"], 1)
                yield
                pe.wait_ge(S["gc2_gelu"], 1)
                mm(b[0][:, 0:1], W(lay + "_gc_w3"), sm[0:32, 2:3]).then_inc(S["gc3"], 1)
                yield
                for k in range(3):
                    src = self.src if k == 0 else self.o[k - 1][:]
                    pe.wait_ge(S["gc3_tanh"] if k == 0 else S["cycle"], max(k, 1))
                    mm(b[0][:], W(lay + "_cn_w1"), src).then_inc(S["cn1"], 1)
                    mm(b[1][:], C("twist"), src).then_inc(S["twist"], 1)
                    yield
                    pe.wait_ge(S["cn1_gelu"], k + 1)
                    mm(b[0][0:64], W(lay + "_cn_w2"), self.h1[:]).then_inc(S["cn2"], 1)
                    yield
                    pe.wait_ge(S["cn2_gelu"], k + 1)
                    mm(b[0][0:32], W(lay + "_cn_w3"), self.h2[0:64]).then_inc(S["cn3"], 1)
                    yield
                    pe.wait_ge(S["cn3_gelu"], k + 1)
                    mm(b[0][:], W(lay + "_cn_w4"), self.h3[0:32]).then_inc(S["cn4"], 1)
                    yield

            def act(self, a):
                S, lay, b, sm, n = self.S, self.lay, self.b, self.sm, self.n
                a.wait_ge(S["gc1"], 1)
                act(sm[0:64, 1:2], b[0][0:64, 0:1], ACT.Gelu, bias=W(lay + "_gc_b1")).then_inc(S["gc1_gelu"], 1)
                yield
                a.wait_ge(S["gc2"], 1)
                act(sm[0:32, 2:3], b[0][0:32, 0:1], ACT.Gelu, bias=W(lay + "_gc_b2")).then_inc(S["gc2_gelu"], 1)
                yield
                a.wait_ge(S["gc3"], 1)
                act(sm[:, 3:4], b[0][:, 0:1], ACT.Tanh, bias=couple[:, n, 3:4], scale=0.5).then_inc(S["gc3_tanh"], 1)
                yield
                for k in range(3):
                    a.wait_ge(S["cn1"], k + 1)
                    act(self.h1[:], b[0][:], ACT.Gelu, bias=W(lay + "_cn_b1")).then_inc(S["cn1_gelu"], 1)
                    yield
                    a.wait_ge(S["cn2"], k + 1)
                    act(self.h2[0:64], b[0][0:64], ACT.Gelu, bias=W(lay + "_cn_b2")).then_inc(S["cn2_gelu"], 1)
                    yield
                    a.wait_ge(S["cn3"], k + 1)
                    act(self.h3[0:32], b[0][0:32], ACT.Gelu, bias=W(lay + "_cn_b3")).then_inc(S["cn3_gelu"], 1)
                    yield
                    a.wait_ge(S["cn4"], k + 1)
                    if k > 0:
                        a.wait_ge(S["cycle_c"], k)
                    act(self.th[:], b[0][:], ACT.Tanh, bias=couple[:, n, 0:1], scale=0.5).then_inc(S["tanh"], 1)
                    yield

            def act_silu(self, a):
                a.wait_ge(self.S["cycle"], 3)
                act(self.th[:], self.o[2][:], ACT.Silu).then_inc(self.S["gate"], 1)

            def dve_context(self, v):
                S, sm = self.S, self.sm
                nc.vector.reduce_sum(sm[:, 4:5], self.src, AX.X).then_inc(S["ctx_sum"], 1)
                v.wait_ge(S["ctx_sum"], 1)
                ts(sm[:, 0:1], sm[:, 4:5], 1.0 / T, None, ALU.mult).then_inc(S["ctx"], 1)

            def dve(self, v):
                S, b, sm, n = self.S, self.b, self.sm, self.n
                for _ in range(3):
                    yield
                v.wait_ge(S["gc3_tanh"], 1)
                ts(sm[:, 5:6], sm[:, 3:4], 0.35, 0.35 - 0.5, ALU.mult, ALU.add).then_inc(S["base_a"], 1)
                v.wait_ge(S["base_a"], 1)
                stt(sm[:, 6:7], sm[:, 5:6], couple[:, n, 1:2], couple[:, n, 2:3], ALU.mult, ALU.add).then_inc(S["base_b"], 1)
                v.wait_ge(S["base_b"], 1)
                ts(sm[:, 7:8], sm[:, 6:7], 0.1, None, ALU.add).then_inc(S["base"], 1)
                v.wait_ge(S["base"], 1)
                for k in range(3):
                    src = self.src if k == 0 else self.o[k - 1][:]
                    for _ in range(4):
                        yield
                    v.wait_ge(S["tanh"], k + 1)
                    ts(self.m[:], self.th[:], couple[:, n, 2:3], sm[:, 7:8], ALU.mult, ALU.add).then_inc(S["cycle_c"], 1)
                    v.wait_ge(S["cycle_c"], k + 1)
                    v.wait_ge(S["twist"], k + 1)
                    tt(self.m[:], self.m[:], b[1][:], ALU.mult).then_inc(S["cycle_m"], 1)
                    v.wait_ge(S["cycle_m"], k + 1)
                    tt(self.o[k][:], src, self.m[:], ALU.add).then_inc(S["cycle"], 1)

        def layer1():
            with ExitStack() as c:
                S = Steps(nc, c, "l1")
                t = lambda n, f=T: sb("l1_" + n, [128, f], c)
                xc, sq, rs = t("xc"), t("sq"), t("rs")
                k_sb, kv, state, sr, y = t("k"), t("kv"), t("state"), t("sr"), t("y")
                h = [xn] + [t(f"h{i}") for i in range(DEPTH)]
                nrm = t("nrm")
                lx = Norm(S, "xn", x[:], xn[:], xc[:], sq[:], rs[:], bank[0][:], bank[1][:])
                la = [Norm(S, f"mix{i}", h[i][:], nrm[:], xc[:], sq[:], rs[:], bank[0][:], bank[1][:],
                           W(f"l1_ln_w{i}"), W(f"l1_ln_b{i}")) for i in range(DEPTH)]
                xf = [xn] + [t(f"f{i}") for i in range(DEPTH)]
                x1 = t("x1")
                hs = t("hs")
                qk = t("qk", 8 * T)
                of = sb("l1_of", [128, 4, T], c)
                sqq, t1 = [of[:, 0], of[:, 1]], [of[:, 2], of[:, 3]]
                rn, t2 = ([t(f"{n}{i}") for i in range(2)] for n in ("rn", "t2_"))
                vt = sb("l1_v", [128, NT, H1, DH + 1], c)
                KW = WIN + 128
                pe_ = sb("l1_probs", [128, H1, 256], c)
                nmax = sb("l1_nmax", [128, H1], c)
                pt = [sb(f"l1_pt{i}", [128, 4, 128], c) for i in range(2)]
                oinv = sb("l1_oinv", [128, H1], c)
                ot = sb("l1_ot", [128, H1, DH], c)
                gg = [k_sb, kv, sr]
                m = state
                lf = [Norm(S, f"ffn{i}", hs[:], nrm[:], xc[:], sq[:], rs[:], bank[0][:], bank[1][:],
                           W(f"l1_lg{i}"), W(f"l1_lb{i}")) for i in range(DEPTH)]
                with nc.Block() as block:
                    @block.tensor
                    def _(pe):
                        def values(pe, i, q, g):
                            kk = 4 * (NT * i + q) + g
                            pe.wait_ge(S["pt"], kk + 1)
                            if g == 0 and q:
                                pe.wait_ge(S["ot"], NT * i + q)
                            for e in range(2):
                                hh = 2 * g + e
                                for s in range(2):
                                    if q == 0 and s == 0:
                                        continue
                                    r = mm(bank[6 + hh // 4][:, 65 * (hh % 4):65 * (hh % 4) + 65],
                                           pt[kk % 2][:, 2 * e + s], vt[:, q - 1 + s, hh, :],
                                           s == 0 or q == 0, s == 1)
                            r.then_inc(S["pv"], 1)

                        lx.pe(pe)
                        for i in range(DEPTH):
                            pe.wait_ge(S["xn"] if i == 0 else S["h"], max(i, 1))
                            la[i].pe(pe)
                            pe.wait_ge(S[f"mix{i}"], 1)
                            mm(bank[2][:], W(f"l1_Wk{i}"), nrm[:]).then_inc(S["k"], 1)
                            mm(bank[3][:], W(f"l1_Wv{i}"), nrm[:]).then_inc(S["v"], 1)
                            mm(bank[4][:], W(f"l1_Wr{i}"), nrm[:]).then_inc(S["r"], 1)
                            pe.wait_ge(S["y"], i + 1)
                            mm(bank[5][:], W(f"l1_Wo{i}"), y[:]).then_inc(S["wo"], 1)
                        pe.wait_ge(S["h"], DEPTH)
                        for i in range(DEPTH):
                            pe.wait_ge(S["hs_a"], i + 1)
                            pe.wait_ge(S["hs_b"], i + 1)

                            def project(n):
                                k = 8 * i + n
                                if n >= 2:
                                    pe.wait_ge(S["t1"], k - 1)
                                    pe.wait_ge(S["t2"], k - 1)
                                mm(bank[n % 2][:], W(f"l1_qkv{i}", lo=128 * n, n=128), hs[:]).then_inc(S["pj"], 1)
                                mm(bank[2 + n % 2][:], W(f"l1_swap{i}", lo=128 * n, n=128), hs[:]).then_inc(S["px"], 1)

                            def norms(n):
                                k = 8 * i + n
                                pe.wait_ge(S["sqq"], k + 1)
                                if n >= 2:
                                    pe.wait_ge(S["rn_ln"], k - 1)
                                mm(bank[4 + n % 2][:], C("head64"), sqq[n % 2][:]).then_inc(S["ss"], 1)

                            for n in range(8):
                                project(n)
                                if n:
                                    norms(n - 1)
                            norms(7)
                            for q in range(NT):
                                k = NT * i + q
                                if q >= 2:
                                    pe.wait_ge(S["vt"], k - 1)
                                mm(bank[6 + q % 2][:], hs[:, 128 * q:128 * q + 128],
                                   W(f"l1_qkv{i}", lo=1024)).then_inc(S["vp"], 1)
                            for q in range(NT):
                                k = NT * i + q
                                lo = 128 * q - WIN if q else 0
                                n0 = 0 if q else WIN
                                if q == 0:
                                    pe.wait_ge(S["qk"], 8 * (i + 1))
                                    pe.wait_ge(S["ones"], 1)
                                else:
                                    pe.wait_ge(S["scored"], 4 * k)
                                for e, f in ((0, 0), (0, 1), (1, 0), (1, 1)):
                                    p0 = 64 * e
                                    for s in range(2):
                                        g = 2 * f + s
                                        r = mm(bank[2 * e + f][:, 256 * s + n0:256 * s + KW],
                                               qk[p0:p0 + 64, g * T + 128 * q:g * T + 128 * q + 128],
                                               qk[p0:p0 + 64, (4 + g) * T + lo:(4 + g) * T + 128 * q + 128])
                                    r.then_inc(S["score"], 1)
                                pe.wait_ge(S["exp"], k + 1)
                                for g in range(4):
                                    kk = 4 * k + g
                                    if kk >= 2:
                                        pe.wait_ge(S["pt"], kk - 1)
                                    if q == 0 and g == 0:
                                        pe.wait_ge(S["rn"], 8 * (i + 1))
                                        pe.wait_ge(S["vt"], NT * (i + 1))
                                    for e in range(2):
                                        for s in range(2):
                                            if q == 0 and s == 0:
                                                continue
                                            r = nc.tensor.transpose(
                                                bank[4 + kk % 2][:, 128 * (2 * e + s):128 * (2 * e + s) + 128],
                                                pe_[:, 2 * g + e, 128 * s:128 * s + 128], C("ident"))
                                    r.then_inc(S["turned"], 1)
                                    if g:
                                        values(pe, i, q, g - 1)
                                values(pe, i, q, 3)
                                pe.wait_ge(S["ot"], k + 1)
                                for g in range(4):
                                    r = nc.tensor.transpose(bank[4][:, 128 * g:128 * g + 128],
                                                            ot[:, 2 * g:2 * g + 2, :].rearrange("p a d -> p (a d)"), C("ident"))
                                r.then_inc(S["oturn"], 1)
                                pe.wait_ge(S["of"], k + 1)
                            for g in range(4):
                                r = mm(bank[0][:], W(f"l1_wo{i}", lo=128 * g, n=128), of[:, g], g == 0, g == 3)
                            r.then_inc(S["attn"], 1)
                            pe.wait_ge(S["hs2_a"], i + 1)
                            pe.wait_ge(S["hs2_b"], i + 1)
                            lf[i].pe(pe)
                            pe.wait_ge(S[f"ffn{i}"], 1)
                            for n, (o, w) in enumerate(HCH):
                                mm(bank[3 + 2 * n][0:w], W(f"l1_w1_{i}", lo=HID + o, n=w), nrm[:]).then_inc(S["gp"], 1)
                                mm(bank[2 + 2 * n][0:w], W(f"l1_w1_{i}", lo=o, n=w), nrm[:]).then_inc(S["ap"], 1)
                            for n, (o, w) in enumerate(HCH):
                                pe.wait_ge(S["gg"], 3 * i + n + 1)
                                r = mm(bank[0][:], W(f"l1_w2_{n}_{i}"), gg[n][0:w], n == 0, n == 2)
                            r.then_inc(S["ffn_out"], 1)

                    @block.scalar
                    def _(a):
                        nc.scalar.preload_act_table_set("natural_log_exp_and_others")
                        lx.act(a)
                        for i in range(DEPTH):
                            la[i].act(a)
                            a.wait_ge(S["k"], i + 1)
                            act(k_sb[:], bank[2][:], ACT.Copy, scale=1.0 - 0.95).then_inc(S["k_sb"], 1)
                            a.wait_ge(S["r"], i + 1)
                            act(sr[:], bank[4][:], ACT.Sigmoid).then_inc(S["sr"], 1)
                            nc.scalar.preload_act_table_set("natural_log_exp_and_others")
                        for i in range(DEPTH):
                            if i:
                                nc.scalar.preload_act_table_set("natural_log_exp_and_others")
                            src = xf[i]
                            if i:
                                a.wait_ge(S["x2"], i)
                            a.wait_ge(S["xn"], 1)
                            act(hs[0:64], src[0:64], ACT.Copy).then_inc(S["hs_a"], 1)

                            def root(n):
                                k = 8 * i + n
                                a.wait_ge(S["ss"], k + 1)
                                if k >= 2:
                                    a.wait_ge(S["qk"], k - 1)
                                act(rn[n % 2][:], bank[4 + n % 2][:], ACT.Ln, scale=NORM_SCALE,
                                    bias=C("floor")).then_inc(S["rn_ln"], 1)
                                a.wait_ge(S["rn_ln"], k + 1)
                                act(rn[n % 2][:], rn[n % 2][:], ACT.Exp, scale=-0.5, bias=C("norm_back")).then_inc(S["rn"], 1)

                            for n in range(8):
                                k = 8 * i + n
                                a.wait_ge(S["pj"], k + 1)
                                if n >= 2:
                                    a.wait_ge(S["ss"], k - 1)
                                act(sqq[n % 2][:], bank[n % 2][:], ACT.Square).then_inc(S["sqq"], 1)
                                if n:
                                    root(n - 1)
                            root(7)
                            for q in range(NT):
                                k = NT * i + q
                                a.wait_ge(S["vp"], k + 1)
                                act(vt[:, q, :, 0:DH], bank[6 + q % 2][:].rearrange("p (h d) -> p h d", d=DH),
                                    ACT.Copy).then_inc(S["vt"], 1)
                            for q in range(NT):
                                k = NT * i + q
                                a.wait_ge(S["centred"], k + 1)
                                act(pe_[:, :, WIN:256], pe_[:, :, WIN:256], ACT.Exp).then_inc(S["exp"], 1)
                                for g in range(4):
                                    kk = 4 * k + g
                                    a.wait_ge(S["turned"], kk + 1)
                                    if kk >= 2:
                                        a.wait_ge(S["pv"], kk - 1)
                                    act(pt[kk % 2][:, (0 if q else 1)::(1 if q else 2)],
                                        bank[4 + kk % 2][:].rearrange("p (s t) -> p s t", s=4)[:, (0 if q else 1)::(1 if q else 2)],
                                        ACT.Copy).then_inc(S["pt"], 1)
                                a.wait_ge(S["oturn"], k + 1)
                                act(of[:, :, 128 * q:128 * q + 128], bank[4][:].rearrange("p (g t) -> p g t", g=4),
                                    ACT.Copy).then_inc(S["of"], 1)
                            a.wait_ge(S["x1"], i + 1)
                            act(hs[0:64], x1[0:64], ACT.Copy).then_inc(S["hs2_a"], 1)
                            lf[i].act(a)
                            for n, (o, w) in enumerate(HCH):
                                a.wait_ge(S["gp"], 3 * i + n + 1)
                                if i:
                                    a.wait_ge(S["ffn_out"], i)
                                act(gg[n][0:w], bank[3 + 2 * n][0:w], ACT.Gelu, bias=W(f"l1_b1g{n}_{i}")).then_inc(S["gelu"], 1)
                        a.wait_ge(S["x2"], DEPTH)
                        act(rs[:], xf[2][:], ACT.Silu).then_inc(S["gate"], 1)

                    @block.vector
                    def _(v):
                        lx.dve(v)
                        v.wait_ge(S["xn"], 1)
                        for i in range(DEPTH):
                            la[i].dve(v)
                            v.wait_ge(S["k_sb"], i + 1)
                            v.wait_ge(S["v"], i + 1)
                            tt(kv[:], bank[3][:], k_sb[:], ALU.mult).then_inc(S["kv"], 1)
                            v.wait_ge(S["kv"], i + 1)
                            nc.vector.tensor_tensor_scan(state[:], C("decay"), kv[:], 0.0, ALU.mult,
                                                         ALU.add).then_inc(S["state"], 1)
                            v.wait_ge(S["state"], i + 1)
                            v.wait_ge(S["sr"], i + 1)
                            tt(y[:], state[:], sr[:], ALU.mult).then_inc(S["y"], 1)
                            v.wait_ge(S["wo"], i + 1)
                            tt(h[i + 1][:], h[i][:], bank[5][:], ALU.add).then_inc(S["h"], 1)
                            v.wait_ge(S["h"], i + 1)
                        nc.vector.memset(vt[:, :, :, DH:DH + 1], 1.0).then_inc(S["ones"], 1)
                        nc.vector.memset(pe_[:], 0.0).then_inc(S["zero"], 1)
                        v.wait_ge(S["zero"], 1)
                        for i in range(DEPTH):
                            src = xf[i]
                            nc.vector.memset(hs[64:128, 0:1], 0.0).then_inc(S["pad"], 1)
                            v.wait_ge(S["pad"], 2 * i + 1)
                            nc.vector.tensor_copy(hs[64:128, 1:T], src[64:128, 0:T - 1]).then_inc(S["hs_b"], 1)

                            def turn(n):
                                k = 8 * i + n
                                v.wait_ge(S["rn"], k + 1)
                                v.wait_ge(S["t3"], k + 1)
                                if n == 0 and i:
                                    v.wait_ge(S["score"], 4 * NT * i)
                                stt(qk[:, n * T:(n + 1) * T], rn[n % 2][:], 1e12, t1[n % 2][:], ALU.min,
                                    ALU.mult).then_inc(S["qk"], 1)

                            for n in range(8):
                                k = 8 * i + n
                                table = 4 * i + 2 * (n // 4)
                                v.wait_ge(S["pj"], k + 1)
                                v.wait_ge(S["sqq"], k + 1)
                                if k >= 2:
                                    v.wait_ge(S["qk"], k - 1)
                                tt(t1[n % 2][:], bank[n % 2][:], rot[:, table], ALU.mult).then_inc(S["t1"], 1)
                                v.wait_ge(S["px"], k + 1)
                                if k >= 2:
                                    v.wait_ge(S["t3"], k - 1)
                                tt(t2[n % 2][:], bank[2 + n % 2][:], rot[:, table + 1], ALU.mult).then_inc(S["t2"], 1)
                                if n:
                                    turn(n - 1)
                            turn(7)
                            for q in range(NT):
                                k = NT * i + q
                                n0 = 0 if q else WIN
                                if k:
                                    v.wait_ge(S["turned"], 4 * k)
                                for g in range(4):
                                    v.wait_ge(S["score"], 4 * k + g + 1)
                                    h0 = 4 * (g % 2) + g // 2
                                    stt(pe_[:, h0:h0 + 3:2, WIN + n0:256],
                                        bank[g][:].rearrange("p (a j) -> p a j", a=2)[:, :, n0:KW], 8.0,
                                        C("band")[:, None, n0:KW].to_broadcast([128, 2, KW - n0]),
                                        ALU.mult, ALU.add).then_inc(S["scored"], 1)
                                v.wait_ge(S["scored"], 4 * k + 4)
                                nc.vector.tensor_reduce(nmax[:], pe_[:, :, WIN + n0:256], AX.X, ALU.max).then_inc(S["max"], 1)
                                v.wait_ge(S["max"], k + 1)
                                if q == 0:
                                    nc.vector.memset(pe_[:, :, WIN:2 * WIN], -BIG).then_inc(S["before"], 1)
                                    v.wait_ge(S["before"], i + 1)
                                tt(pe_[:, :, WIN + n0:256], pe_[:, :, WIN + n0:256],
                                   nmax[:, :, None].to_broadcast([128, H1, KW - n0]), ALU.subtract).then_inc(S["centred"], 1)
                                v.wait_ge(S["pv"], 4 * k + 4)
                                for e in range(2):
                                    o = bank[6 + e][:, 0:260].rearrange("p (h d) -> p h d", d=65)
                                    nc.vector.reciprocal(oinv[:, 4 * e:4 * e + 4, None], o[:, :, 64:65]).then_inc(S["oinv"], 1)
                                v.wait_ge(S["oinv"], 2 * k + 2)
                                if k:
                                    v.wait_ge(S["oturn"], k)
                                for e in range(2):
                                    o = bank[6 + e][:, 0:260].rearrange("p (h d) -> p h d", d=65)
                                    r = tt(ot[:, 4 * e:4 * e + 4], o[:, :, 0:64],
                                           oinv[:, 4 * e:4 * e + 4, None].to_broadcast([128, 4, 64]), ALU.mult)
                                r.then_inc(S["ot"], 1)
                            v.wait_ge(S["attn"], i + 1)
                            tt(x1[:], src[:], bank[0][:], ALU.add).then_inc(S["x1"], 1)
                            v.wait_ge(S["x1"], i + 1)
                            nc.vector.memset(hs[64:128, 0:1], 0.0).then_inc(S["pad"], 1)
                            v.wait_ge(S["pad"], 2 * i + 2)
                            nc.vector.tensor_copy(hs[64:128, 1:T], x1[64:128, 0:T - 1]).then_inc(S["hs2_b"], 1)
                            v.wait_ge(S["hs2_a"], i + 1)
                            v.wait_ge(S["hs2_b"], i + 1)
                            lf[i].dve(v)
                            for n, (o, w) in enumerate(HCH):
                                v.wait_ge(S["gelu"], 3 * i + n + 1)
                                v.wait_ge(S["ap"], 3 * i + n + 1)
                                stt(gg[n][0:w], bank[2 + 2 * n][0:w], W(f"l1_b1a{n}_{i}"), gg[n][0:w], ALU.add,
                                    ALU.mult).then_inc(S["gg"], 1)
                            v.wait_ge(S["ffn_out"], i + 1)
                            stt(xf[i + 1][:], bank[0][:], W(f"l1_b2_{i}"), x1[:], ALU.add, ALU.add).then_inc(S["x2"], 1)
                            v.wait_ge(S["x2"], i + 1)
                        v.wait_ge(S["gate"], 1)
                        tt(m[:], rs[:], h[2][:], ALU.mult).then_inc(S["m"], 1)
                        v.wait_ge(S["m"], 1)
                        tt(x[:], x[:], m[:], ALU.add).then_inc(S["x_new"], 1)

                    @block.gpsimd
                    def _(g):
                        for k in range(8 * DEPTH):
                            g.wait_ge(S["t1"], k + 1)
                            g.wait_ge(S["t2"], k + 1)
                            nc.gpsimd.tensor_tensor(t1[k % 2][:], t1[k % 2][:], t2[k % 2][:], ALU.add).then_inc(S["t3"], 1)
                S.clear()

        def layer2():
            with ExitStack() as c:
                S = Steps(nc, c, "l2")
                t = lambda n, f=T: sb("l2_" + n, [128, f], c)
                xc, sq, rs = t("xc"), t("sq"), t("rs")
                lx = Norm(S, "xn", x[:], xn[:], xc[:], sq[:], rs[:], bank[0][:], bank[1][:])
                xp = sb("l2_xp", [128, 2, T + 3], c)
                cv = sb("l2_cv", [128, 2, T], c)
                u, sg, dt, du = (sb("l2_" + n, [128, 2, T], c) for n in ("u", "sg", "dt", "du"))
                xr, xd = t("xr"), t("xd")
                da, db, hh, hc = ([sb(f"l2_{n}{i}", [128, 2, T], c) for i in range(2)] for n in ("da", "db", "h", "hc"))
                cn = [t(f"cn{i}") for i in range(2)]
                lg = sb("l2_lg", [128, NT, NE], c)
                pw = sb("l2_pw", [128, NT, NE], c)
                g3, g4 = (sb("l2_" + n, [128, NT, NE, NE], c) for n in ("gt", "ge"))
                nm = sb("l2_nm", [128, NT], c)
                gt = [sb("l2_gates", [128, NT, NE], c)][0]
                xg = [cv[:, 0], cv[:, 1]]
                h1 = [da[0][:, 0], da[0][:, 1]]
                hg = [db[0][:, 0], db[0][:, 1]]
                with nc.Block() as block:
                    @block.tensor
                    def _(pe):
                        lx.pe(pe)
                        pe.wait_ge(S["xn"], 1)
                        for n in range(4):
                            mm(bank[n][:], W("l2_in", lo=128 * n, n=128), xn[:]).then_inc(S["in"], 1)
                        for q in range(NT):
                            mm(bank[4][:, NE * q:NE * q + NE], xn[:, 128 * q:128 * q + 128], W("l2_router"), True, False)
                            r = mm(bank[4][:, NE * q:NE * q + NE], C("ones_row"), W("l2_router_b"), False, True)
                        r.then_inc(S["logits"], 1)
                        pe.wait_ge(S["u"], 2)
                        for n in range(2):
                            r = mm(bank[5][0:96], W("l2_xproj", lo=96 * n, n=96), u[:, n], n == 0, n == 1)
                        r.then_inc(S["xproj"], 1)
                        pe.wait_ge(S["xsq"], 1)
                        mm(bank[6][0:96], C("rms"), xr[0:96]).then_inc(S["xms"], 1)
                        pe.wait_ge(S["xd"], 1)
                        for n in range(2):
                            mm(bank[n][:], W("l2_dt", lo=128 * n, n=128), xd[0:64]).then_inc(S["dtp"], 1)
                        pe.wait_ge(S["gates"], 1)
                        pe.wait_ge(S["sg"], 2)

                        def gather(n):
                            for k in range(2):
                                pe.wait_ge(S["hc"], n + 1)
                                r = mm(bank[6 + k][:], C("ident"), hc[n % 2][:, k], n == 0, n == NS - 1)
                            r.then_inc(S["y"], 1)

                        for n in range(NS):
                            if n >= 2:
                                pe.wait_ge(S["db"], n - 1)
                                pe.wait_ge(S["cn"], n - 1)
                            mm(bank[2 + n % 2][:], C("ident", 96)[:, R + n:R + n + 1].to_broadcast([96, 128]),
                               xd[0:96]).then_inc(S["Bn"], 1)
                            mm(bank[4 + n % 2][:], C("ident", 96)[:, R + NS + n:R + NS + n + 1].to_broadcast([96, 128]),
                               xd[0:96]).then_inc(S["Cn"], 1)
                            if n:
                                gather(n - 1)
                        gather(NS - 1)
                        pe.wait_ge(S["yg"], 2)
                        for n in range(2):
                            r = mm(bank[0][:], W("l2_out", lo=128 * n, n=128), cv[:, n], n == 0, n == 1)
                        r.then_inc(S["s"], 1)
                        for e in range(NE):
                            if e:
                                pe.wait_ge(S["xg"], e)
                            for q in range(NT):
                                r = mm(bank[1][:, 128 * q:128 * q + 128], gt[:, q, e:e + 1].to_broadcast([128, 128]),
                                       C("ident"))
                            r.then_inc(S["gbc"], 1)

                            def down(k):
                                n = FCH * e + k
                                pe.wait_ge(S["hg"], n + 1)
                                mm(bank[7][:], W(f"l2_w2_{e}", lo=128 * k, n=128), hg[n % 2], n == 0,
                                   n == NE * FCH - 1).then_inc(S["down"], 1)

                            for k in range(FCH):
                                n = FCH * e + k
                                if n >= 2:
                                    pe.wait_ge(S["hg"], n - 1)
                                mm(bank[2 + n % 2][:], W(f"l2_w1_{e}", lo=128 * k, n=128), xn[:]).then_inc(S["w1"], 1)
                                if k == 0:
                                    pe.wait_ge(S["xg"], e + 1)
                                mm(bank[4 + n % 2][:], W(f"l2_w3_{e}", lo=128 * k, n=128), xg[e % 2]).then_inc(S["w3"], 1)
                                if k:
                                    down(k - 1)
                            down(FCH - 1)

                    @block.scalar
                    def _(a):
                        nc.scalar.preload_act_table_set("natural_log_exp_and_others")
                        lx.act(a)
                        for n in range(2):
                            a.wait_ge(S["in"], n + 1)
                            act(xp[:, n, 1:T + 1], bank[n][:], ACT.Copy).then_inc(S["xp"], 1)
                        for n in range(2):
                            a.wait_ge(S["in"], n + 3)
                            act(sg[:, n], bank[2 + n][:], ACT.Silu).then_inc(S["sg"], 1)
                        for n in range(2):
                            a.wait_ge(S["conv"], n + 1)
                            act(u[:, n], cv[:, n], ACT.Silu).then_inc(S["u"], 1)
                        nc.scalar.preload_act_table_set("natural_log_exp_and_others")
                        a.wait_ge(S["centred"], 1)
                        act(pw[:], lg[:], ACT.Exp).then_inc(S["pw"], 1)
                        a.wait_ge(S["xproj"], 1)
                        act(xr[0:96], bank[5][0:96], ACT.Square).then_inc(S["xsq"], 1)
                        a.wait_ge(S["xms"], 1)
                        act(rs[0:96], bank[6][0:96], ACT.Ln, bias=C("eps6", 96)).then_inc(S["xr_ln"], 1)
                        a.wait_ge(S["xr_ln"], 1)
                        act(rs[0:96], rs[0:96], ACT.Exp, scale=-0.5).then_inc(S["xrs"], 1)
                        for n in range(2):
                            a.wait_ge(S["dtz"], n + 1)
                            act(cv[:, n], dt[:, n], ACT.Abs).then_inc(S["dt_abs"], 1)
                        for n in range(2):
                            a.wait_ge(S["dt_abs"], n + 1)
                            act(cv[:, n], cv[:, n], ACT.Exp, scale=-1.0).then_inc(S["dt_exp"], 1)
                        for n in range(2):
                            a.wait_ge(S["dt_exp"], n + 1)
                            act(cv[:, n], cv[:, n], ACT.Ln, bias=C("one")).then_inc(S["dt_ln"], 1)
                        for n in range(NS):
                            if n == 0:
                                a.wait_ge(S["dt"], 2)
                            if n >= 2:
                                a.wait_ge(S["h"], 2 * n - 2)
                            for k in range(2):
                                act(da[n % 2][:, k], dt[:, k], ACT.Exp,
                                    scale=a_neg[:, NS * k + n:NS * k + n + 1]).then_inc(S["da"], 1)
                            a.wait_ge(S["Cn"], n + 1)
                            if n >= 2:
                                a.wait_ge(S["hc"], n - 1)
                            act(cn[n % 2][:], bank[4 + n % 2][:], ACT.Copy).then_inc(S["cn"], 1)
                        a.wait_ge(S["hc"], NS)
                        a.wait_ge(S["h"], 2 * NS)
                        for n in range(NE * FCH):
                            a.wait_ge(S["w1"], n + 1)
                            if n >= 2:
                                a.wait_ge(S["hg"], n - 1)
                            act(h1[n % 2], bank[2 + n % 2][:], ACT.Silu).then_inc(S["h1"], 1)
                        a.wait_ge(S["down"], NE * FCH)
                        act(rs[:], bank[7][:], ACT.Silu).then_inc(S["gate"], 1)

                    @block.vector
                    def _(v):
                        nc.vector.memset(xp[:, :, 0:1], 0.0).then_inc(S["pads"], 1)
                        nc.vector.memset(xp[:, :, T + 1:T + 3], 0.0).then_inc(S["pads"], 1)
                        lx.dve(v)
                        v.wait_ge(S["pads"], 2)
                        for n in range(2):
                            v.wait_ge(S["xp"], n + 1)
                            ts(cv[:, n], xp[:, n, 0:T], W("l2_conv", lo=4 * n, n=1), W("l2_conv_b", lo=n, n=1),
                               ALU.mult, ALU.add).then_inc(S["tap"], 1)
                            for k in range(1, 4):
                                v.wait_ge(S["tap"], 3 * n + k)
                                r = stt(cv[:, n], xp[:, n, k:k + T], W("l2_conv", lo=4 * n + k, n=1), cv[:, n],
                                        ALU.mult, ALU.add)
                                r.then_inc(S["tap"] if k < 3 else S["conv"], 1)
                        v.wait_ge(S["logits"], 1)
                        l4 = bank[4][:, 0:NT * NE].rearrange("p (q e) -> p q e", e=NE)
                        nc.vector.tensor_reduce(nm[:], l4, AX.X, ALU.max).then_inc(S["lmax"], 1)
                        v.wait_ge(S["lmax"], 1)
                        tt(lg[:], l4, nm[:, :, None].to_broadcast([128, NT, NE]), ALU.subtract).then_inc(S["centred"], 1)
                        v.wait_ge(S["pw"], 1)
                        pf = pw[:, :, None, :].to_broadcast([128, NT, NE, NE])
                        pe_ = pw[:, :, :, None].to_broadcast([128, NT, NE, NE])
                        tt(g3[:], pf, pe_, ALU.is_gt).then_inc(S["gt"], 1)
                        tt(g4[:], pf, pe_, ALU.is_ge).then_inc(S["ge"], 1)
                        v.wait_ge(S["gt"], 1)
                        flat = "p q e f -> p (q e f)"
                        tt(g3[:].rearrange(flat), g3[:].rearrange(flat), C("untie"), ALU.mult).then_inc(S["gt"], 1)
                        v.wait_ge(S["ge"], 1)
                        tt(g4[:].rearrange(flat), g4[:].rearrange(flat), C("tie"), ALU.mult).then_inc(S["ge"], 1)
                        v.wait_ge(S["gt"], 2)
                        v.wait_ge(S["ge"], 2)
                        tt(g3[:], g3[:], g4[:], ALU.add).then_inc(S["gt"], 1)
                        v.wait_ge(S["gt"], 3)
                        nc.vector.tensor_reduce(lg[:], g3[:], AX.X, ALU.add).then_inc(S["rank"], 1)
                        v.wait_ge(S["rank"], 1)
                        stt(gt[:], lg[:], 2.0, pw[:], ALU.is_lt, ALU.mult).then_inc(S["kept"], 1)
                        v.wait_ge(S["kept"], 1)
                        nc.vector.tensor_reduce(nm[:], gt[:], AX.X, ALU.add).then_inc(S["gsum"], 1)
                        v.wait_ge(S["gsum"], 1)
                        nc.vector.reciprocal(nm[:], nm[:]).then_inc(S["ginv"], 1)
                        v.wait_ge(S["ginv"], 1)
                        tt(gt[:], gt[:], nm[:, :, None].to_broadcast([128, NT, NE]), ALU.mult).then_inc(S["gates"], 1)
                        v.wait_ge(S["xrs"], 1)
                        stt(xd[0:96], bank[5][0:96], W("l2_xln"), rs[0:96], ALU.mult, ALU.mult).then_inc(S["xd"], 1)
                        for n in range(2):
                            v.wait_ge(S["dtp"], n + 1)
                            ts(dt[:, n], bank[n][:], W("l2_dt_b", lo=n, n=1), None, ALU.add).then_inc(S["dtz"], 1)
                        for n in range(2):
                            v.wait_ge(S["dt_ln"], n + 1)
                            stt(dt[:, n], dt[:, n], 0.0, cv[:, n], ALU.max, ALU.add).then_inc(S["dt"], 1)
                        for n in range(2):
                            v.wait_ge(S["dt"], n + 1)
                            tt(du[:, n], dt[:, n], u[:, n], ALU.mult).then_inc(S["du"], 1)
                        v.wait_ge(S["du"], 2)

                        def scan(n):
                            for k in range(2):
                                v.wait_ge(S["da"], 2 * n + k + 1)
                                v.wait_ge(S["db"], n + 1)
                                if n >= 2:
                                    v.wait_ge(S["hc"], n - 1)
                                nc.vector.tensor_tensor_scan(hh[n % 2][:, k], da[n % 2][:, k], db[n % 2][:, k], 0.0,
                                                             ALU.mult, ALU.add).then_inc(S["h"], 1)

                        for n in range(NS):
                            v.wait_ge(S["Bn"], n + 1)
                            if n >= 2:
                                v.wait_ge(S["h"], 2 * n - 2)
                            tt(db[n % 2][:], du[:], bank[2 + n % 2][:, None, :].to_broadcast([128, 2, T]),
                               ALU.mult).then_inc(S["db"], 1)
                            if n:
                                scan(n - 1)
                        scan(NS - 1)
                        for n in range(2):
                            v.wait_ge(S["y"], NS)
                            stt(du[:, n], u[:, n], W("l2_D", lo=n, n=1), bank[6 + n][:], ALU.mult, ALU.add).then_inc(S["yd"], 1)
                        for n in range(2):
                            v.wait_ge(S["yd"], n + 1)
                            tt(cv[:, n], du[:, n], sg[:, n], ALU.mult).then_inc(S["yg"], 1)
                        for e in range(NE):
                            v.wait_ge(S["gbc"], e + 1)
                            if e == 0:
                                v.wait_ge(S["s"], 1)
                            if e >= 2:
                                v.wait_ge(S["w3"], FCH * (e - 1))
                            tt(xg[e % 2], xn[:], bank[1][:], ALU.mult).then_inc(S["xg"], 1)
                            for k in range(FCH):
                                n = FCH * e + k
                                v.wait_ge(S["h1"], n + 1)
                                v.wait_ge(S["w3"], n + 1)
                                if n >= 2:
                                    v.wait_ge(S["down"], n - 1)
                                tt(hg[n % 2], h1[n % 2], bank[4 + n % 2][:], ALU.mult).then_inc(S["hg"], 1)
                        v.wait_ge(S["gate"], 1)
                        tt(sq[:], rs[:], bank[0][:], ALU.mult).then_inc(S["m"], 1)
                        v.wait_ge(S["m"], 1)
                        tt(x[:], x[:], sq[:], ALU.add).then_inc(S["x_new"], 1)

                    @block.gpsimd
                    def _(g):
                        for n in range(NS):
                            g.wait_ge(S["h"], 2 * n + 2)
                            g.wait_ge(S["cn"], n + 1)
                            if n >= 2:
                                g.wait_ge(S["y"], n - 1)
                            nc.gpsimd.tensor_tensor(hc[n % 2][:], hh[n % 2][:],
                                                    cn[n % 2][:, None, :].to_broadcast([128, 2, T]),
                                                    ALU.mult).then_inc(S["hc"], 1)
                S.clear()

        def layer3():
            with ExitStack() as c:
                S = Steps(nc, c, "l3")
                t = lambda n, f=T: sb("l3_" + n, [128, f], c)
                xc, sq, rs = t("xc"), t("sq"), t("rs")
                lx = Norm(S, "xn", x[:], xn[:], xc[:], sq[:], rs[:], bank[0][:], bank[1][:])
                cp = Coupling(S, "L3", 1, c, (bank[6], bank[7]), xn[:])
                G = 2 * H3
                qk = sb("l3_qk", [128, NT, G * D3], c)
                qk2 = sb("l3_qk2", [128, NT, G * D3], c)
                mu, var, mx = (sb("l3_" + n, [128, NT * G], c) for n in ("mu", "var", "mx"))
                vt = sb("l3_v", [128, NT, H3, D3 + 1], c)
                kt = t("kt")
                qm = sb("l3_qm", [128, 4, T], c)
                qft = t("qft")
                kvm = sb("l3_kvm", [128, H3, D3 + 1], c)
                ol = sb("l3_ol", [128, NT, H3, D3 + 1], c)
                ex, wk_, pp = ([t(f"{n}{i}") for i in range(2)] for n in ("ex", "wk", "pp"))
                sc = [t(f"sc{i}") for i in range(3)]
                pt = [t(f"pt{i}") for i in range(2)]
                m8 = [sb(f"l3_m8{i}", [128, 4, 8], c) for i in range(2)]
                nmx = [sb(f"l3_nmx{i}", [128, 1], c) for i in range(2)]
                zs = sb("l3_zs", [128, NT, H3], c)
                den = sb("l3_den", [128, 2, H3], c)
                zi = sb("l3_zi", [128, NT, H3], c)
                oo = sb("l3_oo", [128, NT, D], c)
                o1 = sb("l3_o1", [128, H3, D3], c)
                of = t("of")
                SC = D3 ** -0.5
                g8 = "p q (g d) -> p (q g) d"
                tiles = [(q, h) for q in range(NT) for h in range(H3)]
                N = len(tiles)
                with nc.Block() as block:
                    @block.tensor
                    def _(pe):
                        lx.pe(pe)
                        pe.wait_ge(S["xn"], 1)
                        for q in range(NT):
                            mm(bank[q][:, 0:384], xn[:, 128 * q:128 * q + 128], W("l3_qkv"), True, False)
                            mm(bank[q][:, 0:384], C("ones_row"), W("l3_bqkv"), False, True).then_inc(S["qkv"], 1)
                        pe.wait_ge(S["qkn"], 1)
                        for part in range(2):
                            for q in range(NT):
                                r = nc.tensor.transpose(bank[4 + part][:, 128 * q:128 * q + 128],
                                                        qk[:, q, 128 * part:128 * part + 128], C("ident"))
                            r.then_inc(S["qk_turn"], 1)
                        pe.wait_ge(S["soft"], 1)
                        pe.wait_ge(S["vt"], NT)
                        pe.wait_ge(S["ones"], 1)
                        for q in range(NT):
                            r = mm(bank[0][:, 0:H3 * 9], qk2[:, q, 128:256], vt[:, q].rearrange("p h d -> p (h d)"),
                                   q == 0, q == NT - 1)
                        r.then_inc(S["kv"], 1)
                        for q in range(NT):
                            r = nc.tensor.transpose(bank[1][:, 128 * q:128 * q + 128], qk2[:, q, 0:128], C("ident"))
                        r.then_inc(S["qf_turn"], 1)
                        pe.wait_ge(S["kvm"], 1)
                        pe.wait_ge(S["qft"], 1)
                        for q in range(NT):
                            r = mm(bank[2 + q // 2][:, 256 * (q % 2):256 * (q % 2) + H3 * 9],
                                   qft[:, 128 * q:128 * q + 128], kvm[:].rearrange("p h d -> p (h d)"))
                        r.then_inc(S["lin"], 1)

                        def score(n):
                            q, h = tiles[n]
                            if n >= 3:
                                pe.wait_ge(S["sc"], n - 2)
                            p0, r = 32 * (h // 4), h % 4
                            mm(bank[n % 3][:], qm[p0:p0 + 32, r, 128 * q:128 * q + 128],
                               kt[p0:p0 + 32, :]).then_inc(S["score"], 1)

                        def values(n):
                            q, h = tiles[n]
                            pe.wait_ge(S["pt"], n + 1)
                            if h == 0 and q:
                                pe.wait_ge(S["os"], q)
                            for k in range(NT):
                                r = mm(bank[5][:, 9 * h:9 * h + 9], pt[n % 2][:, 128 * k:128 * k + 128], vt[:, k, h],
                                       k == 0, k == NT - 1)
                            r.then_inc(S["pv"], 1)

                        pe.wait_ge(S["ol"], 1)
                        pe.wait_ge(S["qm"], 4)
                        pe.wait_ge(S["kt"], 1)
                        score(0)
                        score(1)
                        ff = cp.pe(pe)
                        for n in range(N):
                            if n + 2 < N:
                                score(n + 2)
                            pe.wait_ge(S["pp"], n + 1)
                            if n >= 2:
                                pe.wait_ge(S["pt"], n - 1)
                            for k in range(NT):
                                r = nc.tensor.transpose(bank[3 + n % 2][:, 128 * k:128 * k + 128],
                                                        pp[n % 2][:, 128 * k:128 * k + 128], C("ident"))
                            r.then_inc(S["turned"], 1)
                            if n:
                                values(n - 1)
                            if n % 2:
                                next(ff, None)
                        values(N - 1)
                        for _ in ff:
                            pass
                        pe.wait_ge(S["oo"], NT)
                        for q in range(NT):
                            r = nc.tensor.transpose(bank[0][:, 128 * q:128 * q + 128], oo[:, q], C("ident"))
                        r.then_inc(S["o_turn"], 1)
                        pe.wait_ge(S["of"], 1)
                        mm(bank[1][:], W("l3_proj"), of[:]).then_inc(S["s"], 1)

                    @block.scalar
                    def _(a):
                        def turn_out(a, n):
                            a.wait_ge(S["turned"], n + 1)
                            if n >= 2:
                                a.wait_ge(S["pv"], n - 1)
                            act(pt[n % 2][:], bank[3 + n % 2][:], ACT.Copy).then_inc(S["pt"], 1)

                        nc.scalar.preload_act_table_set("natural_log_exp_and_others")
                        lx.act(a)
                        for q in range(NT):
                            a.wait_ge(S["qkv"], q + 1)
                            act(qk[:, q], bank[q][:, 0:256], ACT.Copy).then_inc(S["qk"], 1)
                            act(vt[:, q, :, 0:D3], bank[q][:, 256:384].rearrange("p (h d) -> p h d", d=D3),
                                ACT.Copy).then_inc(S["vt"], 1)
                        a.wait_ge(S["qkc"], 1)
                        act(qk2[:], qk[:], ACT.Square).then_inc(S["qk_sq"], 1)
                        a.wait_ge(S["qkv_ss"], 1)
                        act(var[:], mu[:], ACT.Ln, scale=1.0 / D3, bias=C("eps5")).then_inc(S["qk_ln"], 1)
                        a.wait_ge(S["qk_ln"], 1)
                        act(var[:], var[:], ACT.Exp, scale=-0.5).then_inc(S["qk_rs"], 1)
                        a.wait_ge(S["qk_turn"], 1)
                        for r in range(4):
                            act(qm[:, r], bank[4][:], ACT.Copy, scale=C("quarter")[:, r:r + 1]).then_inc(S["qm"], 1)
                        a.wait_ge(S["qk_turn"], 2)
                        act(kt[:], bank[5][:], ACT.Copy).then_inc(S["kt"], 1)
                        a.wait_ge(S["soft_c"], 1)
                        act(qk2[:], qk2[:], ACT.Exp).then_inc(S["soft_e"], 1)
                        a.wait_ge(S["qf_turn"], 1)
                        act(qft[:], bank[1][:], ACT.Copy).then_inc(S["qft"], 1)

                        def fetch(n):
                            a.wait_ge(S["score"], n + 1)
                            if n >= 3:
                                a.wait_ge(S["kept"], n - 2)
                            act(sc[n % 3][:], bank[n % 3][:], ACT.Copy).then_inc(S["sc"], 1)

                        ff = cp.act(a)
                        fetch(0)
                        for n in range(N):
                            q, h = tiles[n]
                            if n + 1 < N:
                                fetch(n + 1)
                            a.wait_ge(S["nmx"], n + 1)
                            if n >= 2:
                                a.wait_ge(S["pp"], n - 1)
                            act(ex[n % 2][:], sc[n % 3][:], ACT.Exp, scale=SC, bias=nmx[n % 2][:],
                                accum_out=zs[:, q, h:h + 1]).then_inc(S["ex"], 1)
                            if n:
                                turn_out(a, n - 1)
                            if n % 2:
                                next(ff, None)
                        turn_out(a, N - 1)
                        for _ in ff:
                            pass
                        cp.act_silu(a)
                        a.wait_ge(S["o_turn"], 1)
                        act(of[:], bank[0][:], ACT.Copy).then_inc(S["of"], 1)

                    @block.vector
                    def _(v):
                        def outputs(v, q):
                            v.wait_ge(S["pv"], H3 * (q + 1))
                            v.wait_ge(S["ex"], H3 * (q + 1))
                            o9 = bank[5][:, 0:H3 * 9].rearrange("p (h d) -> p h d", d=9)
                            stt(den[:, 0, :, None], zs[:, q, :, None], 1e-8, o9[:, :, D3:9], ALU.mult, ALU.add).then_inc(S["den"], 1)
                            v.wait_ge(S["den"], 3 * q + 1)
                            nc.vector.reciprocal(den[:, 1], den[:, 0]).then_inc(S["den"], 1)
                            v.wait_ge(S["den"], 3 * q + 2)
                            tt(den[:, 0], den[:, 1], alpha[:, 0], ALU.mult).then_inc(S["den"], 1)
                            v.wait_ge(S["den"], 3 * q + 3)
                            tt(o1[:], o9[:, :, 0:D3], den[:, 0, :, None].to_broadcast([128, H3, D3]), ALU.mult).then_inc(S["os"], 1)
                            v.wait_ge(S["os"], q + 1)
                            tt(oo[:, q].rearrange("p (h d) -> p h d", d=D3), o1[:], ol[:, q, :, 0:D3], ALU.add).then_inc(S["oo"], 1)

                        nc.vector.memset(vt[:, :, :, D3:D3 + 1], 1.0).then_inc(S["ones"], 1)
                        lx.dve(v)
                        v.wait_ge(S["xn"], 1)
                        cp.dve_context(v)
                        v.wait_ge(S["qk"], NT)
                        q3 = qk[:].rearrange(g8, d=D3)
                        s3 = qk2[:].rearrange(g8, d=D3)
                        wide = lambda z: z[:, :, None].to_broadcast([128, NT * G, D3])
                        nc.vector.tensor_reduce(mx[:], q3, AX.X, ALU.add).then_inc(S["qk_sum"], 1)
                        v.wait_ge(S["qk_sum"], 1)
                        ts(mx[:], mx[:], 1.0 / D3, None, ALU.mult).then_inc(S["qk_mu"], 1)
                        v.wait_ge(S["qk_mu"], 1)
                        tt(q3, q3, wide(mx), ALU.subtract).then_inc(S["qkc"], 1)
                        v.wait_ge(S["qk_sq"], 1)
                        nc.vector.tensor_reduce(mu[:], s3, AX.X, ALU.add).then_inc(S["qkv_ss"], 1)
                        v.wait_ge(S["qk_rs"], 1)
                        tt(q3, q3, wide(var), ALU.mult).then_inc(S["qk_n"], 1)
                        v.wait_ge(S["qk_n"], 1)
                        tt(qk[:], qk[:], W("l3_gamma")[:, None, :].to_broadcast([128, NT, 256]), ALU.mult).then_inc(S["qk_n"], 1)
                        v.wait_ge(S["qk_n"], 2)
                        tt(qk[:], qk[:], W("l3_beta")[:, None, :].to_broadcast([128, NT, 256]), ALU.add).then_inc(S["qkn"], 1)
                        v.wait_ge(S["qkn"], 1)
                        nc.vector.tensor_reduce(mx[:], q3, AX.X, ALU.max).then_inc(S["soft_m"], 1)
                        v.wait_ge(S["soft_m"], 1)
                        tt(s3, q3, wide(mx), ALU.subtract).then_inc(S["soft_c"], 1)
                        v.wait_ge(S["soft_e"], 1)
                        nc.vector.tensor_reduce(mu[:], s3, AX.X, ALU.add).then_inc(S["soft_s"], 1)
                        v.wait_ge(S["soft_s"], 1)
                        nc.vector.reciprocal(mu[:], mu[:]).then_inc(S["soft_r"], 1)
                        v.wait_ge(S["soft_r"], 1)
                        tt(s3, s3, wide(mu), ALU.mult).then_inc(S["soft"], 1)
                        v.wait_ge(S["kv"], 1)
                        tt(kvm[:], bank[0][:, 0:H3 * 9].rearrange("p (h d) -> p h d", d=9),
                           C("headcol")[:, :, None].to_broadcast([128, H3, 9]), ALU.mult).then_inc(S["kvm"], 1)
                        v.wait_ge(S["lin"], 1)
                        for f in range(2):
                            r = nc.vector.tensor_copy(ol[:, 2 * f:2 * f + 2],
                                                      bank[2 + f][:].rearrange("p (q c) -> p q c", q=2)[:, :, 0:H3 * 9]
                                                      .rearrange("p q (h d) -> p q h d", d=9))
                        r.then_inc(S["ol"], 1)
                        v.wait_ge(S["ol"], 1)
                        ts(zi[:], ol[:, :, :, D3], 1e-6, None, ALU.add).then_inc(S["zi"], 1)
                        v.wait_ge(S["zi"], 1)
                        nc.vector.reciprocal(zi[:], zi[:]).then_inc(S["zi"], 1)
                        v.wait_ge(S["zi"], 2)
                        tt(zi[:], zi[:], alpha[:, 1][:, None, :].to_broadcast([128, NT, H3]), ALU.mult).then_inc(S["zi"], 1)
                        v.wait_ge(S["zi"], 3)
                        tt(ol[:, :, :, 0:D3].rearrange("p q h d -> p (q h) d"), ol[:, :, :, 0:D3].rearrange("p q h d -> p (q h) d"),
                           zi[:].rearrange("p q h -> p (q h)")[:, :, None].to_broadcast([128, NT * H3, D3]),
                           ALU.mult).then_inc(S["ol2"], 1)
                        ff = cp.dve(v)
                        for n in range(N):
                            q, h = tiles[n]
                            m, w = m8[n % 2], wk_[n % 2]
                            v.wait_ge(S["sc"], n + 1)
                            if n >= 2:
                                v.wait_ge(S["nmx"], n - 1)
                                v.wait_ge(S["kept"], n - 1)
                            nc.vector.max(m[:, 0], sc[n % 3][:]).then_inc(S["top"], 1)
                            for k in range(TOPK // 8):
                                v.wait_ge(S["top"], 4 * n + k + 1)
                                nc.vector.match_replace(w[:], m[:, k], sc[n % 3][:] if k == 0 else w[:],
                                                        -3e38).then_inc(S["rest"], 1)
                                v.wait_ge(S["rest"], 3 * n + k + 1)
                                nc.vector.max(m[:, k + 1], w[:]).then_inc(S["top"], 1)
                            if h == 1 and q:
                                outputs(v, q - 1)
                            if n % 2:
                                next(ff, None)
                        outputs(v, NT - 1)
                        for _ in ff:
                            pass
                        v.wait_ge(S["s"], 1)
                        v.wait_ge(S["gate"], 1)
                        stt(sq[:], bank[1][:], W("l3_bproj"), cp.th[:], ALU.add, ALU.mult).then_inc(S["m"], 1)
                        v.wait_ge(S["m"], 1)
                        tt(x[:], x[:], sq[:], ALU.add).then_inc(S["x_new"], 1)

                    @block.gpsimd
                    def _(g):
                        def smallest_exponent(n):
                            g.wait_ge(S["top"], 4 * n + 1)
                            if n >= 2:
                                g.wait_ge(S["ex"], n - 1)
                            nc.gpsimd.tensor_scalar(nmx[n % 2][:], m8[n % 2][:, 0, 0:1], -SC, None, ALU.mult).then_inc(S["nmx"], 1)

                        smallest_exponent(0)
                        for n in range(N):
                            g.wait_ge(S["top"], 4 * n + 4)
                            if n >= 2:
                                g.wait_ge(S["turned"], n - 1)
                            nc.gpsimd.tensor_scalar(pp[n % 2][:], sc[n % 3][:], m8[n % 2][:, 3, 0:1], None,
                                                    ALU.is_ge).then_inc(S["kept"], 1)
                            if n + 1 < N:
                                smallest_exponent(n + 1)
                            g.wait_ge(S["kept"], n + 1)
                            g.wait_ge(S["ex"], n + 1)
                            nc.gpsimd.tensor_tensor(pp[n % 2][:], pp[n % 2][:], ex[n % 2][:], ALU.mult).then_inc(S["pp"], 1)
                S.clear()

        with nc.Fori(0, B) as b:
            with ExitStack() as c:
                S = Steps(nc, c, "l0")
                t = lambda n: sb("l0_" + n, [128, T], c)
                xc, sq, rs = t("xc"), t("sq"), t("rs")
                ksq, qsq, rk, rq = t("ksq"), t("qsq"), t("rk"), t("rq")
                beta, kn, u, wk, qn, sg = t("beta"), t("kn"), t("u"), t("wk"), t("qn"), t("sg")
                pr = [t(f"pr{i}") for i in range(2)]
                dec = [t(f"dec{i}") for i in range(2)]
                src = [t(f"src{i}") for i in range(2)]
                st = [t(f"st{i}") for i in range(2)]
                sq8 = [t(f"sq8{i}") for i in range(2)]
                og, osb = t("og"), t("osb")
                m = t("m")
                ln = Norm(S, "xn", x[:], xn[:], xc[:], sq[:], rs[:], bank[0][:], bank[1][:])
                lo = Norm(S, "on", osb[:], og[:], xc[:], sq[:], rs[:], bank[0][:], bank[1][:],
                          W("l0_ln_g"), W("l0_ln_b"))
                cp = Coupling(S, "L0", 0, c, (bank[2], bank[3]), xn[:])
                with nc.Block() as block:
                    @block.sync
                    def _(sp):
                        sp.dma_start(x[:], x_in[b]).then_inc(S["x"], 16)

                    @block.tensor
                    def _(pe):
                        pe.wait_ge(S["x"], 16)
                        ln.pe(pe)
                        pe.wait_ge(S["xn"], 1)
                        mm(bank[2][:], W("l0_Wk"), xn[:]).then_inc(S["k"], 1)
                        mm(bank[3][:], W("l0_Wq"), xn[:]).then_inc(S["q"], 1)
                        mm(bank[4][:], W("l0_Wbeta"), xn[:]).then_inc(S["b"], 1)
                        mm(bank[7][:], W("l0_Wg"), xn[:]).then_inc(S["g"], 1)
                        pe.wait_ge(S["ksq"], 1)
                        mm(bank[5][:], C("head8"), ksq[:]).then_inc(S["kss"], 1)
                        pe.wait_ge(S["qsq"], 1)
                        mm(bank[6][:], C("head8"), qsq[:]).then_inc(S["qss"], 1)
                        pe.wait_ge(S["qn"], 1)
                        pe.wait_ge(S["rq"], 1)
                        pe.wait_ge(S["beta"], 1)

                        def gather(i):
                            pe.wait_ge(S["sq8"], i + 1)
                            mm(bank[6][:], C(f"reduce{i}"), sq8[i % 2][:], i == 0, i == 7).then_inc(S["gathered"], 1)

                        for i in range(8):
                            if i >= 2:
                                pe.wait_ge(S["pr"], i - 1)
                                pe.wait_ge(S["src"], i - 1)
                            mm(bank[2 + i % 2][:], W(f"l0_Wkr{i}"), xn[:]).then_inc(S["kr"], 1)
                            mm(bank[4 + i % 2][:], W(f"l0_Wvr{i}"), xn[:]).then_inc(S["vr"], 1)
                            if i:
                                gather(i - 1)
                        gather(7)
                        pe.wait_ge(S["osb"], 1)
                        lo.pe(pe)
                        pe.wait_ge(S["og2"], 1)
                        mm(bank[7][:], W("l0_Wout"), og[:]).then_inc(S["s"], 1)
                        for _ in cp.pe(pe):
                            pass

                    @block.scalar
                    def _(a):
                        nc.scalar.preload_act_table_set("natural_log_exp_and_others")
                        ln.act(a)
                        a.wait_ge(S["k"], 1)
                        act(ksq[:], bank[2][:], ACT.Square).then_inc(S["ksq"], 1)
                        a.wait_ge(S["q"], 1)
                        act(qsq[:], bank[3][:], ACT.Square).then_inc(S["qsq"], 1)
                        a.wait_ge(S["kss"], 1)
                        act(rk[:], bank[5][:], ACT.Ln, scale=NORM_SCALE, bias=C("floor")).then_inc(S["rk_ln"], 1)
                        a.wait_ge(S["qss"], 1)
                        act(rq[:], bank[6][:], ACT.Ln, scale=NORM_SCALE, bias=C("floor")).then_inc(S["rq_ln"], 1)
                        a.wait_ge(S["rk_ln"], 1)
                        act(rk[:], rk[:], ACT.Exp, scale=-0.5, bias=C("norm_back")).then_inc(S["rk"], 1)
                        a.wait_ge(S["rq_ln"], 1)
                        act(rq[:], rq[:], ACT.Exp, scale=-0.5, bias=C("norm_back")).then_inc(S["rq"], 1)
                        a.wait_ge(S["b"], 1)
                        act(beta[:], bank[4][:], ACT.Sigmoid).then_inc(S["beta"], 1)
                        a.wait_ge(S["g"], 1)
                        act(sg[:], bank[7][:], ACT.Silu).then_inc(S["sg"], 1)
                        for i in range(8):
                            a.wait_ge(S["pr"], i + 1)
                            if i >= 2:
                                a.wait_ge(S["st"], i - 1)
                            act(dec[i % 2][:], pr[i % 2][:], ACT.Identity, scale=-1.0, bias=C("one")).then_inc(S["dec"], 1)
                        a.wait_ge(S["gathered"], 8)
                        act(osb[:], bank[6][:], ACT.Copy).then_inc(S["osb"], 1)
                        nc.scalar.preload_act_table_set("natural_log_exp_and_others")
                        lo.act(a)
                        for _ in cp.act(a):
                            pass
                        cp.act_silu(a)

                    @block.vector
                    def _(v):
                        v.wait_ge(S["x"], 16)
                        ln.dve(v)
                        v.wait_ge(S["xn"], 1)
                        cp.dve_context(v)
                        v.wait_ge(S["rk"], 1)
                        ts(rk[:], rk[:], 1e12, None, ALU.min).then_inc(S["rk_c"], 1)
                        v.wait_ge(S["rk_c"], 1)
                        tt(kn[:], bank[2][:], rk[:], ALU.mult).then_inc(S["kn"], 1)
                        v.wait_ge(S["rq"], 1)
                        ts(rq[:], rq[:], 1e12, None, ALU.min).then_inc(S["rq_c"], 1)
                        v.wait_ge(S["rq_c"], 1)
                        tt(qn[:], bank[3][:], rq[:], ALU.mult).then_inc(S["qn"], 1)
                        v.wait_ge(S["beta"], 1)
                        v.wait_ge(S["kn"], 1)
                        tt(u[:], kn[:], beta[:], ALU.mult).then_inc(S["u"], 1)
                        v.wait_ge(S["u"], 1)
                        tt(wk[:], u[:], rk[:], ALU.mult).then_inc(S["wk"], 1)
                        v.wait_ge(S["wk"], 1)

                        def scan(i):
                            v.wait_ge(S["dec"], i + 1)
                            v.wait_ge(S["src"], i + 1)
                            if i >= 2:
                                v.wait_ge(S["sq8"], i - 1)
                            nc.vector.tensor_tensor_scan(st[i % 2][:], dec[i % 2][:], src[i % 2][:], 0.0,
                                                         ALU.mult, ALU.add).then_inc(S["st"], 1)

                        for i in range(8):
                            v.wait_ge(S["kr"], i + 1)
                            if i >= 2:
                                v.wait_ge(S["dec"], i - 1)
                            tt(pr[i % 2][:], bank[2 + i % 2][:], wk[:], ALU.mult).then_inc(S["pr"], 1)
                            v.wait_ge(S["vr"], i + 1)
                            if i >= 2:
                                v.wait_ge(S["st"], i - 1)
                            tt(src[i % 2][:], bank[4 + i % 2][:], u[:], ALU.mult).then_inc(S["src"], 1)
                            if i:
                                scan(i - 1)
                        scan(7)
                        v.wait_ge(S["osb"], 1)
                        lo.dve(v)
                        v.wait_ge(S["on"], 1)
                        v.wait_ge(S["sg"], 1)
                        tt(og[:], og[:], sg[:], ALU.mult).then_inc(S["og2"], 1)
                        for _ in cp.dve(v):
                            pass
                        v.wait_ge(S["gate"], 1)
                        v.wait_ge(S["s"], 1)
                        tt(m[:], bank[7][:], cp.th[:], ALU.mult).then_inc(S["sg_m"], 1)
                        v.wait_ge(S["sg_m"], 1)
                        tt(x[:], x[:], m[:], ALU.add).then_inc(S["x_new"], 1)

                    @block.gpsimd
                    def _(g):
                        g.wait_ge(S["qn"], 1)
                        for i in range(8):
                            g.wait_ge(S["st"], i + 1)
                            if i >= 2:
                                g.wait_ge(S["gathered"], i - 1)
                            nc.gpsimd.tensor_tensor(sq8[i % 2][:], st[i % 2][:], qn[:], ALU.mult).then_inc(S["sq8"], 1)
                S.clear()

            if upto >= 1:
                layer1()
            if upto >= 2:
                layer2()
            if upto >= 3:
                layer3()

            with ExitStack() as c:
                S = Steps(nc, c, "store")
                with nc.Block(no_gpsimd_drain=True) as block:
                    @block.sync
                    def _(sp):
                        sp.dma_start(out[b], x[:]).then_inc(S["out"], 16)
                        sp.wait_ge(S["out"], 16)
                S.clear()


def columns(parts):
    at, found = 0, {}
    for k, v in parts.items():
        found[k] = (at, v.shape[0], v.shape[1])
        at += v.shape[1]
    return found


def kernel(**inputs):
    import numpy as _np
    import concourse.bacc as _bacc
    from concourse.bass_utils import run_bass_kernel_spmd as _run

    a = {k: _np.asarray(v) for k, v in inputs.items()}
    w, c = weights(a), constants()
    arrays = {"x": _np.ascontiguousarray(a["L0_attn_x"].transpose(0, 2, 1)), "weights": packed(w), "consts": packed(c)}
    nc = _bacc.Bacc("TRN2", target_bir_lowering=False, num_devices=1)
    args = [nc.dram_tensor(n + "_dram", v.shape, F32, kind="ExternalInput").ap() for n, v in arrays.items()]
    out = nc.dram_tensor("out_dram", (B, D, T), F32, kind="ExternalOutput").ap()
    build(nc, *args, out, columns(w), columns(c))
    r = _run(nc, [{n + "_dram": v for n, v in arrays.items()}], core_ids=[0])
    return _np.ascontiguousarray(r.results[0]["out_dram"].transpose(0, 2, 1))
```

```python
from contextlib import ExitStack

import numpy as np
import concourse.bass as bass
from concourse import mybir

F32 = mybir.dt.float32
ALU = mybir.AluOpType
ACT = mybir.ActivationFunctionType
AX = mybir.AxisListType

B, T, D = 8, 512, 128
NT = T // 128
LN_EPS = 1e-5
NORM_SCALE = 2.0 ** 36
NORM_FLOOR = 2.0 ** -64
BIG = 1e30

H1, DH, WIN, HID = 8, 64, 64, 341
HCH = [(0, 128), (128, 128), (256, HID - 256)]
NS, R = 16, 64
NE, FCH = 4, 4
H3, D3 = 16, 8
TOPK = max(1, int(T * 0.05))
DEPTH = 2


def constants():
    p = np.arange(128)
    c = {}
    c["ident"] = np.eye(128)
    c["mean"] = np.full((128, 128), 1.0 / 128)
    c["head8"] = (p[:, None] // 8 == p[None] // 8).astype(float)
    c["head64"] = (p[:, None] // 64 == p[None] // 64).astype(float)
    for i in range(8):
        c[f"reduce{i}"] = ((p[:, None] // 8 == p[None] // 8) & (p[None] % 8 == i)).astype(float)
    tw = np.zeros((128, 128))
    r = np.arange(32)
    tw[64 + r, r] = 1
    tw[96 + r, 32 + r] = -1
    tw[r, 64 + r] = -1
    tw[32 + r, 96 + r] = 1
    c["twist"] = tw
    j = np.arange(WIN + 128)
    ok = (j[None] - WIN <= p[:, None]) & (p[:, None] <= j[None])
    c["band"] = np.where(ok, 0.0, -BIG)
    g = np.zeros((96, 96))
    for a, b in ((0, R), (R, R + NS), (R + NS, R + 2 * NS)):
        g[a:b, a:b] = 1.0 / (b - a)
    c["rms"] = g
    e = np.arange(NE)
    low = (e[None, :] < e[:, None]).astype(float).reshape(1, -1)
    c["tie"] = np.repeat(np.tile(low, (1, NT)), 128, 0)
    c["untie"] = 1.0 - c["tie"]
    c["headcol"] = (p[:, None] // 8 == np.arange(16)[None]).astype(float)
    c["group32"] = (p[:, None] // 32 == np.arange(4)[None]).astype(float)
    c["quarter"] = ((p[:, None] // 8) % 4 == np.arange(4)[None]).astype(float)
    c["ones_row"] = np.ones((1, 128))
    c["decay"] = np.full((128, T), 0.95)
    for n, v in (("eps5", 1e-5), ("eps6", 1e-6), ("floor", NORM_FLOOR),
                 ("norm_back", 0.5 * np.log(NORM_SCALE)), ("one", 1.0), ("zero", 0.0)):
        c[n] = np.full((128, 1), v)
    half = np.arange(0, DH, 2, dtype=np.float32)
    inv = (1.0 / 10000.0 ** (half / np.float32(DH))).astype(np.float32)
    t = np.arange(T, dtype=np.float32)
    fr = (t[:, None] * inv[None]).astype(np.float32)
    base = (half + np.float32(0.4 * DH)) / np.float32(1.4 * DH)
    power = (t - T // 2) / np.float32(WIN // 2)
    sc = (base[None] ** power[:, None]).astype(np.float32)
    dup = lambda a: np.tile(np.concatenate([a, a], 1), (1, 2)).T
    sign = np.where(p % 64 < 32, -1.0, 1.0)[:, None]
    c["first_once"] = np.zeros((128, 0))
    c["cos_q"], c["sin_q"] = dup(np.cos(fr) * sc), dup(np.sin(fr) * sc) * sign
    c["cos_k"], c["sin_k"] = dup(np.cos(fr) / sc), dup(np.sin(fr) / sc) * sign
    return {k: np.asarray(v, np.float32) for k, v in c.items()}


def weights(a):
    w = {}
    col = lambda v: np.reshape(v, (-1, 1))
    for n in ("Wq", "Wk", "Wg", "Wout"):
        w["l0_" + n] = a["L0_attn_" + n]
    for i in range(8):
        w[f"l0_Wkr{i}"] = np.repeat(a["L0_attn_Wk"].reshape(128, 16, 8)[:, :, i], 8, 1)
        w[f"l0_Wvr{i}"] = np.repeat(a["L0_attn_Wv"].reshape(128, 16, 8)[:, :, i], 8, 1)
    w["l0_Wbeta"] = np.repeat(a["L0_attn_Wbeta"], 8, 1)
    w["l0_ln_g"], w["l0_ln_b"] = col(a["L0_attn_ln_g"]), col(a["L0_attn_ln_b"])
    for lay in ("L0", "L3"):
        for n in ("cn_w1", "cn_w2", "cn_w3", "gc_w1", "gc_w2"):
            w[f"{lay}_{n}"] = a[f"{lay}_ffn_{n}"]
        for n in ("cn_b1", "cn_b2", "cn_b3", "gc_b1", "gc_b2"):
            w[f"{lay}_{n}"] = col(a[f"{lay}_ffn_{n}"])
        for n in ("cn_w4", "gc_w3"):
            w[f"{lay}_{n}"] = np.repeat(a[f"{lay}_ffn_{n}"], 128, 1)
        for n in ("cn_b4", "gc_b3", "adaptive_range"):
            w[f"{lay}_{n}"] = np.repeat(col(a[f"{lay}_ffn_{n}"]), 128, 0)
    for i in range(DEPTH):
        w[f"l1_ln_w{i}"], w[f"l1_ln_b{i}"] = col(a["L1_attn_ln_w"][i]), col(a["L1_attn_ln_b"][i])
        for n in ("Wk", "Wv", "Wr", "Wo"):
            w[f"l1_{n}{i}"] = a["L1_attn_" + n][i].T
        qkv = a["L1_ffn_wqkv"][i]
        w[f"l1_qkv{i}"] = qkv
        w[f"l1_swap{i}"] = qkv[:, :1024].reshape(128, 16, 2, 32)[:, :, ::-1].reshape(128, 1024)
        for n, s in (("q", "q_scale"), ("k", "k_scale")):
            v = a["L1_ffn_" + s][i]
            w[f"l1_{n}s{i}"] = col(np.concatenate([v, v]))
            w[f"l1_{n}x{i}"] = col(np.concatenate([v[32:], v[:32], v[32:], v[:32]]))
        w[f"l1_wo{i}"] = a["L1_ffn_wo"][i].reshape(4, 128, 128).transpose(1, 0, 2).reshape(128, 512)
        w[f"l1_lg{i}"], w[f"l1_lb{i}"] = col(a["L1_ffn_ln_g"][i]), col(a["L1_ffn_ln_b"][i])
        w[f"l1_w1_{i}"] = a["L1_ffn_w1"][i]
        for c, (o, m) in enumerate(HCH):
            w[f"l1_b1a{c}_{i}"] = col(a["L1_ffn_b1"][i][o:o + m])
            w[f"l1_b1g{c}_{i}"] = col(a["L1_ffn_b1"][i][HID + o:HID + o + m])
            w[f"l1_w2_{c}_{i}"] = a["L1_ffn_w2"][i][o:o + m]
        w[f"l1_b2_{i}"] = col(a["L1_ffn_b2"][i])
    w["l2_in"] = a["L2_attn_in_proj_w"].T
    two = lambda v: v.reshape(2, 128, -1).transpose(1, 0, 2).reshape(128, -1)
    w["l2_conv"] = two(a["L2_attn_conv_w"].reshape(256, 4))
    w["l2_conv_b"], w["l2_D"], w["l2_dt_b"] = (two(a["L2_attn_" + n]) for n in ("conv_b", "D", "dt_proj_b"))
    w["l2_xproj"] = two(a["L2_attn_x_proj_w"].T)
    w["l2_xln"] = col(np.concatenate([a["L2_attn_dt_ln_w"], a["L2_attn_b_ln_w"], a["L2_attn_c_ln_w"]]))
    w["l2_dt"] = a["L2_attn_dt_proj_w"].T
    w["l2_alog"] = two(a["L2_attn_A_log"])
    w["l2_out"] = two(a["L2_attn_out_proj_w"].T)
    w["l2_router"] = a["L2_ffn_router_w"]
    w["l2_router_b"] = a["L2_ffn_router_b"].reshape(1, NE)
    for e in range(NE):
        w[f"l2_w1_{e}"], w[f"l2_w3_{e}"] = a["L2_ffn_w1"][e], a["L2_ffn_w3"][e]
        w[f"l2_w2_{e}"] = a["L2_ffn_w2"][e].reshape(4, 128, 128).transpose(1, 0, 2).reshape(128, 512)
    w["l3_qkv"] = a["L3_attn_Wqkv"].T
    w["l3_bqkv"] = a["L3_attn_bqkv"].reshape(1, 384)
    for n in ("gamma", "beta"):
        row = np.concatenate([np.tile(a[f"L3_attn_{p}_{n}"], H3) for p in "qk"])
        w["l3_" + n] = np.repeat(row.reshape(1, -1), 128, 0)
    w["l3_alpha"] = np.repeat(a["L3_attn_alpha"].reshape(1, 16), 128, 0)
    w["l3_proj"] = a["L3_attn_Wproj"].T
    w["l3_bproj"] = col(a["L3_attn_bproj"])
    return w


def packed(parts):
    out = np.zeros((128, sum(v.shape[1] for v in parts.values())), np.float32)
    at = 0
    for v in parts.values():
        out[:v.shape[0], at:at + v.shape[1]] = v
        at += v.shape[1]
    return out


class Steps:

    def __init__(self, nc, ctx, layer):
        self.nc, self.ctx, self.layer, self.all = nc, ctx, layer, {}

    def __getitem__(self, name):
        if name not in self.all:
            self.all[name] = self.ctx.enter_context(self.nc.semaphore(f"{self.layer}_{name}"))
        return self.all[name]

    def clear(self):
        engines = (self.nc.sync, self.nc.scalar, self.nc.vector, self.nc.gpsimd, self.nc.tensor)
        for n, s in enumerate(self.all.values()):
            engines[n % 5].sem_clear(s)
        self.nc.all_engine_barrier()


def build(nc, x_in, w_in, c_in, out, wcols, ccols, upto=99, probe=None):
    ctx = ExitStack()

    def sb(name, shape, c=None):
        return (c or ctx).enter_context(nc.sbuf_tensor(name, shape, F32))

    with ctx:
        w_sb = sb("weights", [128, w_in.shape[1]])
        once = ccols["first_once"][0]
        c_sb = sb("consts", [128, once])
        bank = [ctx.enter_context(nc.psum_tensor(f"bank{i}", [128, 512], F32)) for i in range(8)]
        x = sb("x", [128, T])
        xn = sb("xn", [128, T])
        rot = sb("rot", [128, DEPTH * 4, T])
        a_neg = sb("a_neg", [128, 2 * NS])
        alpha = sb("alpha", [128, 2, H3])
        couple = sb("couple", [128, 2, 4])

        def W(name, r=None, lo=0, n=None):
            o, rows, cols = wcols[name]
            return w_sb[0:(r or rows), o + lo:o + lo + (cols - lo if n is None else n)]

        def C(name, r=None):
            o, rows, cols = ccols[name]
            return c_sb[0:(r or rows), o:o + cols]

        def mm(o, lhsT, rhs, start=True, stop=True):
            return nc.tensor.matmul(o, lhsT, rhs, start=start, stop=stop)

        act = nc.scalar.activation
        tt, ts, stt = nc.vector.tensor_tensor, nc.vector.tensor_scalar, nc.vector.scalar_tensor_tensor

        with ExitStack() as c0:
            S = Steps(nc, c0, "setup")
            tables = sb("rotary", [128, c_in.shape[1] - once], c0)
            with nc.Block(no_gpsimd_drain=True) as block:
                @block.sync
                def _(sp):
                    sp.dma_start(w_sb[:], w_in).then_inc(S["loaded"], 16)
                    sp.dma_start(c_sb[:], c_in[:, 0:once]).then_inc(S["loaded"], 16)
                    sp.dma_start(tables[:], c_in[:, once:]).then_inc(S["loaded"], 16)

                @block.scalar
                def _(a):
                    a.wait_ge(S["loaded"], 48)
                    act(a_neg[:], W("l2_alog"), ACT.Exp).then_inc(S["exp_a"], 1)
                    act(alpha[:, 0], W("l3_alpha"), ACT.Sigmoid).then_inc(S["alpha"], 1)

                @block.vector
                def _(v):
                    v.wait_ge(S["loaded"], 48)
                    for i in range(DEPTH):
                        for n, (table, scale) in enumerate((("cos_q", "qs"), ("sin_q", "qx"), ("cos_k", "ks"), ("sin_k", "kx"))):
                            o = ccols[table][0] - once
                            ts(rot[:, 4 * i + n], tables[:, o:o + T], W(f"l1_{scale}{i}"), None, ALU.mult)
                    for n, lay in enumerate(("L0", "L3")):
                        ts(couple[:, n, 0:1], W(f"{lay}_cn_b4"), 0.5, None, ALU.mult)
                        ts(couple[:, n, 1:2], W(f"{lay}_adaptive_range"), 2.0, None, ALU.mult)
                        ts(couple[:, n, 2:3], W(f"{lay}_adaptive_range"), 0.3, None, ALU.mult)
                        ts(couple[:, n, 3:4], W(f"{lay}_gc_b3"), 0.5, None, ALU.mult)
                    v.wait_ge(S["exp_a"], 1)
                    ts(a_neg[:], a_neg[:], -1.0, None, ALU.mult)
                    v.wait_ge(S["alpha"], 1)
                    ts(alpha[:, 1], alpha[:, 0], -1.0, 1.0, ALU.mult, ALU.add)
            S.clear()

        class Norm:

            def __init__(self, S, name, src, dst, xc, sq, rs, mu_bank, var_bank, gain=None, shift=None):
                self.S, self.n, self.src, self.dst, self.xc, self.sq, self.rs = S, name, src, dst, xc, sq, rs
                self.mu, self.var, self.gain, self.shift = mu_bank, var_bank, gain, shift

            def pe(self, pe):
                mm(self.mu, C("mean"), self.src).then_inc(self.S[self.n + "_mu"], 1)
                pe.wait_ge(self.S[self.n + "_sq"], 1)
                mm(self.var, C("mean"), self.sq).then_inc(self.S[self.n + "_var"], 1)

            def act(self, a):
                a.wait_ge(self.S[self.n + "_xc"], 1)
                act(self.sq, self.xc, ACT.Square).then_inc(self.S[self.n + "_sq"], 1)
                a.wait_ge(self.S[self.n + "_var"], 1)
                act(self.rs, self.var, ACT.Ln, bias=C("eps5")).then_inc(self.S[self.n + "_ln"], 1)
                a.wait_ge(self.S[self.n + "_ln"], 1)
                act(self.rs, self.rs, ACT.Exp, scale=-0.5).then_inc(self.S[self.n + "_rs"], 1)

            def dve(self, v):
                v.wait_ge(self.S[self.n + "_mu"], 1)
                tt(self.xc, self.src, self.mu, ALU.subtract).then_inc(self.S[self.n + "_xc"], 1)
                v.wait_ge(self.S[self.n + "_rs"], 1)
                if self.gain is None:
                    tt(self.dst, self.xc, self.rs, ALU.mult).then_inc(self.S[self.n], 1)
                else:
                    stt(self.dst, self.xc, self.gain, self.rs, ALU.mult, ALU.mult).then_inc(self.S[self.n + "_g"], 1)
                    v.wait_ge(self.S[self.n + "_g"], 1)
                    ts(self.dst, self.dst, self.shift, None, ALU.add).then_inc(self.S[self.n], 1)

        class Coupling:

            def __init__(self, S, lay, n, c, banks, src):
                self.S, self.lay, self.n, self.b, self.src = S, lay, n, banks, src
                self.o = [sb(f"{lay}_cyc{k}", [128, T], c) for k in range(3)]
                self.h1, self.h2, self.h3, self.th, self.m = (
                    sb(f"{lay}_ff{k}", [128, T], c) for k in range(5))
                self.sm = sb(f"{lay}_ctx", [128, 8], c)

            def pe(self, pe):
                S, lay, b, sm = self.S, self.lay, self.b, self.sm
                pe.wait_ge(S["ctx"], 1)
                mm(b[0][0:64, 0:1], W(lay + "_gc_w1"), sm[:, 0:1]).then_inc(S["gc1"], 1)
                yield
                pe.wait_ge(S["gc1_gelu"], 1)
                mm(b[0][0:32, 0:1], W(lay + "_gc_w2"), sm[0:64, 1:2]).then_inc(S["gc2"], 1)
                yield
                pe.wait_ge(S["gc2_gelu"], 1)
                mm(b[0][:, 0:1], W(lay + "_gc_w3"), sm[0:32, 2:3]).then_inc(S["gc3"], 1)
                yield
                for k in range(3):
                    src = self.src if k == 0 else self.o[k - 1][:]
                    if k:
                        yield
                    pe.wait_ge(S["gc3_tanh"] if k == 0 else S["cycle"], max(k, 1))
                    mm(b[0][:], W(lay + "_cn_w1"), src).then_inc(S["cn1"], 1)
                    mm(b[1][:], C("twist"), src).then_inc(S["twist"], 1)
                    yield
                    pe.wait_ge(S["cn1_gelu"], k + 1)
                    mm(b[0][0:64], W(lay + "_cn_w2"), self.h1[:]).then_inc(S["cn2"], 1)
                    yield
                    pe.wait_ge(S["cn2_gelu"], k + 1)
                    mm(b[0][0:32], W(lay + "_cn_w3"), self.h2[0:64]).then_inc(S["cn3"], 1)
                    yield
                    pe.wait_ge(S["cn3_gelu"], k + 1)
                    mm(b[0][:], W(lay + "_cn_w4"), self.h3[0:32]).then_inc(S["cn4"], 1)
                    yield

            def act(self, a):
                S, lay, b, sm, n = self.S, self.lay, self.b, self.sm, self.n
                a.wait_ge(S["gc1"], 1)
                act(sm[0:64, 1:2], b[0][0:64, 0:1], ACT.Gelu, bias=W(lay + "_gc_b1")).then_inc(S["gc1_gelu"], 1)
                yield
                a.wait_ge(S["gc2"], 1)
                act(sm[0:32, 2:3], b[0][0:32, 0:1], ACT.Gelu, bias=W(lay + "_gc_b2")).then_inc(S["gc2_gelu"], 1)
                yield
                a.wait_ge(S["gc3"], 1)
                act(sm[:, 3:4], b[0][:, 0:1], ACT.Tanh, bias=couple[:, n, 3:4], scale=0.5).then_inc(S["gc3_tanh"], 1)
                yield
                for k in range(3):
                    if k:
                        yield
                    a.wait_ge(S["cn1"], k + 1)
                    act(self.h1[:], b[0][:], ACT.Gelu, bias=W(lay + "_cn_b1")).then_inc(S["cn1_gelu"], 1)
                    yield
                    a.wait_ge(S["cn2"], k + 1)
                    act(self.h2[0:64], b[0][0:64], ACT.Gelu, bias=W(lay + "_cn_b2")).then_inc(S["cn2_gelu"], 1)
                    yield
                    a.wait_ge(S["cn3"], k + 1)
                    act(self.h3[0:32], b[0][0:32], ACT.Gelu, bias=W(lay + "_cn_b3")).then_inc(S["cn3_gelu"], 1)
                    yield
                    a.wait_ge(S["cn4"], k + 1)
                    if k > 0:
                        a.wait_ge(S["cycle_c"], k)
                    act(self.th[:], b[0][:], ACT.Tanh, bias=couple[:, n, 0:1], scale=0.5).then_inc(S["tanh"], 1)
                    yield

            def act_silu(self, a):
                a.wait_ge(self.S["cycle"], 3)
                act(self.th[:], self.o[2][:], ACT.Silu).then_inc(self.S["gate"], 1)

            def dve_context(self, v):
                S, sm = self.S, self.sm
                nc.vector.reduce_sum(sm[:, 4:5], self.src, AX.X).then_inc(S["ctx_sum"], 1)
                v.wait_ge(S["ctx_sum"], 1)
                ts(sm[:, 0:1], sm[:, 4:5], 1.0 / T, None, ALU.mult).then_inc(S["ctx"], 1)

            def dve(self, v):
                S, b, sm, n = self.S, self.b, self.sm, self.n
                for _ in range(3):
                    yield
                v.wait_ge(S["gc3_tanh"], 1)
                ts(sm[:, 5:6], sm[:, 3:4], 0.35, 0.35 - 0.5, ALU.mult, ALU.add).then_inc(S["base_a"], 1)
                v.wait_ge(S["base_a"], 1)
                stt(sm[:, 6:7], sm[:, 5:6], couple[:, n, 1:2], couple[:, n, 2:3], ALU.mult, ALU.add).then_inc(S["base_b"], 1)
                v.wait_ge(S["base_b"], 1)
                ts(sm[:, 7:8], sm[:, 6:7], 0.1, None, ALU.add).then_inc(S["base"], 1)
                v.wait_ge(S["base"], 1)
                for k in range(3):
                    src = self.src if k == 0 else self.o[k - 1][:]
                    for _ in range(5 if k else 4):
                        yield
                    v.wait_ge(S["tanh"], k + 1)
                    ts(self.m[:], self.th[:], couple[:, n, 2:3], sm[:, 7:8], ALU.mult, ALU.add).then_inc(S["cycle_c"], 1)
                    v.wait_ge(S["cycle_c"], k + 1)
                    v.wait_ge(S["twist"], k + 1)
                    tt(self.m[:], self.m[:], b[1][:], ALU.mult).then_inc(S["cycle_m"], 1)
                    v.wait_ge(S["cycle_m"], k + 1)
                    tt(self.o[k][:], src, self.m[:], ALU.add).then_inc(S["cycle"], 1)

        def layer1():
            with ExitStack() as c:
                S = Steps(nc, c, "l1")
                t = lambda n, f=T: sb("l1_" + n, [128, f], c)
                xc, sq, rs = t("xc"), t("sq"), t("rs")
                k_sb, kv, state, sr, y = t("k"), t("kv"), t("state"), t("sr"), t("y")
                h = [xn] + [t(f"h{i}") for i in range(DEPTH)]
                nrm = t("nrm")
                lx = Norm(S, "xn", x[:], xn[:], xc[:], sq[:], rs[:], bank[0][:], bank[1][:])
                xf = [xn] + [t(f"f{i}") for i in range(DEPTH)]
                x1 = t("x1")
                hs = t("hs")
                qk = t("qk", 8 * T)
                of = sb("l1_of", [128, 4, T], c)
                sqq, t1 = [of[:, 0], of[:, 1]], [of[:, 2], of[:, 3]]
                rn, t2 = ([t(f"{n}{i}") for i in range(2)] for n in ("rn", "t2_"))
                vt = sb("l1_v", [128, NT, H1 + 1, DH + 1], c)
                KW = WIN + 128
                pe_ = [sb(f"l1_probs{e}", [128, 4, 256], c) for e in range(2)]
                nmax = [sb(f"l1_nmax{e}", [128, 4], c) for e in range(2)]
                NU = 2 * NT
                pt = [sb(f"l1_pt{i}", [128, 4, 128], c) for i in range(2)]
                oinv = sb("l1_oinv", [128, H1], c)
                ot = sb("l1_ot", [128, H1, DH], c)
                gg = [k_sb, kv, sr]
                m = state
                lf = [Norm(S, f"ffn{i}", hs[:], nrm[:], xc[:], sq[:], rs[:], bank[0][:], bank[1][:],
                           W(f"l1_lg{i}"), W(f"l1_lb{i}")) for i in range(DEPTH)]
                with nc.Block(no_gpsimd_drain=True) as block:
                    @block.tensor
                    def _(pe):
                        def score(i, u):
                            q, e = u // 2, u % 2
                            k = NU * i + u
                            lo = 128 * q - WIN if q else 0
                            n0 = 0 if q else WIN
                            if u >= 2:
                                pe.wait_ge(S["scored"], 2 * (k - 1))
                            for f in range(2):
                                for s in range(2):
                                    g = 2 * f + s
                                    r = mm(bank[2 * e + f][:, 256 * s + n0:256 * s + KW],
                                           qk[64 * e:64 * e + 64, g * T + 128 * q:g * T + 128 * q + 128],
                                           qk[64 * e:64 * e + 64, (4 + g) * T + lo:(4 + g) * T + 128 * q + 128])
                                r.then_inc(S["score"], 1)

                        def attend(i, u):
                            q, e = u // 2, u % 2
                            k = NU * i + u
                            parts = (0, 1) if q else (1,)
                            pe.wait_ge(S["exp"], k + 1)
                            if k:
                                pe.wait_ge(S["pt"], 2 * k)
                            if e and q:
                                pe.wait_ge(S["of"], NT * i + q)
                            for f in range(2):
                                for s in range(2):
                                    for d in parts:
                                        r = nc.tensor.transpose(bank[4 + f][:, 128 * (2 * s + d):128 * (2 * s + d) + 128],
                                                                pe_[e][:, 2 * f + s, 128 * d:128 * d + 128], C("ident"))
                                r.then_inc(S["turned"], 1)
                            if u >= 2:
                                pe.wait_ge(S["ot"], k - 1)
                            for f in range(2):
                                pe.wait_ge(S["pt"], 2 * k + f + 1)
                                for s in range(2):
                                    j = 2 * f + s
                                    for d in parts:
                                        r = mm(bank[6 + e][:, 65 * j:65 * j + 130], pt[f][:, 2 * s + d],
                                               vt[:, q - 1 + d, 2 * j + e:2 * j + e + 2, :].rearrange("p h d -> p (h d)"),
                                               d == parts[0], d == 1)
                                r.then_inc(S["pv"], 1)

                        def turn_outputs(i, q):
                            pe.wait_ge(S["ot"], NU * i + 2 * q + 2)
                            for g in range(4):
                                r = nc.tensor.transpose(bank[4][:, 128 * g:128 * g + 128],
                                                        ot[:, 2 * g:2 * g + 2, :].rearrange("p a d -> p (a d)"), C("ident"))
                            r.then_inc(S["oturn"], 1)

                        lx.pe(pe)
                        def time_mix(i):
                            pe.wait_ge(S["xn"] if i == 0 else S["h"], 1)
                            mm(bank[6][:], C("mean"), h[i][:]).then_inc(S["mix_mu"], 1)
                            yield
                            pe.wait_ge(S["mix_sq"], i + 1)
                            mm(bank[7][:], C("mean"), sq[:]).then_inc(S["mix_var"], 1)
                            yield
                            pe.wait_ge(S["mix"], i + 1)
                            mm(bank[6][:], W(f"l1_Wk{i}"), nrm[:]).then_inc(S["k"], 1)
                            mm(bank[7][:], W(f"l1_Wv{i}"), nrm[:]).then_inc(S["v"], 1)
                            yield
                            pe.wait_ge(S["k_sb"], i + 1)
                            mm(bank[6][:], W(f"l1_Wr{i}"), nrm[:]).then_inc(S["r"], 1)
                            yield
                            pe.wait_ge(S["y"], i + 1)
                            mm(bank[7][:], W(f"l1_Wo{i}"), y[:]).then_inc(S["wo"], 1)

                        for i in range(DEPTH):
                            pe.wait_ge(S["hs_a"], i + 1)
                            pe.wait_ge(S["hs_b"], i + 1)

                            def project(n):
                                k = 8 * i + n
                                if n >= 2:
                                    pe.wait_ge(S["t1"], k - 1)
                                    pe.wait_ge(S["t2"], k - 1)
                                mm(bank[n % 2][:], W(f"l1_qkv{i}", lo=128 * n, n=128), hs[:]).then_inc(S["pj"], 1)
                                mm(bank[2 + n % 2][:], W(f"l1_swap{i}", lo=128 * n, n=128), hs[:]).then_inc(S["px"], 1)

                            def norms(n):
                                k = 8 * i + n
                                pe.wait_ge(S["sqq"], k + 1)
                                if n >= 2:
                                    pe.wait_ge(S["rn_ln"], k - 1)
                                mm(bank[4 + n % 2][:], C("head64"), sqq[n % 2][:]).then_inc(S["ss"], 1)

                            mix = time_mix(i)
                            for n in range(8):
                                project(n)
                                if n:
                                    norms(n - 1)
                                next(mix, None)
                            norms(7)
                            pe.wait_ge(S["h"], i + 1)
                            for q in range(NT):
                                k = NT * i + q
                                if q >= 2:
                                    pe.wait_ge(S["vt"], k - 1)
                                mm(bank[6 + q % 2][:], hs[:, 128 * q:128 * q + 128],
                                   W(f"l1_qkv{i}", lo=1024)).then_inc(S["vp"], 1)
                            pe.wait_ge(S["qk"], 8 * (i + 1))
                            pe.wait_ge(S["ones"], 2)
                            score(i, 0)
                            pe.wait_ge(S["rn"], 8 * (i + 1))
                            pe.wait_ge(S["vt"], NT * (i + 1))
                            for u in range(NU):
                                if u + 1 < NU:
                                    score(i, u + 1)
                                attend(i, u)
                                if u % 2 == 0 and u:
                                    turn_outputs(i, u // 2 - 1)
                            turn_outputs(i, NT - 1)
                            pe.wait_ge(S["of"], NT * (i + 1))
                            for g in range(4):
                                r = mm(bank[0][:], W(f"l1_wo{i}", lo=128 * g, n=128), of[:, g], g == 0, g == 3)
                            r.then_inc(S["attn"], 1)
                            pe.wait_ge(S["hs2_a"], i + 1)
                            pe.wait_ge(S["hs2_b"], i + 1)
                            lf[i].pe(pe)
                            pe.wait_ge(S[f"ffn{i}"], 1)
                            for n, (o, w) in enumerate(HCH):
                                mm(bank[3 + 2 * n][0:w], W(f"l1_w1_{i}", lo=HID + o, n=w), nrm[:]).then_inc(S["gp"], 1)
                                mm(bank[2 + 2 * n][0:w], W(f"l1_w1_{i}", lo=o, n=w), nrm[:]).then_inc(S["ap"], 1)
                            for n, (o, w) in enumerate(HCH):
                                pe.wait_ge(S["gg"], 3 * i + n + 1)
                                r = mm(bank[0][:], W(f"l1_w2_{n}_{i}"), gg[n][0:w], n == 0, n == 2)
                            r.then_inc(S["ffn_out"], 1)

                    @block.scalar
                    def _(a):
                        nc.scalar.preload_act_table_set("natural_log_exp_and_others")
                        lx.act(a)
                        def time_mix(i):
                            a.wait_ge(S["mix_xc"], i + 1)
                            act(sq[:], xc[:], ACT.Square).then_inc(S["mix_sq"], 1)
                            yield
                            a.wait_ge(S["mix_var"], i + 1)
                            act(rs[:], bank[7][:], ACT.Ln, bias=C("eps5")).then_inc(S["mix_ln"], 1)
                            a.wait_ge(S["mix_ln"], i + 1)
                            act(rs[:], rs[:], ACT.Exp, scale=-0.5).then_inc(S["mix_rs"], 1)
                            yield
                            a.wait_ge(S["k"], i + 1)
                            act(k_sb[:], bank[6][:], ACT.Copy, scale=1.0 - 0.95).then_inc(S["k_sb"], 1)
                            yield
                            a.wait_ge(S["r"], i + 1)
                            act(sr[:], bank[6][:], ACT.Sigmoid).then_inc(S["sr"], 1)
                            nc.scalar.preload_act_table_set("natural_log_exp_and_others")

                        for i in range(DEPTH):
                            if i:
                                nc.scalar.preload_act_table_set("natural_log_exp_and_others")
                            src = xf[i]
                            if i:
                                a.wait_ge(S["x2"], i)
                            a.wait_ge(S["xn"], 1)
                            act(hs[0:64], src[0:64], ACT.Copy).then_inc(S["hs_a"], 1)

                            def root(n):
                                k = 8 * i + n
                                a.wait_ge(S["ss"], k + 1)
                                if k >= 2:
                                    a.wait_ge(S["qk"], k - 1)
                                act(rn[n % 2][:], bank[4 + n % 2][:], ACT.Ln, scale=NORM_SCALE,
                                    bias=C("floor")).then_inc(S["rn_ln"], 1)
                                a.wait_ge(S["rn_ln"], k + 1)
                                act(rn[n % 2][:], rn[n % 2][:], ACT.Exp, scale=-0.5, bias=C("norm_back")).then_inc(S["rn"], 1)

                            mix = time_mix(i)
                            for n in range(8):
                                k = 8 * i + n
                                a.wait_ge(S["pj"], k + 1)
                                if n >= 2:
                                    a.wait_ge(S["ss"], k - 1)
                                act(sqq[n % 2][:], bank[n % 2][:], ACT.Square).then_inc(S["sqq"], 1)
                                if n:
                                    root(n - 1)
                                next(mix, None)
                            root(7)
                            for q in range(NT):
                                k = NT * i + q
                                a.wait_ge(S["vp"], k + 1)
                                act(vt[:, q, 0:H1, 0:DH], bank[6 + q % 2][:].rearrange("p (h d) -> p h d", d=DH),
                                    ACT.Copy).then_inc(S["vt"], 1)
                            def outputs_back(q):
                                a.wait_ge(S["oturn"], NT * i + q + 1)
                                act(of[:, :, 128 * q:128 * q + 128], bank[4][:].rearrange("p (g t) -> p g t", g=4),
                                    ACT.Copy).then_inc(S["of"], 1)

                            for u in range(NU):
                                q, e = u // 2, u % 2
                                k = NU * i + u
                                n0 = WIN if q else 2 * WIN
                                a.wait_ge(S["centred"], k + 1)
                                act(pe_[e][:, :, n0:256], pe_[e][:, :, n0:256], ACT.Exp).then_inc(S["exp"], 1)
                                for f in range(2):
                                    a.wait_ge(S["turned"], 2 * k + f + 1)
                                    if k:
                                        a.wait_ge(S["pv"], 2 * (k - 1) + f + 1)
                                    act(pt[f][:, (0 if q else 1)::(1 if q else 2)],
                                        bank[4 + f][:].rearrange("p (s t) -> p s t", s=4)[:, (0 if q else 1)::(1 if q else 2)],
                                        ACT.Copy).then_inc(S["pt"], 1)
                                if e == 0 and q:
                                    outputs_back(q - 1)
                            outputs_back(NT - 1)
                            a.wait_ge(S["x1"], i + 1)
                            act(hs[0:64], x1[0:64], ACT.Copy).then_inc(S["hs2_a"], 1)
                            lf[i].act(a)
                            for n, (o, w) in enumerate(HCH):
                                a.wait_ge(S["gp"], 3 * i + n + 1)
                                if i:
                                    a.wait_ge(S["ffn_out"], i)
                                act(gg[n][0:w], bank[3 + 2 * n][0:w], ACT.Gelu, bias=W(f"l1_b1g{n}_{i}")).then_inc(S["gelu"], 1)
                        a.wait_ge(S["x2"], DEPTH)
                        act(rs[:], xf[2][:], ACT.Silu).then_inc(S["gate"], 1)

                    @block.vector
                    def _(v):
                        nc.vector.memset(vt[:, :, 0:H1, DH:DH + 1], 1.0).then_inc(S["ones"], 1)
                        nc.vector.memset(vt[:, :, H1:], 0.0).then_inc(S["ones"], 1)
                        for e in range(2):
                            nc.vector.memset(pe_[e][:], 0.0).then_inc(S["zero"], 1)
                        v.wait_ge(S["zero"], 2)
                        lx.dve(v)
                        v.wait_ge(S["xn"], 1)
                        def time_mix(i):
                            src = h[i][:]
                            v.wait_ge(S["mix_mu"], i + 1)
                            tt(xc[:], src, bank[6][:], ALU.subtract).then_inc(S["mix_xc"], 1)
                            yield
                            v.wait_ge(S["mix_rs"], i + 1)
                            stt(nrm[:], xc[:], W(f"l1_ln_w{i}"), rs[:], ALU.mult, ALU.mult).then_inc(S["mix_g"], 1)
                            v.wait_ge(S["mix_g"], i + 1)
                            ts(nrm[:], nrm[:], W(f"l1_ln_b{i}"), None, ALU.add).then_inc(S["mix"], 1)
                            yield
                            v.wait_ge(S["k_sb"], i + 1)
                            v.wait_ge(S["v"], i + 1)
                            tt(kv[:], bank[7][:], k_sb[:], ALU.mult).then_inc(S["kv"], 1)
                            v.wait_ge(S["kv"], i + 1)
                            nc.vector.tensor_tensor_scan(state[:], C("decay"), kv[:], 0.0, ALU.mult,
                                                         ALU.add).then_inc(S["state"], 1)
                            yield
                            v.wait_ge(S["state"], i + 1)
                            v.wait_ge(S["sr"], i + 1)
                            tt(y[:], state[:], sr[:], ALU.mult).then_inc(S["y"], 1)
                            yield
                            v.wait_ge(S["wo"], i + 1)
                            tt(h[i + 1][:], src, bank[7][:], ALU.add).then_inc(S["h"], 1)

                        for i in range(DEPTH):
                            src = xf[i]
                            nc.vector.memset(hs[64:128, 0:1], 0.0).then_inc(S["pad"], 1)
                            v.wait_ge(S["pad"], 2 * i + 1)
                            nc.vector.tensor_copy(hs[64:128, 1:T], src[64:128, 0:T - 1]).then_inc(S["hs_b"], 1)

                            def turn(n):
                                k = 8 * i + n
                                v.wait_ge(S["rn"], k + 1)
                                v.wait_ge(S["t3"], k + 1)
                                if n == 0 and i:
                                    v.wait_ge(S["score"], 2 * NU * i)
                                stt(qk[:, n * T:(n + 1) * T], rn[n % 2][:], 1e12, t1[n % 2][:], ALU.min,
                                    ALU.mult).then_inc(S["qk"], 1)

                            mix = time_mix(i)
                            for n in range(8):
                                k = 8 * i + n
                                table = 4 * i + 2 * (n // 4)
                                v.wait_ge(S["pj"], k + 1)
                                v.wait_ge(S["sqq"], k + 1)
                                if k >= 2:
                                    v.wait_ge(S["qk"], k - 1)
                                tt(t1[n % 2][:], bank[n % 2][:], rot[:, table], ALU.mult).then_inc(S["t1"], 1)
                                v.wait_ge(S["px"], k + 1)
                                if k >= 2:
                                    v.wait_ge(S["t3"], k - 1)
                                tt(t2[n % 2][:], bank[2 + n % 2][:], rot[:, table + 1], ALU.mult).then_inc(S["t2"], 1)
                                if n:
                                    turn(n - 1)
                                next(mix, None)
                            turn(7)
                            def centre(u):
                                q, e = u // 2, u % 2
                                k = NU * i + u
                                n0 = 0 if q else WIN
                                if k >= 2:
                                    v.wait_ge(S["turned"], 2 * (k - 1))
                                for f in range(2):
                                    v.wait_ge(S["score"], 2 * k + f + 1)
                                    stt(pe_[e][:, 2 * f:2 * f + 2, WIN + n0:256],
                                        bank[2 * e + f][:].rearrange("p (a j) -> p a j", a=2)[:, :, n0:KW], 8.0,
                                        C("band")[:, None, n0:KW].to_broadcast([128, 2, KW - n0]),
                                        ALU.mult, ALU.add).then_inc(S["scored"], 1)
                                v.wait_ge(S["scored"], 2 * k + 2)
                                nc.vector.tensor_reduce(nmax[e][:], pe_[e][:, :, WIN + n0:256], AX.X, ALU.max).then_inc(S["max"], 1)
                                v.wait_ge(S["max"], k + 1)
                                tt(pe_[e][:, :, WIN + n0:256], pe_[e][:, :, WIN + n0:256],
                                   nmax[e][:, :, None].to_broadcast([128, 4, KW - n0]), ALU.subtract).then_inc(S["centred"], 1)

                            def outputs(u):
                                q, e = u // 2, u % 2
                                k = NU * i + u
                                v.wait_ge(S["pv"], 2 * k + 2)
                                o = bank[6 + e][:, 0:260].rearrange("p (h d) -> p h d", d=65)
                                nc.vector.reciprocal(oinv[:, 4 * e:4 * e + 4, None], o[:, :, 64:65]).then_inc(S["oinv"], 1)
                                v.wait_ge(S["oinv"], k + 1)
                                if k >= 2:
                                    v.wait_ge(S["oturn"], NT * i + q)
                                tt(ot[:, e:H1:2], o[:, :, 0:64],
                                   oinv[:, 4 * e:4 * e + 4, None].to_broadcast([128, 4, 64]), ALU.mult).then_inc(S["ot"], 1)

                            centre(0)
                            for u in range(NU):
                                if u + 1 < NU:
                                    centre(u + 1)
                                outputs(u)
                            v.wait_ge(S["attn"], i + 1)
                            tt(x1[:], src[:], bank[0][:], ALU.add).then_inc(S["x1"], 1)
                            v.wait_ge(S["x1"], i + 1)
                            nc.vector.memset(hs[64:128, 0:1], 0.0).then_inc(S["pad"], 1)
                            v.wait_ge(S["pad"], 2 * i + 2)
                            nc.vector.tensor_copy(hs[64:128, 1:T], x1[64:128, 0:T - 1]).then_inc(S["hs2_b"], 1)
                            v.wait_ge(S["hs2_a"], i + 1)
                            v.wait_ge(S["hs2_b"], i + 1)
                            lf[i].dve(v)
                            for n, (o, w) in enumerate(HCH):
                                v.wait_ge(S["gelu"], 3 * i + n + 1)
                                v.wait_ge(S["ap"], 3 * i + n + 1)
                                stt(gg[n][0:w], bank[2 + 2 * n][0:w], W(f"l1_b1a{n}_{i}"), gg[n][0:w], ALU.add,
                                    ALU.mult).then_inc(S["gg"], 1)
                            v.wait_ge(S["ffn_out"], i + 1)
                            stt(xf[i + 1][:], bank[0][:], W(f"l1_b2_{i}"), x1[:], ALU.add, ALU.add).then_inc(S["x2"], 1)
                            v.wait_ge(S["x2"], i + 1)
                        v.wait_ge(S["gate"], 1)
                        v.wait_ge(S["h"], DEPTH)
                        tt(m[:], rs[:], h[2][:], ALU.mult).then_inc(S["m"], 1)
                        v.wait_ge(S["m"], 1)
                        tt(x[:], x[:], m[:], ALU.add).then_inc(S["x_new"], 1)

                    @block.gpsimd
                    def _(g):
                        for k in range(8 * DEPTH):
                            g.wait_ge(S["t1"], k + 1)
                            g.wait_ge(S["t2"], k + 1)
                            nc.gpsimd.tensor_tensor(t1[k % 2][:], t1[k % 2][:], t2[k % 2][:], ALU.add).then_inc(S["t3"], 1)
                S.clear()

        def layer2():
            with ExitStack() as c:
                S = Steps(nc, c, "l2")
                t = lambda n, f=T: sb("l2_" + n, [128, f], c)
                xc, sq, rs = t("xc"), t("sq"), t("rs")
                lx = Norm(S, "xn", x[:], xn[:], xc[:], sq[:], rs[:], bank[0][:], bank[1][:])
                xp = sb("l2_xp", [128, 2, T + 3], c)
                cv = sb("l2_cv", [128, 2, T], c)
                u, sg, dt, du = (sb("l2_" + n, [128, 2, T], c) for n in ("u", "sg", "dt", "du"))
                xr, xd = t("xr"), t("xd")
                da, db, hh, hc = ([sb(f"l2_{n}{i}", [128, 2, T], c) for i in range(2)] for n in ("da", "db", "h", "hc"))
                cn = [t(f"cn{i}") for i in range(2)]
                lg = sb("l2_lg", [128, NT, NE], c)
                pw = sb("l2_pw", [128, NT, NE], c)
                g3, g4 = (sb("l2_" + n, [128, NT, NE, NE], c) for n in ("gt", "ge"))
                nm = sb("l2_nm", [128, NT], c)
                gt = [sb("l2_gates", [128, NT, NE], c)][0]
                xg = [cv[:, 0], cv[:, 1]]
                h1, hg = ([t(f"{n}{i}") for i in range(2)] for n in ("h1", "hg"))
                with nc.Block(no_gpsimd_drain=True) as block:
                    @block.tensor
                    def _(pe):
                        lx.pe(pe)
                        pe.wait_ge(S["xn"], 1)
                        for n in range(4):
                            mm(bank[n][:], W("l2_in", lo=128 * n, n=128), xn[:]).then_inc(S["in"], 1)
                        for q in range(NT):
                            mm(bank[4][:, NE * q:NE * q + NE], xn[:, 128 * q:128 * q + 128], W("l2_router"), True, False)
                            r = mm(bank[4][:, NE * q:NE * q + NE], C("ones_row"), W("l2_router_b"), False, True)
                        r.then_inc(S["logits"], 1)
                        pe.wait_ge(S["u"], 2)
                        for n in range(2):
                            r = mm(bank[5][0:96], W("l2_xproj", lo=96 * n, n=96), u[:, n], n == 0, n == 1)
                        r.then_inc(S["xproj"], 1)
                        pe.wait_ge(S["xsq"], 1)
                        mm(bank[6][0:96], C("rms"), xr[0:96]).then_inc(S["xms"], 1)
                        pe.wait_ge(S["xd"], 1)
                        for n in range(2):
                            mm(bank[n][:], W("l2_dt", lo=128 * n, n=128), xd[0:64]).then_inc(S["dtp"], 1)
                        pe.wait_ge(S["gates"], 1)
                        pe.wait_ge(S["sg"], 2)
                        pe.wait_ge(S["dtz"], 2)

                        def gather(n):
                            for k in range(2):
                                pe.wait_ge(S["hc"], n + 1)
                                r = mm(bank[6 + k][:], C("ident"), hc[n % 2][:, k], n == 0, n == NS - 1)
                            r.then_inc(S["y"], 1)

                        def down(n):
                            pe.wait_ge(S["hg"], n + 1)
                            mm(bank[0][:], W(f"l2_w2_{n // FCH}", lo=128 * (n % FCH), n=128), hg[n % 2][:], n == 0,
                               n == NE * FCH - 1).then_inc(S["down"], 1)

                        assert NS == NE * FCH
                        for n in range(NS):
                            e, k = n // FCH, n % FCH
                            if k == 0:
                                if e:
                                    pe.wait_ge(S["xg"], e)
                                for q in range(NT):
                                    r = mm(bank[1][:, 128 * q:128 * q + 128], gt[:, q, e:e + 1].to_broadcast([128, 128]),
                                           C("ident"))
                                r.then_inc(S["gbc"], 1)
                            if n:
                                pe.wait_ge(S["db"], n)
                            mm(bank[2][:], C("ident", 96)[:, R + n:R + n + 1].to_broadcast([96, 128]),
                               xd[0:96]).then_inc(S["Bn"], 1)
                            if n:
                                pe.wait_ge(S["cn"], n)
                            mm(bank[3][:], C("ident", 96)[:, R + NS + n:R + NS + n + 1].to_broadcast([96, 128]),
                               xd[0:96]).then_inc(S["Cn"], 1)
                            if n >= 2:
                                gather(n - 2)
                            if n:
                                pe.wait_ge(S["hg"], n)
                            mm(bank[4][:], W(f"l2_w1_{e}", lo=128 * k, n=128), xn[:]).then_inc(S["w1"], 1)
                            if k == 0:
                                pe.wait_ge(S["xg"], e + 1)
                            mm(bank[5][:], W(f"l2_w3_{e}", lo=128 * k, n=128), xg[e % 2]).then_inc(S["w3"], 1)
                            if n:
                                down(n - 1)
                        gather(NS - 2)
                        gather(NS - 1)
                        down(NS - 1)
                        pe.wait_ge(S["yg"], 2)
                        for n in range(2):
                            r = mm(bank[2][:], W("l2_out", lo=128 * n, n=128), cv[:, n], n == 0, n == 1)
                        r.then_inc(S["s"], 1)

                    @block.scalar
                    def _(a):
                        nc.scalar.preload_act_table_set("natural_log_exp_and_others")
                        lx.act(a)
                        for n in range(2):
                            a.wait_ge(S["in"], n + 1)
                            act(xp[:, n, 1:T + 1], bank[n][:], ACT.Copy).then_inc(S["xp"], 1)
                        for n in range(2):
                            a.wait_ge(S["in"], n + 3)
                            act(sg[:, n], bank[2 + n][:], ACT.Silu).then_inc(S["sg"], 1)
                        for n in range(2):
                            a.wait_ge(S["conv"], n + 1)
                            act(u[:, n], cv[:, n], ACT.Silu).then_inc(S["u"], 1)
                        nc.scalar.preload_act_table_set("natural_log_exp_and_others")
                        a.wait_ge(S["centred"], 1)
                        act(pw[:], lg[:], ACT.Exp).then_inc(S["pw"], 1)
                        a.wait_ge(S["xproj"], 1)
                        act(xr[0:96], bank[5][0:96], ACT.Square).then_inc(S["xsq"], 1)
                        a.wait_ge(S["xms"], 1)
                        act(rs[0:96], bank[6][0:96], ACT.Ln, bias=C("eps6", 96)).then_inc(S["xr_ln"], 1)
                        a.wait_ge(S["xr_ln"], 1)
                        act(rs[0:96], rs[0:96], ACT.Exp, scale=-0.5).then_inc(S["xrs"], 1)
                        for n in range(2):
                            a.wait_ge(S["dtz"], n + 1)
                            act(cv[:, n], dt[:, n], ACT.Abs).then_inc(S["dt_abs"], 1)
                        for n in range(2):
                            a.wait_ge(S["dt_abs"], n + 1)
                            act(cv[:, n], cv[:, n], ACT.Exp, scale=-1.0).then_inc(S["dt_exp"], 1)
                        for n in range(2):
                            a.wait_ge(S["dt_exp"], n + 1)
                            act(cv[:, n], cv[:, n], ACT.Ln, bias=C("one")).then_inc(S["dt_ln"], 1)
                        nc.scalar.preload_act_table_set("exp_and_others")

                        def expert(n):
                            a.wait_ge(S["w1"], n + 1)
                            if n >= 2:
                                a.wait_ge(S["hg"], n - 1)
                            act(h1[n % 2][:], bank[4][:], ACT.Tanh, scale=0.5).then_inc(S["h1"], 1)

                        a.wait_ge(S["dt"], 2)
                        for n in range(NS):
                            if n:
                                expert(n - 1)
                            a.wait_ge(S["Cn"], n + 1)
                            if n >= 2:
                                a.wait_ge(S["hc"], n - 1)
                            act(cn[n % 2][:], bank[3][:], ACT.Copy).then_inc(S["cn"], 1)
                            if n >= 2:
                                a.wait_ge(S["h"], 2 * n - 2)
                            for k in range(2):
                                act(da[n % 2][:, k], dt[:, k], ACT.Exp,
                                    scale=a_neg[:, NS * k + n:NS * k + n + 1]).then_inc(S["da"], 1)
                        expert(NS - 1)
                        a.wait_ge(S["down"], NE * FCH)
                        act(rs[:], bank[0][:], ACT.Silu).then_inc(S["gate"], 1)

                    @block.vector
                    def _(v):
                        nc.vector.memset(xp[:, :, 0:1], 0.0).then_inc(S["pads"], 1)
                        nc.vector.memset(xp[:, :, T + 1:T + 3], 0.0).then_inc(S["pads"], 1)
                        lx.dve(v)
                        v.wait_ge(S["pads"], 2)
                        for n in range(2):
                            v.wait_ge(S["xp"], n + 1)
                            ts(cv[:, n], xp[:, n, 0:T], W("l2_conv", lo=4 * n, n=1), W("l2_conv_b", lo=n, n=1),
                               ALU.mult, ALU.add).then_inc(S["tap"], 1)
                            for k in range(1, 4):
                                v.wait_ge(S["tap"], 3 * n + k)
                                r = stt(cv[:, n], xp[:, n, k:k + T], W("l2_conv", lo=4 * n + k, n=1), cv[:, n],
                                        ALU.mult, ALU.add)
                                r.then_inc(S["tap"] if k < 3 else S["conv"], 1)
                        v.wait_ge(S["logits"], 1)
                        l4 = bank[4][:, 0:NT * NE].rearrange("p (q e) -> p q e", e=NE)
                        nc.vector.tensor_reduce(nm[:], l4, AX.X, ALU.max).then_inc(S["lmax"], 1)
                        v.wait_ge(S["lmax"], 1)
                        tt(lg[:], l4, nm[:, :, None].to_broadcast([128, NT, NE]), ALU.subtract).then_inc(S["centred"], 1)
                        v.wait_ge(S["pw"], 1)
                        pf = pw[:, :, None, :].to_broadcast([128, NT, NE, NE])
                        pe_ = pw[:, :, :, None].to_broadcast([128, NT, NE, NE])
                        tt(g3[:], pf, pe_, ALU.is_gt).then_inc(S["gt"], 1)
                        tt(g4[:], pf, pe_, ALU.is_ge).then_inc(S["ge"], 1)
                        v.wait_ge(S["gt"], 1)
                        flat = "p q e f -> p (q e f)"
                        tt(g3[:].rearrange(flat), g3[:].rearrange(flat), C("untie"), ALU.mult).then_inc(S["gt"], 1)
                        v.wait_ge(S["ge"], 1)
                        tt(g4[:].rearrange(flat), g4[:].rearrange(flat), C("tie"), ALU.mult).then_inc(S["ge"], 1)
                        v.wait_ge(S["gt"], 2)
                        v.wait_ge(S["ge"], 2)
                        tt(g3[:], g3[:], g4[:], ALU.add).then_inc(S["gt"], 1)
                        v.wait_ge(S["gt"], 3)
                        nc.vector.tensor_reduce(lg[:], g3[:], AX.X, ALU.add).then_inc(S["rank"], 1)
                        v.wait_ge(S["rank"], 1)
                        stt(gt[:], lg[:], 2.0, pw[:], ALU.is_lt, ALU.mult).then_inc(S["kept"], 1)
                        v.wait_ge(S["kept"], 1)
                        nc.vector.tensor_reduce(nm[:], gt[:], AX.X, ALU.add).then_inc(S["gsum"], 1)
                        v.wait_ge(S["gsum"], 1)
                        nc.vector.reciprocal(nm[:], nm[:]).then_inc(S["ginv"], 1)
                        v.wait_ge(S["ginv"], 1)
                        stt(gt[:], gt[:], 0.5, nm[:, :, None].to_broadcast([128, NT, NE]), ALU.mult,
                            ALU.mult).then_inc(S["gates"], 1)
                        v.wait_ge(S["xrs"], 1)
                        stt(xd[0:96], bank[5][0:96], W("l2_xln"), rs[0:96], ALU.mult, ALU.mult).then_inc(S["xd"], 1)
                        for n in range(2):
                            v.wait_ge(S["dtp"], n + 1)
                            ts(dt[:, n], bank[n][:], W("l2_dt_b", lo=n, n=1), None, ALU.add).then_inc(S["dtz"], 1)
                        for n in range(2):
                            v.wait_ge(S["dt_ln"], n + 1)
                            stt(dt[:, n], dt[:, n], 0.0, cv[:, n], ALU.max, ALU.add).then_inc(S["dt"], 1)
                        for n in range(2):
                            v.wait_ge(S["dt"], n + 1)
                            tt(du[:, n], dt[:, n], u[:, n], ALU.mult).then_inc(S["du"], 1)
                        v.wait_ge(S["du"], 2)

                        def scan(n):
                            for k in range(2):
                                v.wait_ge(S["da"], 2 * n + k + 1)
                                v.wait_ge(S["db"], n + 1)
                                if n >= 2:
                                    v.wait_ge(S["hc"], n - 1)
                                nc.vector.tensor_tensor_scan(hh[n % 2][:, k], da[n % 2][:, k], db[n % 2][:, k], 0.0,
                                                             ALU.mult, ALU.add).then_inc(S["h"], 1)

                        def expert(n):
                            v.wait_ge(S["h1"], n + 1)
                            stt(h1[n % 2][:], h1[n % 2][:], 1.0, bank[4][:], ALU.add, ALU.mult).then_inc(S["silu"], 1)
                            v.wait_ge(S["silu"], n + 1)
                            v.wait_ge(S["w3"], n + 1)
                            if n >= 2:
                                v.wait_ge(S["down"], n - 1)
                            tt(hg[n % 2][:], h1[n % 2][:], bank[5][:], ALU.mult).then_inc(S["hg"], 1)

                        for n in range(NS):
                            e = n // FCH
                            v.wait_ge(S["Bn"], n + 1)
                            if n >= 2:
                                v.wait_ge(S["h"], 2 * n - 2)
                            tt(db[n % 2][:], du[:], bank[2][:, None, :].to_broadcast([128, 2, T]),
                               ALU.mult).then_inc(S["db"], 1)
                            if n % FCH == 0:
                                v.wait_ge(S["gbc"], e + 1)
                                if e >= 2:
                                    v.wait_ge(S["w3"], FCH * (e - 1))
                                tt(xg[e % 2], xn[:], bank[1][:], ALU.mult).then_inc(S["xg"], 1)
                            if n:
                                expert(n - 1)
                                scan(n - 1)
                        expert(NS - 1)
                        scan(NS - 1)
                        for n in range(2):
                            v.wait_ge(S["y"], NS)
                            stt(du[:, n], u[:, n], W("l2_D", lo=n, n=1), bank[6 + n][:], ALU.mult, ALU.add).then_inc(S["yd"], 1)
                        v.wait_ge(S["w3"], NE * FCH)
                        for n in range(2):
                            v.wait_ge(S["yd"], n + 1)
                            tt(cv[:, n], du[:, n], sg[:, n], ALU.mult).then_inc(S["yg"], 1)
                        v.wait_ge(S["s"], 1)
                        v.wait_ge(S["gate"], 1)
                        tt(sq[:], rs[:], bank[2][:], ALU.mult).then_inc(S["m"], 1)
                        v.wait_ge(S["m"], 1)
                        tt(x[:], x[:], sq[:], ALU.add).then_inc(S["x_new"], 1)

                    @block.gpsimd
                    def _(g):
                        for n in range(NS):
                            g.wait_ge(S["h"], 2 * n + 2)
                            g.wait_ge(S["cn"], n + 1)
                            if n >= 2:
                                g.wait_ge(S["y"], n - 1)
                            nc.gpsimd.tensor_tensor(hc[n % 2][:], hh[n % 2][:],
                                                    cn[n % 2][:, None, :].to_broadcast([128, 2, T]),
                                                    ALU.mult).then_inc(S["hc"], 1)
                S.clear()

        def layer3():
            with ExitStack() as c:
                S = Steps(nc, c, "l3")
                t = lambda n, f=T: sb("l3_" + n, [128, f], c)
                xc, sq, rs = t("xc"), t("sq"), t("rs")
                lx = Norm(S, "xn", x[:], xn[:], xc[:], sq[:], rs[:], bank[0][:], bank[1][:])
                cp = Coupling(S, "L3", 1, c, (bank[6], bank[7]), xn[:])
                G = 2 * H3
                qk = sb("l3_qk", [128, NT, G * D3], c)
                qk2 = sb("l3_qk2", [128, NT, G * D3], c)
                mu, var, mx = (sb("l3_" + n, [128, NT * G], c) for n in ("mu", "var", "mx"))
                VW = 11
                vt = sb("l3_v", [128, NT, H3 + VW, D3 + 1], c)
                km = sb("l3_km", [128, 4, T], c)
                qm = sb("l3_qm", [128, 4, T], c)
                qft = t("qft")
                kvm = sb("l3_kvm", [128, H3, D3 + 1], c)
                ol = sb("l3_ol", [128, NT, H3, D3 + 1], c)
                wk_, pp, pt = ([t(f"{n}{i}") for i in range(2)] for n in ("wk", "pp", "pt"))
                RS, RM = 6, 4
                sc = [t(f"sc{i}") for i in range(RS)]
                ex = [t(f"ex{i}") for i in range(RM)]
                m8 = [sb(f"l3_m8{i}", [128, 4, 8], c) for i in range(RM)]
                nmx = [sb(f"l3_nmx{i}", [128, 1], c) for i in range(RM)]
                og = [sb(f"l3_og{i}", [128, H3, D3 + 1], c) for i in range(2)]
                zs = sb("l3_zs", [128, NT, H3], c)
                den = sb("l3_den", [128, 2, H3], c)
                zi = sb("l3_zi", [128, NT, H3], c)
                oo = qk[:, :, 0:D]
                o1 = qk2[:, 0, 0:D].rearrange("p (h d) -> p h d", d=D3)
                of = qft
                SC = D3 ** -0.5
                g8 = "p q (g d) -> p (q g) d"
                tiles = [(q, h) for q in range(NT) for h in range(H3)]
                N = len(tiles)
                tops = lambda n, k: 8 * (n // 2) + 2 * k + n % 2 + 1
                rests = lambda n, k: 6 * (n // 2) + 2 * k + n % 2 + 1
                with nc.Block(no_gpsimd_drain=True) as block:
                    @block.tensor
                    def _(pe):
                        lx.pe(pe)
                        pe.wait_ge(S["xn"], 1)
                        for q in range(NT):
                            mm(bank[q][:, 0:384], xn[:, 128 * q:128 * q + 128], W("l3_qkv"), True, False)
                            mm(bank[q][:, 0:384], C("ones_row"), W("l3_bqkv"), False, True).then_inc(S["qkv"], 1)
                        pe.wait_ge(S["qkn"], 1)
                        for part in range(2):
                            for q in range(NT):
                                r = nc.tensor.transpose(bank[4 + part][:, 128 * q:128 * q + 128],
                                                        qk[:, q, 128 * part:128 * part + 128], C("ident"))
                            r.then_inc(S["qk_turn"], 1)
                        pe.wait_ge(S["soft"], 1)
                        pe.wait_ge(S["vt"], NT)
                        pe.wait_ge(S["ones"], 1)
                        for q in range(NT):
                            r = mm(bank[0][:, 0:H3 * 9], qk2[:, q, 128:256], vt[:, q, 0:H3].rearrange("p h d -> p (h d)"),
                                   q == 0, q == NT - 1)
                        r.then_inc(S["kv"], 1)
                        for q in range(NT):
                            r = nc.tensor.transpose(bank[1][:, 128 * q:128 * q + 128], qk2[:, q, 0:128], C("ident"))
                        r.then_inc(S["qf_turn"], 1)
                        pe.wait_ge(S["kvm"], 1)
                        pe.wait_ge(S["qft"], 1)
                        for q in range(NT):
                            r = mm(bank[2 + q // 2][:, 256 * (q % 2):256 * (q % 2) + H3 * 9],
                                   qft[:, 128 * q:128 * q + 128], kvm[:].rearrange("p h d -> p (h d)"))
                        r.then_inc(S["lin"], 1)

                        def score(n):
                            q, h = tiles[n]
                            if n >= 3:
                                pe.wait_ge(S["sc"], n - 2)
                            mm(bank[n % 3][:], qm[:, h % 4, 128 * q:128 * q + 128],
                               km[:, h // 4, :]).then_inc(S["score"], 1)

                        def values(n):
                            q, h = tiles[n]
                            pe.wait_ge(S["pt"], n + 1)
                            if h == 0 and q:
                                pe.wait_ge(S["og"], q)
                            for k in range(NT):
                                r = mm(bank[5][:, 9 * h:9 * (h + VW)], pt[n % 2][:, 128 * k:128 * k + 128],
                                       vt[:, k, h:h + VW].rearrange("p h d -> p (h d)"),
                                       k == 0, k == NT - 1)
                            r.then_inc(S["pv"], 1)

                        pe.wait_ge(S["ol"], 1)
                        pe.wait_ge(S["qm"], 4)
                        pe.wait_ge(S["km"], 4)
                        pe.wait_ge(S["zeros"], 1)
                        LEAD = 5
                        for n in range(LEAD):
                            score(n)
                        ff = cp.pe(pe)
                        for n in range(N):
                            if n + LEAD < N:
                                score(n + LEAD)
                            pe.wait_ge(S["pp"], n + 1)
                            if n >= 2:
                                pe.wait_ge(S["pt"], n - 1)
                            for k in range(NT):
                                r = nc.tensor.transpose(bank[3 + n % 2][:, 128 * k:128 * k + 128],
                                                        pp[n % 2][:, 128 * k:128 * k + 128], C("ident"))
                            r.then_inc(S["turned"], 1)
                            if n:
                                values(n - 1)
                            if n % 2:
                                next(ff, None)
                        values(N - 1)
                        for _ in ff:
                            pass
                        pe.wait_ge(S["oo"], NT)
                        for q in range(NT):
                            r = nc.tensor.transpose(bank[0][:, 128 * q:128 * q + 128], oo[:, q], C("ident"))
                        r.then_inc(S["o_turn"], 1)
                        pe.wait_ge(S["of"], 1)
                        mm(bank[1][:], W("l3_proj"), of[:]).then_inc(S["s"], 1)

                    @block.scalar
                    def _(a):
                        def turn_out(a, n):
                            a.wait_ge(S["turned"], n + 1)
                            if n >= 2:
                                a.wait_ge(S["pv"], n - 1)
                            act(pt[n % 2][:], bank[3 + n % 2][:], ACT.Copy).then_inc(S["pt"], 1)

                        nc.scalar.preload_act_table_set("natural_log_exp_and_others")
                        lx.act(a)
                        for q in range(NT):
                            a.wait_ge(S["qkv"], q + 1)
                            act(qk[:, q], bank[q][:, 0:256], ACT.Copy).then_inc(S["qk"], 1)
                            act(vt[:, q, 0:H3, 0:D3], bank[q][:, 256:384].rearrange("p (h d) -> p h d", d=D3),
                                ACT.Copy).then_inc(S["vt"], 1)
                        a.wait_ge(S["qkc"], 1)
                        act(qk2[:], qk[:], ACT.Square).then_inc(S["qk_sq"], 1)
                        a.wait_ge(S["qkv_ss"], 1)
                        act(var[:], mu[:], ACT.Ln, scale=1.0 / D3, bias=C("eps5")).then_inc(S["qk_ln"], 1)
                        a.wait_ge(S["qk_ln"], 1)
                        act(var[:], var[:], ACT.Exp, scale=-0.5).then_inc(S["qk_rs"], 1)
                        a.wait_ge(S["qk_turn"], 1)
                        for r in range(4):
                            act(qm[:, r], bank[4][:], ACT.Copy, scale=C("quarter")[:, r:r + 1]).then_inc(S["qm"], 1)
                        a.wait_ge(S["qk_turn"], 2)
                        for g in range(4):
                            act(km[:, g], bank[5][:], ACT.Copy, scale=C("group32")[:, g:g + 1]).then_inc(S["km"], 1)
                        a.wait_ge(S["soft_c"], 1)
                        act(qk2[:], qk2[:], ACT.Exp).then_inc(S["soft_e"], 1)
                        a.wait_ge(S["qf_turn"], 1)
                        act(qft[:], bank[1][:], ACT.Copy).then_inc(S["qft"], 1)

                        def fetch(n):
                            a.wait_ge(S["score"], n + 1)
                            if n >= RS:
                                a.wait_ge(S["kept"], n - RS + 1)
                            act(sc[n % RS][:], bank[n % 3][:], ACT.Copy).then_inc(S["sc"], 1)

                        def exponent(n):
                            q, h = tiles[n]
                            a.wait_ge(S["nmx"], n + 1)
                            if n >= RM:
                                a.wait_ge(S["pp"], n - RM + 1)
                            act(ex[n % RM][:], sc[n % RS][:], ACT.Exp, scale=SC, bias=nmx[n % RM][:],
                                accum_out=zs[:, q, h:h + 1]).then_inc(S["ex"], 1)

                        def take_outputs(q):
                            a.wait_ge(S["pv"], H3 * (q + 1))
                            if q >= 2:
                                a.wait_ge(S["os"], q - 1)
                            act(og[q % 2][:], bank[5][:, 0:H3 * 9].rearrange("p (h d) -> p h d", d=9),
                                ACT.Copy).then_inc(S["og"], 1)

                        ff = cp.act(a)
                        for n in range(4):
                            fetch(n)
                        for p in range(N // 2):
                            exponent(2 * p)
                            exponent(2 * p + 1)
                            for e in range(2):
                                if p:
                                    turn_out(a, 2 * p - 2 + e)
                                    if e == 0 and p > 1 and (2 * p - 2) % H3 == 0:
                                        take_outputs((2 * p - 2) // H3 - 1)
                                if 2 * p + 4 + e < N:
                                    fetch(2 * p + 4 + e)
                            if p:
                                next(ff, None)
                        turn_out(a, N - 2)
                        turn_out(a, N - 1)
                        take_outputs(NT - 1)
                        for _ in ff:
                            pass
                        cp.act_silu(a)
                        a.wait_ge(S["o_turn"], 1)
                        act(of[:], bank[0][:], ACT.Copy).then_inc(S["of"], 1)

                    @block.vector
                    def _(v):
                        def outputs(v, q):
                            v.wait_ge(S["og"], q + 1)
                            v.wait_ge(S["ex"], H3 * (q + 1))
                            o9 = og[q % 2][:]
                            stt(den[:, 0, :, None], zs[:, q, :, None], 1e-8, o9[:, :, D3:9], ALU.mult, ALU.add).then_inc(S["den"], 1)
                            v.wait_ge(S["den"], 3 * q + 1)
                            nc.vector.reciprocal(den[:, 1], den[:, 0]).then_inc(S["den"], 1)
                            v.wait_ge(S["den"], 3 * q + 2)
                            tt(den[:, 0], den[:, 1], alpha[:, 0], ALU.mult).then_inc(S["den"], 1)
                            v.wait_ge(S["den"], 3 * q + 3)
                            tt(o1[:], o9[:, :, 0:D3], den[:, 0, :, None].to_broadcast([128, H3, D3]), ALU.mult).then_inc(S["os"], 1)
                            v.wait_ge(S["os"], q + 1)
                            tt(oo[:, q].rearrange("p (h d) -> p h d", d=D3), o1[:], ol[:, q, :, 0:D3], ALU.add).then_inc(S["oo"], 1)

                        nc.vector.memset(vt[:, :, 0:H3, D3:D3 + 1], 1.0).then_inc(S["ones"], 1)
                        lx.dve(v)
                        v.wait_ge(S["xn"], 1)
                        cp.dve_context(v)
                        v.wait_ge(S["qk"], NT)
                        q3 = qk[:].rearrange(g8, d=D3)
                        s3 = qk2[:].rearrange(g8, d=D3)
                        wide = lambda z: z[:, :, None].to_broadcast([128, NT * G, D3])
                        nc.vector.tensor_reduce(mx[:], q3, AX.X, ALU.add).then_inc(S["qk_sum"], 1)
                        v.wait_ge(S["qk_sum"], 1)
                        ts(mx[:], mx[:], 1.0 / D3, None, ALU.mult).then_inc(S["qk_mu"], 1)
                        v.wait_ge(S["qk_mu"], 1)
                        tt(q3, q3, wide(mx), ALU.subtract).then_inc(S["qkc"], 1)
                        v.wait_ge(S["qk_sq"], 1)
                        nc.vector.tensor_reduce(mu[:], s3, AX.X, ALU.add).then_inc(S["qkv_ss"], 1)
                        v.wait_ge(S["qk_rs"], 1)
                        tt(q3, q3, wide(var), ALU.mult).then_inc(S["qk_n"], 1)
                        v.wait_ge(S["qk_n"], 1)
                        tt(qk[:], qk[:], W("l3_gamma")[:, None, :].to_broadcast([128, NT, 256]), ALU.mult).then_inc(S["qk_n"], 1)
                        v.wait_ge(S["qk_n"], 2)
                        tt(qk[:], qk[:], W("l3_beta")[:, None, :].to_broadcast([128, NT, 256]), ALU.add).then_inc(S["qkn"], 1)
                        v.wait_ge(S["qkn"], 1)
                        nc.vector.tensor_reduce(mx[:], q3, AX.X, ALU.max).then_inc(S["soft_m"], 1)
                        v.wait_ge(S["soft_m"], 1)
                        tt(s3, q3, wide(mx), ALU.subtract).then_inc(S["soft_c"], 1)
                        v.wait_ge(S["soft_e"], 1)
                        nc.vector.tensor_reduce(mu[:], s3, AX.X, ALU.add).then_inc(S["soft_s"], 1)
                        v.wait_ge(S["soft_s"], 1)
                        nc.vector.reciprocal(mu[:], mu[:]).then_inc(S["soft_r"], 1)
                        v.wait_ge(S["soft_r"], 1)
                        tt(s3, s3, wide(mu), ALU.mult).then_inc(S["soft"], 1)
                        v.wait_ge(S["kv"], 1)
                        tt(kvm[:], bank[0][:, 0:H3 * 9].rearrange("p (h d) -> p h d", d=9),
                           C("headcol")[:, :, None].to_broadcast([128, H3, 9]), ALU.mult).then_inc(S["kvm"], 1)
                        v.wait_ge(S["lin"], 1)
                        for f in range(2):
                            r = nc.vector.tensor_copy(ol[:, 2 * f:2 * f + 2],
                                                      bank[2 + f][:].rearrange("p (q c) -> p q c", q=2)[:, :, 0:H3 * 9]
                                                      .rearrange("p q (h d) -> p q h d", d=9))
                        r.then_inc(S["ol"], 1)
                        v.wait_ge(S["ol"], 1)
                        ts(zi[:], ol[:, :, :, D3], 1e-6, None, ALU.add).then_inc(S["zi"], 1)
                        v.wait_ge(S["zi"], 1)
                        nc.vector.reciprocal(zi[:], zi[:]).then_inc(S["zi"], 1)
                        v.wait_ge(S["zi"], 2)
                        tt(zi[:], zi[:], alpha[:, 1][:, None, :].to_broadcast([128, NT, H3]), ALU.mult).then_inc(S["zi"], 1)
                        v.wait_ge(S["zi"], 3)
                        tt(ol[:, :, :, 0:D3].rearrange("p q h d -> p (q h) d"), ol[:, :, :, 0:D3].rearrange("p q h d -> p (q h) d"),
                           zi[:].rearrange("p q h -> p (q h)")[:, :, None].to_broadcast([128, NT * H3, D3]),
                           ALU.mult).then_inc(S["ol2"], 1)
                        ff = cp.dve(v)
                        for p in range(N // 2):
                            pair = (2 * p, 2 * p + 1)
                            for n in pair:
                                v.wait_ge(S["sc"], n + 1)
                                if n >= RM:
                                    v.wait_ge(S["nmx"], n - RM + 1)
                                    v.wait_ge(S["kept"], n - RM + 1)
                                nc.vector.max(m8[n % RM][:, 0], sc[n % RS][:]).then_inc(S["top"], 1)
                            for k in range(TOPK // 8):
                                for n in pair:
                                    w = wk_[n % 2]
                                    v.wait_ge(S["top"], tops(n, k))
                                    nc.vector.match_replace(w[:], m8[n % RM][:, k], sc[n % RS][:] if k == 0 else w[:],
                                                            -3e38).then_inc(S["rest"], 1)
                                for n in pair:
                                    v.wait_ge(S["rest"], rests(n, k))
                                    nc.vector.max(m8[n % RM][:, k + 1], wk_[n % 2][:]).then_inc(S["top"], 1)
                            if p > 2 and (2 * p - 4) % H3 == 0:
                                outputs(v, (2 * p - 4) // H3 - 1)
                            if p:
                                next(ff, None)
                        outputs(v, NT - 1)
                        for _ in ff:
                            pass
                        v.wait_ge(S["s"], 1)
                        v.wait_ge(S["gate"], 1)
                        stt(sq[:], bank[1][:], W("l3_bproj"), cp.th[:], ALU.add, ALU.mult).then_inc(S["m"], 1)
                        v.wait_ge(S["m"], 1)
                        tt(x[:], x[:], sq[:], ALU.add).then_inc(S["x_new"], 1)

                    @block.gpsimd
                    def _(g):
                        def smallest_exponent(n):
                            g.wait_ge(S["top"], tops(n, 0))
                            if n >= RM:
                                g.wait_ge(S["ex"], n - RM + 1)
                            nc.gpsimd.tensor_scalar(nmx[n % RM][:], m8[n % RM][:, 0, 0:1], -SC, None, ALU.mult).then_inc(S["nmx"], 1)

                        nc.gpsimd.memset(vt[:, :, H3:, :], 0.0).then_inc(S["zeros"], 1)
                        smallest_exponent(0)
                        smallest_exponent(1)
                        for n in range(N):
                            g.wait_ge(S["top"], tops(n, 3))
                            if n >= 2:
                                g.wait_ge(S["turned"], n - 1)
                            nc.gpsimd.tensor_scalar(pp[n % 2][:], sc[n % RS][:], m8[n % RM][:, 3, 0:1], None,
                                                    ALU.is_ge).then_inc(S["kept"], 1)
                            if n % 2 == 0 and n + 2 < N:
                                smallest_exponent(n + 2)
                                smallest_exponent(n + 3)
                            g.wait_ge(S["kept"], n + 1)
                            g.wait_ge(S["ex"], n + 1)
                            nc.gpsimd.tensor_tensor(pp[n % 2][:], pp[n % 2][:], ex[n % RM][:], ALU.mult).then_inc(S["pp"], 1)
                S.clear()

        with nc.Fori(0, B) as b:
            with ExitStack() as c:
                S = Steps(nc, c, "l0")
                t = lambda n: sb("l0_" + n, [128, T], c)
                xc, sq, rs = t("xc"), t("sq"), t("rs")
                ksq, qsq, rk, rq = t("ksq"), t("qsq"), t("rk"), t("rq")
                beta, kn, u, wk, qn, sg = t("beta"), t("kn"), t("u"), t("wk"), t("qn"), t("sg")
                pr = [t(f"pr{i}") for i in range(2)]
                dec = [t(f"dec{i}") for i in range(2)]
                src = [t(f"src{i}") for i in range(2)]
                st = [t(f"st{i}") for i in range(2)]
                sq8 = [t(f"sq8{i}") for i in range(2)]
                og, osb = t("og"), t("osb")
                m = t("m")
                ln = Norm(S, "xn", x[:], xn[:], xc[:], sq[:], rs[:], bank[0][:], bank[1][:])
                lo = Norm(S, "on", osb[:], og[:], xc[:], sq[:], rs[:], bank[2][:], bank[3][:],
                          W("l0_ln_g"), W("l0_ln_b"))
                cp = Coupling(S, "L0", 0, c, (bank[0], bank[1]), xn[:])
                with nc.Block(no_gpsimd_drain=True) as block:
                    @block.sync
                    def _(sp):
                        sp.dma_start(x[:], x_in[b]).then_inc(S["x"], 16)

                    @block.tensor
                    def _(pe):
                        pe.wait_ge(S["x"], 16)
                        ln.pe(pe)
                        pe.wait_ge(S["xn"], 1)
                        mm(bank[2][:], W("l0_Wk"), xn[:]).then_inc(S["k"], 1)
                        mm(bank[3][:], W("l0_Wq"), xn[:]).then_inc(S["q"], 1)
                        mm(bank[4][:], W("l0_Wbeta"), xn[:]).then_inc(S["b"], 1)
                        mm(bank[7][:], W("l0_Wg"), xn[:]).then_inc(S["g"], 1)
                        pe.wait_ge(S["ksq"], 1)
                        mm(bank[5][:], C("head8"), ksq[:]).then_inc(S["kss"], 1)
                        pe.wait_ge(S["qsq"], 1)
                        mm(bank[6][:], C("head8"), qsq[:]).then_inc(S["qss"], 1)
                        pe.wait_ge(S["qn"], 1)
                        pe.wait_ge(S["rq"], 1)
                        pe.wait_ge(S["beta"], 1)

                        def gather(i):
                            pe.wait_ge(S["sq8"], i + 1)
                            mm(bank[6][:], C(f"reduce{i}"), sq8[i % 2][:], i == 0, i == 7).then_inc(S["gathered"], 1)

                        ff = cp.pe(pe)
                        for i in range(9):
                            if i < 8:
                                if i >= 2:
                                    pe.wait_ge(S["pr"], i - 1)
                                    pe.wait_ge(S["src"], i - 1)
                                mm(bank[2 + i % 2][:], W(f"l0_Wkr{i}"), xn[:]).then_inc(S["kr"], 1)
                                mm(bank[4 + i % 2][:], W(f"l0_Wvr{i}"), xn[:]).then_inc(S["vr"], 1)
                            if i:
                                next(ff, None)
                            if i >= 2:
                                gather(i - 2)
                            if i:
                                next(ff, None)
                        gather(7)
                        for _ in ff:
                            pass
                        pe.wait_ge(S["osb"], 1)
                        lo.pe(pe)
                        pe.wait_ge(S["og2"], 1)
                        mm(bank[7][:], W("l0_Wout"), og[:]).then_inc(S["s"], 1)

                    @block.scalar
                    def _(a):
                        nc.scalar.preload_act_table_set("natural_log_exp_and_others")
                        ln.act(a)
                        a.wait_ge(S["k"], 1)
                        act(ksq[:], bank[2][:], ACT.Square).then_inc(S["ksq"], 1)
                        a.wait_ge(S["q"], 1)
                        act(qsq[:], bank[3][:], ACT.Square).then_inc(S["qsq"], 1)
                        a.wait_ge(S["kss"], 1)
                        act(rk[:], bank[5][:], ACT.Ln, scale=NORM_SCALE, bias=C("floor")).then_inc(S["rk_ln"], 1)
                        a.wait_ge(S["qss"], 1)
                        act(rq[:], bank[6][:], ACT.Ln, scale=NORM_SCALE, bias=C("floor")).then_inc(S["rq_ln"], 1)
                        a.wait_ge(S["rk_ln"], 1)
                        act(rk[:], rk[:], ACT.Exp, scale=-0.5, bias=C("norm_back")).then_inc(S["rk"], 1)
                        a.wait_ge(S["rq_ln"], 1)
                        act(rq[:], rq[:], ACT.Exp, scale=-0.5, bias=C("norm_back")).then_inc(S["rq"], 1)
                        a.wait_ge(S["b"], 1)
                        act(beta[:], bank[4][:], ACT.Sigmoid).then_inc(S["beta"], 1)
                        a.wait_ge(S["g"], 1)
                        act(sg[:], bank[7][:], ACT.Silu).then_inc(S["sg"], 1)
                        nc.scalar.preload_act_table_set("gelu_and_others")
                        ff = cp.act(a)
                        for i in range(8):
                            next(ff, None)
                            a.wait_ge(S["pr"], i + 1)
                            if i >= 2:
                                a.wait_ge(S["st"], i - 1)
                            act(dec[i % 2][:], pr[i % 2][:], ACT.Identity, scale=-1.0, bias=C("one")).then_inc(S["dec"], 1)
                            next(ff, None)
                        a.wait_ge(S["gathered"], 8)
                        act(osb[:], bank[6][:], ACT.Copy).then_inc(S["osb"], 1)
                        for _ in ff:
                            pass
                        cp.act_silu(a)
                        nc.scalar.preload_act_table_set("natural_log_exp_and_others")
                        lo.act(a)

                    @block.vector
                    def _(v):
                        v.wait_ge(S["x"], 16)
                        ln.dve(v)
                        v.wait_ge(S["xn"], 1)
                        cp.dve_context(v)
                        v.wait_ge(S["rk"], 1)
                        ts(rk[:], rk[:], 1e12, None, ALU.min).then_inc(S["rk_c"], 1)
                        v.wait_ge(S["rk_c"], 1)
                        tt(kn[:], bank[2][:], rk[:], ALU.mult).then_inc(S["kn"], 1)
                        v.wait_ge(S["rq"], 1)
                        ts(rq[:], rq[:], 1e12, None, ALU.min).then_inc(S["rq_c"], 1)
                        v.wait_ge(S["rq_c"], 1)
                        tt(qn[:], bank[3][:], rq[:], ALU.mult).then_inc(S["qn"], 1)
                        v.wait_ge(S["beta"], 1)
                        v.wait_ge(S["kn"], 1)
                        tt(u[:], kn[:], beta[:], ALU.mult).then_inc(S["u"], 1)
                        v.wait_ge(S["u"], 1)
                        tt(wk[:], u[:], rk[:], ALU.mult).then_inc(S["wk"], 1)
                        v.wait_ge(S["wk"], 1)

                        def scan(i):
                            v.wait_ge(S["dec"], i + 1)
                            v.wait_ge(S["src"], i + 1)
                            if i >= 2:
                                v.wait_ge(S["sq8"], i - 1)
                            nc.vector.tensor_tensor_scan(st[i % 2][:], dec[i % 2][:], src[i % 2][:], 0.0,
                                                         ALU.mult, ALU.add).then_inc(S["st"], 1)

                        ff = cp.dve(v)
                        for i in range(8):
                            v.wait_ge(S["kr"], i + 1)
                            if i >= 2:
                                v.wait_ge(S["dec"], i - 1)
                            tt(pr[i % 2][:], bank[2 + i % 2][:], wk[:], ALU.mult).then_inc(S["pr"], 1)
                            if i:
                                scan(i - 1)
                            v.wait_ge(S["vr"], i + 1)
                            if i >= 2:
                                v.wait_ge(S["st"], i - 1)
                            tt(src[i % 2][:], bank[4 + i % 2][:], u[:], ALU.mult).then_inc(S["src"], 1)
                            next(ff, None)
                            next(ff, None)
                        scan(7)
                        for _ in ff:
                            pass
                        v.wait_ge(S["osb"], 1)
                        lo.dve(v)
                        v.wait_ge(S["on"], 1)
                        v.wait_ge(S["sg"], 1)
                        tt(og[:], og[:], sg[:], ALU.mult).then_inc(S["og2"], 1)
                        v.wait_ge(S["gate"], 1)
                        v.wait_ge(S["s"], 1)
                        tt(m[:], bank[7][:], cp.th[:], ALU.mult).then_inc(S["sg_m"], 1)
                        v.wait_ge(S["sg_m"], 1)
                        tt(x[:], x[:], m[:], ALU.add).then_inc(S["x_new"], 1)

                    @block.gpsimd
                    def _(g):
                        g.wait_ge(S["qn"], 1)
                        for i in range(8):
                            g.wait_ge(S["st"], i + 1)
                            if i >= 2:
                                g.wait_ge(S["gathered"], i - 1)
                            nc.gpsimd.tensor_tensor(sq8[i % 2][:], st[i % 2][:], qn[:], ALU.mult).then_inc(S["sq8"], 1)
                S.clear()

            if upto >= 1:
                layer1()
            if upto >= 2:
                layer2()
            if upto >= 3:
                layer3()

            with ExitStack() as c:
                S = Steps(nc, c, "store")
                with nc.Block(no_gpsimd_drain=True) as block:
                    @block.sync
                    def _(sp):
                        sp.dma_start(out[b], x[:]).then_inc(S["out"], 16)
                        sp.wait_ge(S["out"], 16)
                S.clear()


def columns(parts):
    at, found = 0, {}
    for k, v in parts.items():
        found[k] = (at, v.shape[0], v.shape[1])
        at += v.shape[1]
    return found


def kernel(**inputs):
    import numpy as _np
    import concourse.bacc as _bacc
    from concourse.bass_utils import run_bass_kernel_spmd as _run

    a = {k: _np.asarray(v) for k, v in inputs.items()}
    w, c = weights(a), constants()
    arrays = {"x": _np.ascontiguousarray(a["L0_attn_x"].transpose(0, 2, 1)), "weights": packed(w), "consts": packed(c)}
    nc = _bacc.Bacc("TRN2", target_bir_lowering=False, num_devices=1)
    args = [nc.dram_tensor(n + "_dram", v.shape, F32, kind="ExternalInput").ap() for n, v in arrays.items()]
    out = nc.dram_tensor("out_dram", (B, D, T), F32, kind="ExternalOutput").ap()
    build(nc, *args, out, columns(w), columns(c))
    r = _run(nc, [{n + "_dram": v for n, v in arrays.items()}], core_ids=[0])
    return _np.ascontiguousarray(r.results[0]["out_dram"].transpose(0, 2, 1))
```

```python
from contextlib import ExitStack

import numpy as np
import concourse.bass as bass
from concourse import mybir

F32 = mybir.dt.float32
BF16 = mybir.dt.bfloat16
ALU = mybir.AluOpType
ACT = mybir.ActivationFunctionType
AX = mybir.AxisListType

B, T, D = 8, 512, 128
NT = T // 128
LN_EPS = 1e-5
NORM_SCALE = 2.0 ** 36
NORM_FLOOR = 2.0 ** -64
BIG = 1e30

H1, DH, WIN, HID = 8, 64, 64, 341
HCH = [(0, 128), (128, 128), (256, HID - 256)]
NS, R = 16, 64
NE, FCH = 4, 4
H3, D3 = 16, 8
TOPK = max(1, int(T * 0.05))
DEPTH = 2


def constants():
    p = np.arange(128)
    c = {}
    c["ident"] = np.eye(128)
    c["mean"] = np.full((128, 128), 1.0 / 128)
    c["centre"] = np.eye(128) - 1.0 / 128
    c["head8"] = (p[:, None] // 8 == p[None] // 8).astype(float)
    c["head64"] = (p[:, None] // 64 == p[None] // 64).astype(float)
    for i in range(8):
        c[f"reduce{i}"] = ((p[:, None] // 8 == p[None] // 8) & (p[None] % 8 == i)).astype(float)
    tw = np.zeros((128, 128))
    r = np.arange(32)
    tw[64 + r, r] = 1
    tw[96 + r, 32 + r] = -1
    tw[r, 64 + r] = -1
    tw[32 + r, 96 + r] = 1
    c["twist"] = tw
    j = np.arange(WIN + 128)
    ok = (j[None] - WIN <= p[:, None]) & (p[:, None] <= j[None])
    c["band"] = np.where(ok, 0.0, -BIG)
    g = np.zeros((96, 96))
    for a, b in ((0, R), (R, R + NS), (R + NS, R + 2 * NS)):
        g[a:b, a:b] = 1.0 / (b - a)
    c["rms"] = g
    e = np.arange(NE)
    low = (e[None, :] < e[:, None]).astype(float).reshape(1, -1)
    c["tie"] = np.repeat(np.tile(low, (1, NT)), 128, 0)
    c["untie"] = 1.0 - c["tie"]
    c["headcol"] = (p[:, None] // 8 == np.arange(16)[None]).astype(float)
    c["group32"] = (p[:, None] // 32 == np.arange(4)[None]).astype(float)
    c["three"] = np.zeros((96, 96))
    for i in range(3):
        c["three"][64:96, 32 * i:32 * i + 32] = np.eye(32)
    c["pick"] = (p[:96, None] % 32 == np.arange(32)[None]).astype(float)
    c["quarter"] = ((p[:, None] // 8) % 4 == np.arange(4)[None]).astype(float)
    c["ones_row"] = np.ones((1, 128))
    c["decay"] = np.full((128, T), 0.95)
    for n, v in (("eps5", 1e-5), ("eps6", 1e-6), ("floor", NORM_FLOOR),
                 ("norm_back", 0.5 * np.log(NORM_SCALE)), ("one", 1.0), ("zero", 0.0)):
        c[n] = np.full((128, 1), v)
    half = np.arange(0, DH, 2, dtype=np.float32)
    inv = (1.0 / 10000.0 ** (half / np.float32(DH))).astype(np.float32)
    t = np.arange(T, dtype=np.float32)
    fr = (t[:, None] * inv[None]).astype(np.float32)
    base = (half + np.float32(0.4 * DH)) / np.float32(1.4 * DH)
    power = (t - T // 2) / np.float32(WIN // 2)
    sc = (base[None] ** power[:, None]).astype(np.float32)
    dup = lambda a: np.tile(np.concatenate([a, a], 1), (1, 2)).T
    sign = np.where(p % 64 < 32, -1.0, 1.0)[:, None]
    c["first_once"] = np.zeros((128, 0))
    c["cos_q"], c["sin_q"] = dup(np.cos(fr) * sc), dup(np.sin(fr) * sc) * sign
    c["cos_k"], c["sin_k"] = dup(np.cos(fr) / sc), dup(np.sin(fr) / sc) * sign
    return {k: np.asarray(v, np.float32) for k, v in c.items()}


def weights(a):
    w = {}
    col = lambda v: np.reshape(v, (-1, 1))
    for n in ("Wq", "Wk", "Wg", "Wout"):
        w["l0_" + n] = a["L0_attn_" + n]
    for i in range(8):
        w[f"l0_Wkr{i}"] = np.repeat(a["L0_attn_Wk"].reshape(128, 16, 8)[:, :, i], 8, 1)
        w[f"l0_Wvr{i}"] = np.repeat(a["L0_attn_Wv"].reshape(128, 16, 8)[:, :, i], 8, 1)
    w["l0_Wbeta"] = np.repeat(a["L0_attn_Wbeta"], 8, 1)
    w["l0_ln_g"], w["l0_ln_b"] = col(a["L0_attn_ln_g"]), col(a["L0_attn_ln_b"])
    for lay in ("L0", "L3"):
        for n in ("cn_w1", "cn_w2", "cn_w3", "gc_w1", "gc_w2"):
            w[f"{lay}_{n}"] = a[f"{lay}_ffn_{n}"]
        for n in ("cn_b1", "cn_b2", "cn_b3", "gc_b1", "gc_b2"):
            w[f"{lay}_{n}"] = col(a[f"{lay}_ffn_{n}"])
        for n in ("cn_w4", "gc_w3"):
            w[f"{lay}_{n}"] = np.repeat(a[f"{lay}_ffn_{n}"], 128, 1)
        for n in ("cn_b4", "gc_b3", "adaptive_range"):
            w[f"{lay}_{n}"] = np.repeat(col(a[f"{lay}_ffn_{n}"]), 128, 0)
    for i in range(DEPTH):
        w[f"l1_ln_w{i}"], w[f"l1_ln_b{i}"] = col(a["L1_attn_ln_w"][i]), col(a["L1_attn_ln_b"][i])
        for n in ("Wk", "Wv", "Wr", "Wo"):
            w[f"l1_{n}{i}"] = a["L1_attn_" + n][i].T
        qkv = a["L1_ffn_wqkv"][i]
        w[f"l1_qkv{i}"] = qkv
        w[f"l1_swap{i}"] = qkv[:, :1024].reshape(128, 16, 2, 32)[:, :, ::-1].reshape(128, 1024)
        for n, s in (("q", "q_scale"), ("k", "k_scale")):
            v = a["L1_ffn_" + s][i]
            w[f"l1_{n}s{i}"] = col(np.concatenate([v, v]))
            w[f"l1_{n}x{i}"] = col(np.concatenate([v[32:], v[:32], v[32:], v[:32]]))
        w[f"l1_wo{i}"] = a["L1_ffn_wo"][i].reshape(4, 128, 128).transpose(1, 0, 2).reshape(128, 512)
        w[f"l1_lg{i}"], w[f"l1_lb{i}"] = col(a["L1_ffn_ln_g"][i]), col(a["L1_ffn_ln_b"][i])
        w[f"l1_w1_{i}"] = a["L1_ffn_w1"][i]
        for c, (o, m) in enumerate(HCH):
            w[f"l1_b1a{c}_{i}"] = col(a["L1_ffn_b1"][i][o:o + m])
            w[f"l1_b1g{c}_{i}"] = col(a["L1_ffn_b1"][i][HID + o:HID + o + m])
            w[f"l1_w2_{c}_{i}"] = a["L1_ffn_w2"][i][o:o + m]
        w[f"l1_b2_{i}"] = col(a["L1_ffn_b2"][i])
    w["l2_in"] = a["L2_attn_in_proj_w"].T
    two = lambda v: v.reshape(2, 128, -1).transpose(1, 0, 2).reshape(128, -1)
    w["l2_conv"] = two(a["L2_attn_conv_w"].reshape(256, 4))
    w["l2_conv_b"], w["l2_D"], w["l2_dt_b"] = (two(a["L2_attn_" + n]) for n in ("conv_b", "D", "dt_proj_b"))
    w["l2_xproj"] = two(a["L2_attn_x_proj_w"].T)
    w["l2_xln"] = col(np.concatenate([a["L2_attn_dt_ln_w"], a["L2_attn_b_ln_w"], a["L2_attn_c_ln_w"]]))
    w["l2_dt"] = a["L2_attn_dt_proj_w"].T
    w["l2_alog"] = two(a["L2_attn_A_log"])
    w["l2_out"] = two(a["L2_attn_out_proj_w"].T)
    w["l2_router"] = a["L2_ffn_router_w"]
    w["l2_router_b"] = a["L2_ffn_router_b"].reshape(1, NE)
    for e in range(NE):
        w[f"l2_w1_{e}"], w[f"l2_w3_{e}"] = a["L2_ffn_w1"][e], a["L2_ffn_w3"][e]
        w[f"l2_w2_{e}"] = a["L2_ffn_w2"][e].reshape(4, 128, 128).transpose(1, 0, 2).reshape(128, 512)
    w["l3_qkv"] = a["L3_attn_Wqkv"].T
    w["l3_bqkv"] = np.repeat(a["L3_attn_bqkv"].reshape(1, 384), 128, 0)
    for n in ("gamma", "beta"):
        row = np.concatenate([np.tile(a[f"L3_attn_{p}_{n}"], H3) for p in "qk"])
        w["l3_" + n] = np.repeat(row.reshape(1, -1), 128, 0)
    w["l3_alpha"] = np.repeat(a["L3_attn_alpha"].reshape(1, 16), 128, 0)
    w["l3_proj"] = a["L3_attn_Wproj"].T
    w["l3_bproj"] = col(a["L3_attn_bproj"])
    return w


def packed(parts):
    out = np.zeros((128, sum(v.shape[1] for v in parts.values())), np.float32)
    at = 0
    for v in parts.values():
        out[:v.shape[0], at:at + v.shape[1]] = v
        at += v.shape[1]
    return out


class Steps:

    def __init__(self, nc, ctx, layer):
        self.nc, self.ctx, self.layer, self.all = nc, ctx, layer, {}

    def __getitem__(self, name):
        if name not in self.all:
            self.all[name] = self.ctx.enter_context(self.nc.semaphore(f"{self.layer}_{name}"))
        return self.all[name]

    def clear(self):
        engines = (self.nc.sync, self.nc.scalar, self.nc.vector, self.nc.gpsimd, self.nc.tensor)
        for n, s in enumerate(self.all.values()):
            engines[n % 5].sem_clear(s)
        self.nc.all_engine_barrier()


def build(nc, x_in, w_in, c_in, out, wcols, ccols, upto=99, probe=None):
    ctx = ExitStack()

    def sb(name, shape, c=None):
        return (c or ctx).enter_context(nc.sbuf_tensor(name, shape, F32))

    with ctx:
        w_sb = sb("weights", [128, w_in.shape[1]])
        once = ccols["first_once"][0]
        c_sb = sb("consts", [128, once])
        bank = [ctx.enter_context(nc.psum_tensor(f"bank{i}", [128, 512], F32)) for i in range(8)]
        x = sb("x", [128, T])
        xn = sb("xn", [128, T])
        hold = sb("hold", [128, 6, T])
        wk, u, qn, sg, x0, xn0 = (hold[:, i] for i in range(6))
        rot = sb("rot", [128, DEPTH * 4, T])
        pick = ctx.enter_context(nc.sbuf_tensor("pick", [96, 32], BF16))
        a_neg = sb("a_neg", [128, 2 * NS])
        alpha = sb("alpha", [128, 2, H3])
        couple = sb("couple", [128, 2, 4])

        keep = sb("keep", [128, 4, 4])

        def W(name, r=None, lo=0, n=None):
            o, rows, cols = wcols[name]
            return w_sb[0:(r or rows), o + lo:o + lo + (cols - lo if n is None else n)]

        def C(name, r=None):
            o, rows, cols = ccols[name]
            return c_sb[0:(r or rows), o:o + cols]

        def mm(o, lhsT, rhs, start=True, stop=True):
            return nc.tensor.matmul(o, lhsT, rhs, start=start, stop=stop)

        act = nc.scalar.activation
        tt, ts, stt = nc.vector.tensor_tensor, nc.vector.tensor_scalar, nc.vector.scalar_tensor_tensor

        with ExitStack() as c0:
            S = Steps(nc, c0, "setup")
            tables = sb("rotary", [128, c_in.shape[1] - once], c0)
            head_sum = sb("head_sum", [128, 2, 2 * H3], c0)
            by_channel = sb("by_channel", [128, 4], c0)
            with nc.Block(no_gpsimd_drain=True) as block:
                @block.sync
                def _(sp):
                    sp.dma_start(w_sb[:], w_in).then_inc(S["loaded"], 16)
                    sp.dma_start(c_sb[:], c_in[:, 0:once]).then_inc(S["loaded"], 16)
                    sp.dma_start(tables[:], c_in[:, once:]).then_inc(S["loaded"], 16)

                @block.tensor
                def _(pe):
                    pe.wait_ge(S["loaded"], 48)
                    for n, (name, part) in enumerate((name, part) for name in ("gamma", "beta") for part in range(2)):
                        r = nc.tensor.transpose(bank[0][:, 128 * n:128 * n + 128],
                                                W(f"l3_{name}", lo=128 * part, n=128), C("ident"))
                    r.then_inc(S["by_channel"], 1)

                @block.scalar
                def _(a):
                    a.wait_ge(S["loaded"], 48)
                    act(pick[:], C("pick"), ACT.Copy)
                    act(a_neg[:], W("l2_alog"), ACT.Exp).then_inc(S["exp_a"], 1)
                    act(alpha[:, 0], W("l3_alpha"), ACT.Sigmoid).then_inc(S["alpha"], 1)

                @block.vector
                def _(v):
                    nc.vector.memset(x[:], 0.0)
                    v.wait_ge(S["loaded"], 48)
                    for i in range(DEPTH):
                        for n, (table, scale) in enumerate((("cos_q", "qs"), ("sin_q", "qx"), ("cos_k", "ks"), ("sin_k", "kx"))):
                            o = ccols[table][0] - once
                            ts(rot[:, 4 * i + n], tables[:, o:o + T], W(f"l1_{scale}{i}"), None, ALU.mult)
                    for n, lay in enumerate(("L0", "L3")):
                        ts(couple[:, n, 0:1], W(f"{lay}_cn_b4"), 0.5, None, ALU.mult)
                        ts(couple[:, n, 1:2], W(f"{lay}_adaptive_range"), 2.0, None, ALU.mult)
                        ts(couple[:, n, 2:3], W(f"{lay}_adaptive_range"), 0.3, None, ALU.mult)
                        ts(couple[:, n, 3:4], W(f"{lay}_gc_b3"), 0.5, None, ALU.mult)
                    v.wait_ge(S["exp_a"], 1)
                    ts(a_neg[:], a_neg[:], -1.0, None, ALU.mult)
                    v.wait_ge(S["alpha"], 1)
                    ts(alpha[:, 1], alpha[:, 0], -1.0, 1.0, ALU.mult, ALU.add)
                    heads = [W(name, n=256).rearrange("p (g d) -> p g d", d=D3) for name in ("l3_qkv", "l3_bqkv")]
                    for n, w3 in enumerate(heads):
                        nc.vector.tensor_reduce(head_sum[:, n], w3, AX.X, ALU.add).then_inc(S["head_sum"], 1)
                    v.wait_ge(S["head_sum"], 2)
                    ts(head_sum[:], head_sum[:], 1.0 / D3, None, ALU.mult).then_inc(S["head_mean"], 1)
                    v.wait_ge(S["head_mean"], 1)
                    for n, w3 in enumerate(heads):
                        tt(w3, w3, head_sum[:, n, :, None].to_broadcast([128, 2 * H3, D3]), ALU.subtract)
                    v.wait_ge(S["by_channel"], 1)
                    nc.vector.tensor_copy(by_channel[:], bank[0][:, 0:512:128]).then_inc(S["by_channel_sb"], 1)
                    v.wait_ge(S["by_channel_sb"], 1)
                    for n, kept in enumerate(("quarter", "group32", "quarter", "group32")):
                        ts(keep[:, n], C(kept), by_channel[:, n:n + 1], None, ALU.mult)
            S.clear()

        def keep_clock(b, n):
            for _ in range(n):
                mm(b[:], C("ident"), rot[:, 0])

        class Norm:

            def __init__(self, S, name, src, dst, sq, rs, banks, gain=None, shift=None):
                self.S, self.n, self.src, self.dst, self.sq, self.rs = S, name, src, dst, sq, rs
                self.xc, self.var, self.gain, self.shift = banks[0:2], banks[2:4], gain, shift
                self.halves = [(e, slice(e * T // 2, (e + 1) * T // 2)) for e in range(2)]

            def pe(self, pe):
                for e, half in self.halves:
                    mm(self.xc[e][:, 0:T // 2], C("centre"), self.src[:, half]).then_inc(self.S[self.n + "_xc"], 1)
                for e, half in self.halves:
                    pe.wait_ge(self.S[self.n + "_sq"], e + 1)
                    mm(self.var[e][:, 0:T // 2], C("mean"), self.sq[:, half]).then_inc(self.S[self.n + "_var"], 1)

            def act(self, a):
                for e, half in self.halves:
                    a.wait_ge(self.S[self.n + "_xc"], e + 1)
                    act(self.sq[:, half], self.xc[e][:, 0:T // 2], ACT.Square).then_inc(self.S[self.n + "_sq"], 1)
                for e, half in self.halves:
                    a.wait_ge(self.S[self.n + "_var"], e + 1)
                    act(self.rs[:, half], self.var[e][:, 0:T // 2], ACT.Ln, bias=C("eps5")).then_inc(self.S[self.n + "_ln"], 1)
                    a.wait_ge(self.S[self.n + "_ln"], e + 1)
                    act(self.rs[:, half], self.rs[:, half], ACT.Exp, scale=-0.5).then_inc(self.S[self.n + "_rs"], 1)

            def dve(self, v):
                done = [self.n + "_half", self.n]
                for e, half in self.halves:
                    v.wait_ge(self.S[self.n + "_rs"], e + 1)
                    dst, xc, rs = self.dst[:, half], self.xc[e][:, 0:T // 2], self.rs[:, half]
                    if self.gain is None:
                        tt(dst, xc, rs, ALU.mult).then_inc(self.S[done[e]], 1)
                    else:
                        stt(dst, xc, self.gain, rs, ALU.mult, ALU.mult).then_inc(self.S[self.n + "_g"], 1)
                if self.gain is not None:
                    for e, half in self.halves:
                        v.wait_ge(self.S[self.n + "_g"], e + 1)
                        ts(self.dst[:, half], self.dst[:, half], self.shift, None, ALU.add).then_inc(self.S[done[e]], 1)

        class Coupling:

            def __init__(self, S, lay, n, c, banks, src, relieved=False):
                self.relieved = relieved
                self.S, self.lay, self.n, self.b, self.src = S, lay, n, banks, src
                self.o = [sb(f"{lay}_cyc{k}", [128, T], c) for k in range(3)]
                self.h1, self.h2, self.h3, self.th, self.m = (
                    sb(f"{lay}_ff{k}", [128, T], c) for k in range(5))
                self.sm = sb(f"{lay}_ctx", [128, 8], c)

            def pe(self, pe):
                S, lay, b, sm = self.S, self.lay, self.b, self.sm
                pe.wait_ge(S["ctx"], 1)
                mm(b[0][0:64, 0:1], W(lay + "_gc_w1"), sm[:, 0:1]).then_inc(S["gc1"], 1)
                yield
                pe.wait_ge(S["gc1_gelu"], 1)
                mm(b[0][0:32, 0:1], W(lay + "_gc_w2"), sm[0:64, 1:2]).then_inc(S["gc2"], 1)
                yield
                pe.wait_ge(S["gc2_gelu"], 1)
                mm(b[0][:, 0:1], W(lay + "_gc_w3"), sm[0:32, 2:3]).then_inc(S["gc3"], 1)
                yield
                for k in range(3):
                    src = self.src if k == 0 else self.o[k - 1][:]
                    if k:
                        yield
                    pe.wait_ge(S["gc3_tanh"] if k == 0 else S["cycle"], max(k, 1))
                    mm(b[0][:], W(lay + "_cn_w1"), src).then_inc(S["cn1"], 1)
                    mm(b[1][:], C("twist"), src).then_inc(S["twist"], 1)
                    yield
                    pe.wait_ge(S["cn1_gelu"], k + 1)
                    mm(b[0][0:64], W(lay + "_cn_w2"), self.h1[:]).then_inc(S["cn2"], 1)
                    yield
                    pe.wait_ge(S["cn2_gelu"], k + 1)
                    mm(b[0][0:32], W(lay + "_cn_w3"), self.h2[0:64]).then_inc(S["cn3"], 1)
                    yield
                    pe.wait_ge(S["cn3_gelu"], k + 1)
                    mm(b[0][:], W(lay + "_cn_w4"), self.h3[0:32]).then_inc(S["cn4"], 1)
                    yield

            def act(self, a):
                S, lay, b, sm, n = self.S, self.lay, self.b, self.sm, self.n
                a.wait_ge(S["gc1"], 1)
                act(sm[0:64, 1:2], b[0][0:64, 0:1], ACT.Gelu, bias=W(lay + "_gc_b1")).then_inc(S["gc1_gelu"], 1)
                yield
                a.wait_ge(S["gc2"], 1)
                act(sm[0:32, 2:3], b[0][0:32, 0:1], ACT.Gelu, bias=W(lay + "_gc_b2")).then_inc(S["gc2_gelu"], 1)
                yield
                a.wait_ge(S["gc3"], 1)
                act(sm[:, 3:4], b[0][:, 0:1], ACT.Tanh, bias=couple[:, n, 3:4], scale=0.5).then_inc(S["gc3_tanh"], 1)
                yield
                for k in range(3):
                    if k:
                        yield
                    a.wait_ge(S["cn1"], k + 1)
                    act(self.h1[:], b[0][:], ACT.Gelu, bias=W(lay + "_cn_b1")).then_inc(S["cn1_gelu"], 1)
                    yield
                    a.wait_ge(S["cn2"], k + 1)
                    act(self.h2[0:64], b[0][0:64], ACT.Gelu, bias=W(lay + "_cn_b2")).then_inc(S["cn2_gelu"], 1)
                    yield
                    a.wait_ge(S["cn3"], k + 1)
                    act(self.h3[0:32], b[0][0:32], ACT.Gelu, bias=W(lay + "_cn_b3")).then_inc(S["cn3_gelu"], 1)
                    yield
                    a.wait_ge(S["cn4"], k + 1)
                    if k > 0:
                        a.wait_ge(S["cycle_c"], k)
                    act(self.th[:], b[0][:], ACT.Tanh, bias=couple[:, n, 0:1], scale=0.5).then_inc(S["tanh"], 1)
                    if self.relieved:
                        if k == 0:
                            a.wait_ge(S["base"], 1)
                        a.wait_ge(S["tanh"], k + 1)
                        act(self.m[:], self.th[:], ACT.Identity, scale=couple[:, n, 2:3],
                            bias=sm[:, 7:8]).then_inc(S["cycle_c"], 1)
                    yield

            def act_silu(self, a):
                a.wait_ge(self.S["cycle"], 3)
                act(self.th[:], self.o[2][:], ACT.Silu).then_inc(self.S["gate"], 1)

            def dve_context(self, v):
                S, sm = self.S, self.sm
                nc.vector.reduce_sum(sm[:, 4:5], self.src, AX.X).then_inc(S["ctx_sum"], 1)
                v.wait_ge(S["ctx_sum"], 1)
                ts(sm[:, 0:1], sm[:, 4:5], 1.0 / T, None, ALU.mult).then_inc(S["ctx"], 1)

            def dve(self, v):
                S, b, sm, n = self.S, self.b, self.sm, self.n
                for _ in range(3):
                    yield
                v.wait_ge(S["gc3_tanh"], 1)
                ts(sm[:, 5:6], sm[:, 3:4], 0.35, 0.35 - 0.5, ALU.mult, ALU.add).then_inc(S["base_a"], 1)
                v.wait_ge(S["base_a"], 1)
                stt(sm[:, 6:7], sm[:, 5:6], couple[:, n, 1:2], couple[:, n, 2:3], ALU.mult, ALU.add).then_inc(S["base_b"], 1)
                v.wait_ge(S["base_b"], 1)
                ts(sm[:, 7:8], sm[:, 6:7], 0.1, None, ALU.add).then_inc(S["base"], 1)
                v.wait_ge(S["base"], 1)
                for k in range(3):
                    src = self.src if k == 0 else self.o[k - 1][:]
                    for _ in range(5 if k else 4):
                        yield
                    if not self.relieved:
                        v.wait_ge(S["tanh"], k + 1)
                        ts(self.m[:], self.th[:], couple[:, n, 2:3], sm[:, 7:8], ALU.mult, ALU.add).then_inc(S["cycle_c"], 1)
                    v.wait_ge(S["cycle_c"], k + 1)
                    v.wait_ge(S["twist"], k + 1)
                    tt(self.m[:], self.m[:], b[1][:], ALU.mult).then_inc(S["cycle_m"], 1)
                    if not self.relieved:
                        v.wait_ge(S["cycle_m"], k + 1)
                        tt(self.o[k][:], src, self.m[:], ALU.add).then_inc(S["cycle"], 1)

            def gpsimd(self, g, k):
                src = self.src if k == 0 else self.o[k - 1][:]
                g.wait_ge(self.S["cycle_m"], k + 1)
                nc.gpsimd.tensor_tensor(self.o[k][:], src, self.m[:], ALU.add).then_inc(self.S["cycle"], 1)

        def layer1():
            with ExitStack() as c:
                S = Steps(nc, c, "l1")
                t = lambda n, f=T: sb("l1_" + n, [128, f], c)
                sq, rs = t("sq"), t("rs")
                k_sb, kv, state, sr, y, nrm = (hold[:, i] for i in range(6))
                h = [xn] + [t(f"h{i}") for i in range(DEPTH)]
                lx = Norm(S, "xn", x[:], xn[:], sq[:], rs[:], bank[0:4])
                xf = [xn] + [t(f"f{i}") for i in range(DEPTH)]
                x1 = t("x1")
                hs = t("hs")
                qk = t("qk", 8 * T)
                of = sb("l1_of", [128, 4, T], c)
                sqq, t1 = [of[:, 0], of[:, 1]], [of[:, 2], of[:, 3]]
                rn, t2 = ([t(f"{n}{i}") for i in range(2)] for n in ("rn", "t2_"))
                vt = sb("l1_v", [128, NT, H1 + 1, DH + 1], c)
                KW = WIN + 128
                pe_ = [sb(f"l1_probs{e}", [128, 4, 256], c) for e in range(2)]
                nmax = [sb(f"l1_nmax{e}", [128, 4], c) for e in range(2)]
                NU = 2 * NT
                PW = 104
                pt = [sb(f"l1_pt{i}", [128, 4, 128], c) for i in range(2)]
                oinv = sb("l1_oinv", [128, H1], c)
                ot = sb("l1_ot", [128, H1, DH], c)
                gg = [k_sb, kv, sr]
                m = state
                lf = [Norm(S, f"ffn{i}", hs[:], nrm[:], sq[:], rs[:], bank[0:4],
                           W(f"l1_lg{i}"), W(f"l1_lb{i}")) for i in range(DEPTH)]
                with nc.Block(no_gpsimd_drain=True) as block:
                    @block.tensor
                    def _(pe):
                        def score(i, u):
                            q, e = u // 2, u % 2
                            k = NU * i + u
                            lo = 128 * q - WIN if q else 0
                            n0 = 0 if q else WIN
                            if u >= 2:
                                pe.wait_ge(S["scored"], 2 * (k - 1))
                            for f in range(2):
                                for s in range(2):
                                    g = 2 * f + s
                                    r = mm(bank[2 * e + f][:, 256 * s + n0:256 * s + KW],
                                           qk[64 * e:64 * e + 64, g * T + 128 * q:g * T + 128 * q + 128],
                                           qk[64 * e:64 * e + 64, (4 + g) * T + lo:(4 + g) * T + 128 * q + 128])
                                r.then_inc(S["score"], 1)

                        def attend(i, u):
                            q, e = u // 2, u % 2
                            k = NU * i + u
                            parts = (0, 1) if q else (1,)
                            pe.wait_ge(S["exp"], k + 1)
                            if k:
                                pe.wait_ge(S["pt"], 2 * k)
                            if e and q:
                                pe.wait_ge(S["of"], NT * i + q)
                            for f in range(2):
                                for s in range(2):
                                    for d in parts:
                                        r = nc.tensor.transpose(bank[4 + f][:, 128 * (2 * s + d):128 * (2 * s + d) + 128],
                                                                pe_[e][:, 2 * f + s, 128 * d:128 * d + 128], C("ident"))
                                r.then_inc(S["turned"], 1)
                            if u + 2 < NU:
                                score(i, u + 2)
                            if u == 0:
                                pe.wait_ge(S["vt"], NT * (i + 1))
                            if u >= 2:
                                pe.wait_ge(S["ot"], k - 1)
                            for f in range(2):
                                pe.wait_ge(S["pt"], 2 * k + f + 1)
                                for s in range(2):
                                    j = 2 * f + s
                                    for d in parts:
                                        v2 = vt[:, q - 1 + d, 2 * j + e:2 * j + e + 2, :].rearrange("p h d -> p (h d)")
                                        r = mm(bank[6 + e][:, 65 * j:65 * j + PW], pt[f][:, 2 * s + d], v2[:, 0:PW],
                                               d == parts[0], d == 1)
                                r.then_inc(S["pv"], 1)

                        def turn_outputs(i, q):
                            pe.wait_ge(S["ot"], NU * i + 2 * q + 2)
                            for g in range(4):
                                r = nc.tensor.transpose(bank[4][:, 128 * g:128 * g + 128],
                                                        ot[:, 2 * g:2 * g + 2, :].rearrange("p a d -> p (a d)"), C("ident"))
                            r.then_inc(S["oturn"], 1)

                        lx.pe(pe)
                        keep_clock(bank[7], 1)
                        def time_mix(i):
                            pe.wait_ge(S["xn"] if i == 0 else S["h"], 1)
                            mm(bank[6][:], C("centre"), h[i][:]).then_inc(S["mix_xc"], 1)
                            yield
                            pe.wait_ge(S["mix_sq"], i + 1)
                            mm(bank[7][:], C("mean"), sq[:]).then_inc(S["mix_var"], 1)
                            yield
                            pe.wait_ge(S["mix"], i + 1)
                            mm(bank[6][:], W(f"l1_Wk{i}"), nrm[:]).then_inc(S["k"], 1)
                            mm(bank[7][:], W(f"l1_Wv{i}"), nrm[:]).then_inc(S["v"], 1)
                            yield
                            pe.wait_ge(S["k_sb"], i + 1)
                            mm(bank[6][:], W(f"l1_Wr{i}"), nrm[:]).then_inc(S["r"], 1)
                            yield
                            pe.wait_ge(S["y"], i + 1)
                            mm(bank[7][:], W(f"l1_Wo{i}"), y[:]).then_inc(S["wo"], 1)

                        for i in range(DEPTH):
                            pe.wait_ge(S["hs_a"], i + 1)
                            pe.wait_ge(S["hs_b"], i + 1)

                            def project(n):
                                k = 8 * i + n
                                if n >= 2:
                                    pe.wait_ge(S["t1"], k - 1)
                                    pe.wait_ge(S["t2"], k - 1)
                                mm(bank[n % 2][:], W(f"l1_qkv{i}", lo=128 * n, n=128), hs[:]).then_inc(S["pj"], 1)
                                mm(bank[2 + n % 2][:], W(f"l1_swap{i}", lo=128 * n, n=128), hs[:]).then_inc(S["px"], 1)

                            def norms(n):
                                k = 8 * i + n
                                pe.wait_ge(S["sqq"], k + 1)
                                if n >= 2:
                                    pe.wait_ge(S["rn_ln"], k - 1)
                                mm(bank[4 + n % 2][:], C("head64"), sqq[n % 2][:]).then_inc(S["ss"], 1)

                            mix = time_mix(i)
                            for n in range(8):
                                project(n)
                                if n:
                                    norms(n - 1)
                                next(mix, None)
                            norms(7)
                            pe.wait_ge(S["h"], i + 1)
                            for q in range(NT):
                                k = NT * i + q
                                if q == 2:
                                    pe.wait_ge(S["qk"], 8 * (i + 1))
                                    score(i, 0)
                                    score(i, 1)
                                if q >= 2:
                                    pe.wait_ge(S["vt"], k - 1)
                                mm(bank[6 + q % 2][:], hs[:, 128 * q:128 * q + 128],
                                   W(f"l1_qkv{i}", lo=1024)).then_inc(S["vp"], 1)
                            pe.wait_ge(S["ones"], 2)
                            pe.wait_ge(S["rn"], 8 * (i + 1))
                            for u in range(NU):
                                if u == NU - 1:
                                    pe.wait_ge(S["scored"], 2 * (NU * i + NU - 2) + 2)
                                    pe.wait_ge(S["of"], NT * i + NT - 1)
                                    for g in range(4):
                                        mm(bank[0][:, 0:T - 128], W(f"l1_wo{i}", lo=128 * g, n=128),
                                           of[:, g, 0:T - 128], g == 0, g == 3)
                                attend(i, u)
                                if u % 2 == 0 and u:
                                    turn_outputs(i, u // 2 - 1)
                            turn_outputs(i, NT - 1)
                            pe.wait_ge(S["of"], NT * (i + 1))
                            for g in range(4):
                                r = mm(bank[0][:, T - 128:T], W(f"l1_wo{i}", lo=128 * g, n=128), of[:, g, T - 128:T],
                                       g == 0, g == 3)
                            r.then_inc(S["attn"], 1)
                            pe.wait_ge(S["hs2_a"], i + 1)
                            pe.wait_ge(S["hs2_b"], i + 1)
                            lf[i].pe(pe)
                            keep_clock(bank[6], 3)
                            pe.wait_ge(S[f"ffn{i}"], 1)
                            for n, (o, w) in enumerate(HCH):
                                mm(bank[3 + 2 * n][0:w], W(f"l1_w1_{i}", lo=HID + o, n=w), nrm[:]).then_inc(S["gp"], 1)
                                mm(bank[2 + 2 * n][0:w], W(f"l1_w1_{i}", lo=o, n=w), nrm[:]).then_inc(S["ap"], 1)
                            for n, (o, w) in enumerate(HCH):
                                pe.wait_ge(S["gg"], 3 * i + n + 1)
                                r = mm(bank[0][:], W(f"l1_w2_{n}_{i}"), gg[n][0:w], n == 0, n == 2)
                            r.then_inc(S["ffn_out"], 1)

                    @block.scalar
                    def _(a):
                        nc.scalar.preload_act_table_set("natural_log_exp_and_others")
                        lx.act(a)
                        def time_mix(i):
                            a.wait_ge(S["mix_xc"], i + 1)
                            act(sq[:], bank[6][:], ACT.Square).then_inc(S["mix_sq"], 1)
                            yield
                            a.wait_ge(S["mix_var"], i + 1)
                            act(rs[:], bank[7][:], ACT.Ln, bias=C("eps5")).then_inc(S["mix_ln"], 1)
                            a.wait_ge(S["mix_ln"], i + 1)
                            act(rs[:], rs[:], ACT.Exp, scale=-0.5).then_inc(S["mix_rs"], 1)
                            yield
                            a.wait_ge(S["k"], i + 1)
                            act(k_sb[:], bank[6][:], ACT.Copy, scale=1.0 - 0.95).then_inc(S["k_sb"], 1)
                            yield
                            a.wait_ge(S["r"], i + 1)
                            act(sr[:], bank[6][:], ACT.Sigmoid).then_inc(S["sr"], 1)
                            nc.scalar.preload_act_table_set("natural_log_exp_and_others")

                        for i in range(DEPTH):
                            if i:
                                nc.scalar.preload_act_table_set("natural_log_exp_and_others")
                            src = xf[i]
                            if i:
                                a.wait_ge(S["x2"], i)
                            a.wait_ge(S["xn"], 1)
                            act(hs[0:64], src[0:64], ACT.Copy).then_inc(S["hs_a"], 1)

                            def root(n):
                                k = 8 * i + n
                                a.wait_ge(S["ss"], k + 1)
                                if k >= 2:
                                    a.wait_ge(S["qk"], k - 1)
                                act(rn[n % 2][:], bank[4 + n % 2][:], ACT.Ln, scale=NORM_SCALE,
                                    bias=C("floor")).then_inc(S["rn_ln"], 1)
                                a.wait_ge(S["rn_ln"], k + 1)
                                act(rn[n % 2][:], rn[n % 2][:], ACT.Exp, scale=-0.5, bias=C("norm_back")).then_inc(S["rn"], 1)

                            mix = time_mix(i)
                            for n in range(8):
                                k = 8 * i + n
                                a.wait_ge(S["pj"], k + 1)
                                if n >= 2:
                                    a.wait_ge(S["ss"], k - 1)
                                act(sqq[n % 2][:], bank[n % 2][:], ACT.Square).then_inc(S["sqq"], 1)
                                if n:
                                    root(n - 1)
                                next(mix, None)
                            root(7)

                            def fetch_v(q):
                                a.wait_ge(S["vp"], NT * i + q + 1)
                                act(vt[:, q, 0:H1, 0:DH], bank[6 + q % 2][:].rearrange("p (h d) -> p h d", d=DH),
                                    ACT.Copy).then_inc(S["vt"], 1)

                            fetch_v(0)
                            fetch_v(1)
                            def outputs_back(q):
                                a.wait_ge(S["oturn"], NT * i + q + 1)
                                act(of[:, :, 128 * q:128 * q + 128], bank[4][:].rearrange("p (g t) -> p g t", g=4),
                                    ACT.Copy).then_inc(S["of"], 1)

                            def exponent(u):
                                e, n0 = u % 2, WIN if u >= 2 else 2 * WIN
                                a.wait_ge(S["centred"], NU * i + u + 1)
                                act(pe_[e][:, :, n0:256], pe_[e][:, :, n0:256], ACT.Exp).then_inc(S["exp"], 1)

                            fetch_v(2)
                            exponent(0)
                            fetch_v(3)
                            for u in range(NU):
                                q, e = u // 2, u % 2
                                k = NU * i + u
                                for f in range(2):
                                    a.wait_ge(S["turned"], 2 * k + f + 1)
                                    if k:
                                        a.wait_ge(S["pv"], 2 * (k - 1) + f + 1)
                                    act(pt[f][:, (0 if q else 1)::(1 if q else 2)],
                                        bank[4 + f][:].rearrange("p (s t) -> p s t", s=4)[:, (0 if q else 1)::(1 if q else 2)],
                                        ACT.Copy).then_inc(S["pt"], 1)
                                if u + 1 < NU:
                                    exponent(u + 1)
                                if e == 0 and q:
                                    outputs_back(q - 1)
                            outputs_back(NT - 1)
                            a.wait_ge(S["x1"], i + 1)
                            act(hs[0:64], x1[0:64], ACT.Copy).then_inc(S["hs2_a"], 1)
                            lf[i].act(a)
                            for n, (o, w) in enumerate(HCH):
                                a.wait_ge(S["gp"], 3 * i + n + 1)
                                if i:
                                    a.wait_ge(S["ffn_out"], i)
                                act(gg[n][0:w], bank[3 + 2 * n][0:w], ACT.Gelu, bias=W(f"l1_b1g{n}_{i}")).then_inc(S["gelu"], 1)
                        a.wait_ge(S["x2"], DEPTH)
                        act(rs[:], xf[2][:], ACT.Silu).then_inc(S["gate"], 1)

                    @block.vector
                    def _(v):
                        nc.vector.memset(vt[:, :, 0:H1, DH:DH + 1], 1.0).then_inc(S["ones"], 1)
                        nc.vector.memset(vt[:, :, H1:], 0.0).then_inc(S["ones"], 1)
                        for e in range(2):
                            nc.vector.memset(pe_[e][:], 0.0).then_inc(S["zero"], 1)
                        nc.vector.memset(hs[64:128, 0:1], 0.0).then_inc(S["zero"], 1)
                        v.wait_ge(S["zero"], 3)
                        lx.dve(v)
                        v.wait_ge(S["xn"], 1)
                        def time_mix(i):
                            src = h[i][:]
                            yield
                            v.wait_ge(S["mix_rs"], i + 1)
                            stt(nrm[:], bank[6][:], W(f"l1_ln_w{i}"), rs[:], ALU.mult, ALU.mult).then_inc(S["mix_g"], 1)
                            v.wait_ge(S["mix_g"], i + 1)
                            ts(nrm[:], nrm[:], W(f"l1_ln_b{i}"), None, ALU.add).then_inc(S["mix"], 1)
                            yield
                            v.wait_ge(S["k_sb"], i + 1)
                            v.wait_ge(S["v"], i + 1)
                            tt(kv[:], bank[7][:], k_sb[:], ALU.mult).then_inc(S["kv"], 1)
                            v.wait_ge(S["kv"], i + 1)
                            nc.vector.tensor_tensor_scan(state[:], C("decay"), kv[:], 0.0, ALU.mult,
                                                         ALU.add).then_inc(S["state"], 1)
                            yield
                            v.wait_ge(S["state"], i + 1)
                            v.wait_ge(S["sr"], i + 1)
                            tt(y[:], state[:], sr[:], ALU.mult).then_inc(S["y"], 1)
                            yield
                            v.wait_ge(S["wo"], i + 1)
                            tt(h[i + 1][:], src, bank[7][:], ALU.add).then_inc(S["h"], 1)

                        for i in range(DEPTH):
                            src = xf[i]
                            nc.vector.tensor_copy(hs[64:128, 1:T], src[64:128, 0:T - 1]).then_inc(S["hs_b"], 1)

                            def turn(n):
                                k = 8 * i + n
                                v.wait_ge(S["rn"], k + 1)
                                v.wait_ge(S["t3"], k + 1)
                                if n == 0 and i:
                                    v.wait_ge(S["score"], 2 * NU * i)
                                stt(qk[:, n * T:(n + 1) * T], rn[n % 2][:], 1e12, t1[n % 2][:], ALU.min,
                                    ALU.mult).then_inc(S["qk"], 1)

                            mix = time_mix(i)
                            for n in range(8):
                                k = 8 * i + n
                                table = 4 * i + 2 * (n // 4)
                                v.wait_ge(S["pj"], k + 1)
                                v.wait_ge(S["sqq"], k + 1)
                                if k >= 2:
                                    v.wait_ge(S["qk"], k - 1)
                                tt(t1[n % 2][:], bank[n % 2][:], rot[:, table], ALU.mult).then_inc(S["t1"], 1)
                                v.wait_ge(S["px"], k + 1)
                                if k >= 2:
                                    v.wait_ge(S["t3"], k - 1)
                                tt(t2[n % 2][:], bank[2 + n % 2][:], rot[:, table + 1], ALU.mult).then_inc(S["t2"], 1)
                                if n:
                                    turn(n - 1)
                                next(mix, None)
                            turn(7)
                            def centre(u):
                                q, e = u // 2, u % 2
                                k = NU * i + u
                                n0 = 0 if q else WIN
                                if k >= 2:
                                    v.wait_ge(S["turned"], 2 * (k - 1))
                                for f in range(2):
                                    v.wait_ge(S["score"], 2 * k + f + 1)
                                    stt(pe_[e][:, 2 * f:2 * f + 2, WIN + n0:256],
                                        bank[2 * e + f][:].rearrange("p (a j) -> p a j", a=2)[:, :, n0:KW], 8.0,
                                        C("band")[:, None, n0:KW].to_broadcast([128, 2, KW - n0]),
                                        ALU.mult, ALU.add).then_inc(S["scored"], 1)
                                v.wait_ge(S["scored"], 2 * k + 2)
                                nc.vector.tensor_reduce(nmax[e][:], pe_[e][:, :, WIN + n0:256], AX.X, ALU.max).then_inc(S["max"], 1)
                                v.wait_ge(S["max"], k + 1)
                                tt(pe_[e][:, :, WIN + n0:256], pe_[e][:, :, WIN + n0:256],
                                   nmax[e][:, :, None].to_broadcast([128, 4, KW - n0]), ALU.subtract).then_inc(S["centred"], 1)

                            def outputs(u):
                                q, e = u // 2, u % 2
                                k = NU * i + u
                                v.wait_ge(S["pv"], 2 * k + 2)
                                o = bank[6 + e][:, 0:260].rearrange("p (h d) -> p h d", d=65)
                                nc.vector.reciprocal(oinv[:, 4 * e:4 * e + 4, None], o[:, :, 64:65]).then_inc(S["oinv"], 1)
                                v.wait_ge(S["oinv"], k + 1)
                                if k >= 2:
                                    v.wait_ge(S["oturn"], NT * i + q)
                                tt(ot[:, e:H1:2], o[:, :, 0:64],
                                   oinv[:, 4 * e:4 * e + 4, None].to_broadcast([128, 4, 64]), ALU.mult).then_inc(S["ot"], 1)

                            centre(0)
                            centre(1)
                            for u in range(NU):
                                if u + 2 < NU:
                                    centre(u + 2)
                                outputs(u)
                            v.wait_ge(S["attn"], i + 1)
                            tt(x1[:], src[:], bank[0][:], ALU.add).then_inc(S["x1"], 1)
                            v.wait_ge(S["x1"], i + 1)
                            nc.vector.tensor_copy(hs[64:128, 1:T], x1[64:128, 0:T - 1]).then_inc(S["hs2_b"], 1)
                            v.wait_ge(S["hs2_a"], i + 1)
                            v.wait_ge(S["hs2_b"], i + 1)
                            lf[i].dve(v)
                            for n, (o, w) in enumerate(HCH):
                                v.wait_ge(S["gelu"], 3 * i + n + 1)
                                v.wait_ge(S["ap"], 3 * i + n + 1)
                                stt(gg[n][0:w], bank[2 + 2 * n][0:w], W(f"l1_b1a{n}_{i}"), gg[n][0:w], ALU.add,
                                    ALU.mult).then_inc(S["gg"], 1)
                            v.wait_ge(S["ffn_out"], i + 1)
                            stt(xf[i + 1][:], bank[0][:], W(f"l1_b2_{i}"), x1[:], ALU.add, ALU.add).then_inc(S["x2"], 1)
                            v.wait_ge(S["x2"], i + 1)
                        v.wait_ge(S["gate"], 1)
                        v.wait_ge(S["h"], DEPTH)
                        tt(m[:], rs[:], h[2][:], ALU.mult).then_inc(S["m"], 1)
                        v.wait_ge(S["m"], 1)
                        tt(x[:], x[:], m[:], ALU.add).then_inc(S["x_new"], 1)

                    @block.gpsimd
                    def _(g):
                        for k in range(8 * DEPTH):
                            g.wait_ge(S["t1"], k + 1)
                            g.wait_ge(S["t2"], k + 1)
                            nc.gpsimd.tensor_tensor(t1[k % 2][:], t1[k % 2][:], t2[k % 2][:], ALU.add).then_inc(S["t3"], 1)
                S.clear()

        def layer2():
            with ExitStack() as c:
                S = Steps(nc, c, "l2")
                t = lambda n, f=T: sb("l2_" + n, [128, f], c)
                sq, rs, left, y1 = (hold[:, i] for i in range(4))
                lx = Norm(S, "xn", x[:], xn[:], sq[:], rs[:], bank[0:4])
                xp = sb("l2_xp", [128, 2, T + 3], c)
                cv = sb("l2_cv", [128, 2, T], c)
                u, sg, dt, du = (sb("l2_" + n, [128, 2, T], c) for n in ("u", "sg", "dt", "du"))
                xr, xd = t("xr"), t("xd")
                da, db, hh, hc = ([sb(f"l2_{n}{i}", [128, 2, T], c) for i in range(2)] for n in ("da", "db", "h", "hc"))
                cn = [t(f"cn{i}") for i in range(3)]
                parts, mid = (c.enter_context(nc.sbuf_tensor("l2_" + n, [96, T], BF16)) for n in ("parts", "mid"))
                lg = sb("l2_lg", [128, NT, NE], c)
                pw = sb("l2_pw", [128, NT, NE], c)
                g3, g4 = (sb("l2_" + n, [128, NT, NE, NE], c) for n in ("gt", "ge"))
                nm = sb("l2_nm", [128, NT], c)
                gt = [sb("l2_gates", [128, NT, NE], c)][0]
                xg = [cv[:, 0], cv[:, 1]]
                h1 = [hold[:, 4], hold[:, 5]]
                hg = [t(f"hg{i}") for i in range(2)]
                with nc.Block(no_gpsimd_drain=True) as block:
                    @block.tensor
                    def _(pe):
                        lx.pe(pe)
                        keep_clock(bank[7], 1)
                        pe.wait_ge(S["xn"], 1)
                        for n in range(4):
                            mm(bank[n][:], W("l2_in", lo=128 * n, n=128), xn[:]).then_inc(S["in"], 1)
                        for q in range(NT):
                            mm(bank[4][:, NE * q:NE * q + NE], xn[:, 128 * q:128 * q + 128], W("l2_router"), True, False)
                            r = mm(bank[4][:, NE * q:NE * q + NE], C("ones_row"), W("l2_router_b"), False, True)
                        r.then_inc(S["logits"], 1)
                        keep_clock(bank[7], 2)
                        for n in range(2):
                            pe.wait_ge(S["u"], n + 1)
                            r = mm(bank[5][0:96], W("l2_xproj", lo=96 * n, n=96), u[:, n], n == 0, n == 1)
                        r.then_inc(S["xproj"], 1)
                        keep_clock(bank[7], 1)
                        pe.wait_ge(S["xsq"], 1)
                        mm(bank[6][0:96], C("rms"), xr[0:96]).then_inc(S["xms"], 1)
                        keep_clock(bank[7], 2)
                        pe.wait_ge(S["xd"], 1)
                        for n in range(2):
                            mm(bank[n][:], W("l2_dt", lo=128 * n, n=128), xd[0:64]).then_inc(S["dtp"], 1)
                        mm(bank[6][0:96], C("three"), xd[0:96]).then_inc(S["three"], 1)
                        pe.wait_ge(S["gates"], 1)
                        pe.wait_ge(S["sg"], 2)
                        pe.wait_ge(S["dtz"], 2)

                        def gather(n):
                            pe.wait_ge(S["hc"], n + 1)
                            mm(bank[6][:], C("ident"), hc[n % 2][:, 0], n == 0, n == NS - 1).then_inc(S["y"], 1)

                        def down(n):
                            pe.wait_ge(S["hg"], n + 1)
                            mm(bank[0][:], W(f"l2_w2_{n // FCH}", lo=128 * (n % FCH), n=128), hg[n % 2][:], n == 0,
                               n == NE * FCH - 1).then_inc(S["down"], 1)

                        assert NS == NE * FCH
                        def w1(n):
                            e, k = n // FCH, n % FCH
                            if n >= 2:
                                pe.wait_ge(S["silu"], n - 1)
                            mm(bank[4 + 3 * (n % 2)][:], W(f"l2_w1_{e}", lo=128 * k, n=128), xn[:]).then_inc(S["w1"], 1)

                        for n in range(NS):
                            e, k = n // FCH, n % FCH
                            if k == 0:
                                if e:
                                    pe.wait_ge(S["xg"], e)
                                for q in range(NT):
                                    r = mm(bank[1][:, 128 * q:128 * q + 128], gt[:, q, e:e + 1].to_broadcast([128, 128]),
                                           C("ident"))
                                r.then_inc(S["gbc"], 1)
                            if n == 0:
                                w1(0)
                                pe.wait_ge(S["parts"], 3)
                            if n:
                                pe.wait_ge(S["db"], n)
                            mm(bank[2][:], pick[:, n:n + 1].to_broadcast([96, 128]), parts[:]).then_inc(S["Bn"], 1)
                            if n:
                                pe.wait_ge(S["cn"], n)
                            mm(bank[3][:], pick[:, NS + n:NS + n + 1].to_broadcast([96, 128]), parts[:]).then_inc(S["Cn"], 1)
                            if n:
                                w1(n)
                            if n >= 2:
                                gather(n - 2)
                            if n:
                                pe.wait_ge(S["hg"], n)
                            if k == 0:
                                pe.wait_ge(S["xg"], e + 1)
                            mm(bank[5][:], W(f"l2_w3_{e}", lo=128 * k, n=128), xg[e % 2]).then_inc(S["w3"], 1)
                            if n:
                                down(n - 1)
                        gather(NS - 2)
                        gather(NS - 1)
                        down(NS - 1)
                        pe.wait_ge(S["yg"], 2)
                        for n in range(2):
                            r = mm(bank[2][:], W("l2_out", lo=128 * n, n=128), cv[:, n], n == 0, n == 1)
                        r.then_inc(S["s"], 1)

                    @block.scalar
                    def _(a):
                        nc.scalar.preload_act_table_set("natural_log_exp_and_others")
                        lx.act(a)
                        for n in range(2):
                            a.wait_ge(S["in"], n + 1)
                            act(xp[:, n, 1:T + 1], bank[n][:], ACT.Copy).then_inc(S["xp"], 1)
                        for n in range(2):
                            a.wait_ge(S["in"], n + 3)
                            act(sg[:, n], bank[2 + n][:], ACT.Silu).then_inc(S["sg"], 1)
                        for n in range(2):
                            a.wait_ge(S["conv"], n + 1)
                            act(u[:, n], cv[:, n], ACT.Silu).then_inc(S["u"], 1)
                        nc.scalar.preload_act_table_set("natural_log_exp_and_others")
                        a.wait_ge(S["centred"], 1)
                        act(pw[:], lg[:], ACT.Exp).then_inc(S["pw"], 1)
                        a.wait_ge(S["xproj"], 1)
                        act(xr[0:96], bank[5][0:96], ACT.Square).then_inc(S["xsq"], 1)
                        a.wait_ge(S["xms"], 1)
                        act(rs[0:96], bank[6][0:96], ACT.Ln, bias=C("eps6", 96)).then_inc(S["xr_ln"], 1)
                        a.wait_ge(S["xr_ln"], 1)
                        act(rs[0:96], rs[0:96], ACT.Exp, scale=-0.5).then_inc(S["xrs"], 1)
                        for n in range(2):
                            a.wait_ge(S["dtp"], n + 1)
                            act(cv[:, n], bank[n][:], ACT.Abs, bias=W("l2_dt_b", lo=n, n=1)).then_inc(S["dt_abs"], 1)
                        for n in range(2):
                            a.wait_ge(S["dt_abs"], n + 1)
                            act(cv[:, n], cv[:, n], ACT.Exp, scale=-1.0).then_inc(S["dt_exp"], 1)
                        a.wait_ge(S["three"], 1)
                        act(parts[:], bank[6][0:96], ACT.Copy).then_inc(S["parts"], 1)
                        a.wait_ge(S["dt_exp"], 1)
                        act(cv[:, 0], cv[:, 0], ACT.Ln, bias=C("one")).then_inc(S["dt_ln"], 1)
                        a.wait_ge(S["left"], 1)
                        act(mid[:], left[0:96], ACT.Copy).then_inc(S["mid"], 1)
                        a.wait_ge(S["dt_exp"], 2)
                        act(cv[:, 1], cv[:, 1], ACT.Ln, bias=C("one")).then_inc(S["dt_ln"], 1)
                        a.wait_ge(S["mid"], 1)
                        act(parts[32:64], mid[32:64], ACT.Copy).then_inc(S["parts"], 1)
                        nc.scalar.preload_act_table_set("exp_and_others")

                        def expert(n):
                            a.wait_ge(S["w1"], n + 1)
                            if n >= 2:
                                a.wait_ge(S["hg"], n - 1)
                            act(h1[n % 2][:], bank[4 + 3 * (n % 2)][:], ACT.Tanh, scale=0.5).then_inc(S["h1"], 1)

                        a.wait_ge(S["dt"], 2)
                        for n in range(NS):
                            if n:
                                expert(n - 1)
                            a.wait_ge(S["Cn"], n + 1)
                            if n >= 3:
                                a.wait_ge(S["hc"], n - 2)
                            act(cn[n % 3][:], bank[3][:], ACT.Copy).then_inc(S["cn"], 1)
                            if n >= 2:
                                a.wait_ge(S["h"], 2 * n - 2)
                            for k in range(2):
                                act(da[n % 2][:, k], dt[:, k], ACT.Exp,
                                    scale=a_neg[:, NS * k + n:NS * k + n + 1]).then_inc(S["da"], 1)
                        expert(NS - 1)
                        a.wait_ge(S["down"], NE * FCH)
                        act(rs[:], bank[0][:], ACT.Silu).then_inc(S["gate"], 1)

                    @block.vector
                    def _(v):
                        nc.vector.memset(xp[:, :, 0:1], 0.0).then_inc(S["pads"], 1)
                        nc.vector.memset(xp[:, :, T + 1:T + 3], 0.0).then_inc(S["pads"], 1)
                        lx.dve(v)
                        v.wait_ge(S["pads"], 2)
                        for n in range(2):
                            v.wait_ge(S["xp"], n + 1)
                            ts(cv[:, n], xp[:, n, 0:T], W("l2_conv", lo=4 * n, n=1), W("l2_conv_b", lo=n, n=1),
                               ALU.mult, ALU.add).then_inc(S["tap"], 1)
                            for k in range(1, 4):
                                v.wait_ge(S["tap"], 3 * n + k)
                                r = stt(cv[:, n], xp[:, n, k:k + T], W("l2_conv", lo=4 * n + k, n=1), cv[:, n],
                                        ALU.mult, ALU.add)
                                r.then_inc(S["tap"] if k < 3 else S["conv"], 1)
                        v.wait_ge(S["logits"], 1)
                        l4 = bank[4][:, 0:NT * NE].rearrange("p (q e) -> p q e", e=NE)
                        nc.vector.tensor_reduce(nm[:], l4, AX.X, ALU.max).then_inc(S["lmax"], 1)
                        v.wait_ge(S["lmax"], 1)
                        tt(lg[:], l4, nm[:, :, None].to_broadcast([128, NT, NE]), ALU.subtract).then_inc(S["centred"], 1)
                        v.wait_ge(S["pw"], 1)
                        pf = pw[:, :, None, :].to_broadcast([128, NT, NE, NE])
                        pe_ = pw[:, :, :, None].to_broadcast([128, NT, NE, NE])
                        tt(g3[:], pf, pe_, ALU.is_gt).then_inc(S["gt"], 1)
                        tt(g4[:], pf, pe_, ALU.is_ge).then_inc(S["ge"], 1)
                        v.wait_ge(S["gt"], 1)
                        flat = "p q e f -> p (q e f)"
                        tt(g3[:].rearrange(flat), g3[:].rearrange(flat), C("untie"), ALU.mult).then_inc(S["gt"], 1)
                        v.wait_ge(S["ge"], 1)
                        tt(g4[:].rearrange(flat), g4[:].rearrange(flat), C("tie"), ALU.mult).then_inc(S["ge"], 1)
                        v.wait_ge(S["gt"], 2)
                        v.wait_ge(S["ge"], 2)
                        tt(g3[:], g3[:], g4[:], ALU.add).then_inc(S["gt"], 1)
                        v.wait_ge(S["gt"], 3)
                        nc.vector.tensor_reduce(lg[:], g3[:], AX.X, ALU.add).then_inc(S["rank"], 1)
                        v.wait_ge(S["rank"], 1)
                        stt(gt[:], lg[:], 2.0, pw[:], ALU.is_lt, ALU.mult).then_inc(S["kept"], 1)
                        v.wait_ge(S["kept"], 1)
                        nc.vector.tensor_reduce(nm[:], gt[:], AX.X, ALU.add).then_inc(S["gsum"], 1)
                        v.wait_ge(S["gsum"], 1)
                        nc.vector.reciprocal(nm[:], nm[:]).then_inc(S["ginv"], 1)
                        v.wait_ge(S["ginv"], 1)
                        stt(gt[:], gt[:], 0.5, nm[:, :, None].to_broadcast([128, NT, NE]), ALU.mult,
                            ALU.mult).then_inc(S["gates"], 1)
                        v.wait_ge(S["xrs"], 1)
                        stt(xd[0:96], bank[5][0:96], W("l2_xln"), rs[0:96], ALU.mult, ALU.mult).then_inc(S["xd"], 1)
                        for n in range(2):
                            v.wait_ge(S["dt_abs"], n + 1)
                            ts(dt[:, n], bank[n][:], W("l2_dt_b", lo=n, n=1), None, ALU.add).then_inc(S["dtz"], 1)
                        v.wait_ge(S["parts"], 1)
                        tt(left[0:96], bank[6][0:96], parts[:], ALU.subtract).then_inc(S["left"], 1)
                        def step_size(n):
                            v.wait_ge(S["dtz"], n + 1)
                            v.wait_ge(S["dt_ln"], n + 1)
                            stt(dt[:, n], dt[:, n], 0.0, cv[:, n], ALU.max, ALU.add).then_inc(S["dt"], 1)

                        def gate(e):
                            v.wait_ge(S["gbc"], e + 1)
                            if e == 0:
                                v.wait_ge(S["dt"], 1)
                            if e >= 2:
                                v.wait_ge(S["w3"], FCH * (e - 1))
                            tt(xg[e % 2], xn[:], bank[1][:], ALU.mult).then_inc(S["xg"], 1)

                        step_size(0)
                        v.wait_ge(S["mid"], 1)
                        v.wait_ge(S["left"], 1)
                        tt(parts[64:96], left[64:96], mid[64:96], ALU.subtract).then_inc(S["parts"], 1)
                        gate(0)
                        step_size(1)
                        for n in range(2):
                            v.wait_ge(S["dt"], n + 1)
                            tt(du[:, n], dt[:, n], u[:, n], ALU.mult).then_inc(S["du"], 1)
                        v.wait_ge(S["du"], 2)

                        def scan(n):
                            for k in range(2):
                                v.wait_ge(S["da"], 2 * n + k + 1)
                                v.wait_ge(S["db"], n + 1)
                                if n >= 2:
                                    v.wait_ge(S["hc"], n - 1)
                                nc.vector.tensor_tensor_scan(hh[n % 2][:, k], da[n % 2][:, k], db[n % 2][:, k], 0.0,
                                                             ALU.mult, ALU.add).then_inc(S["h"], 1)

                        def expert(n):
                            v.wait_ge(S["h1"], n + 1)
                            stt(h1[n % 2][:], h1[n % 2][:], 1.0, bank[4 + 3 * (n % 2)][:], ALU.add, ALU.mult).then_inc(S["silu"], 1)
                            v.wait_ge(S["silu"], n + 1)
                            v.wait_ge(S["w3"], n + 1)
                            if n >= 2:
                                v.wait_ge(S["down"], n - 1)
                            tt(hg[n % 2][:], h1[n % 2][:], bank[5][:], ALU.mult).then_inc(S["hg"], 1)

                        for n in range(NS):
                            e = n // FCH
                            if n:
                                expert(n - 1)
                            v.wait_ge(S["Bn"], n + 1)
                            if n >= 2:
                                v.wait_ge(S["h"], 2 * n - 2)
                            tt(db[n % 2][:], du[:], bank[2][:, None, :].to_broadcast([128, 2, T]),
                               ALU.mult).then_inc(S["db"], 1)
                            if n and n % FCH == 0:
                                gate(e)
                            if n:
                                scan(n - 1)
                        expert(NS - 1)
                        scan(NS - 1)
                        v.wait_ge(S["y"], NS)
                        v.wait_ge(S["y1"], NS - 1)
                        for n, yn in enumerate((bank[6], y1)):
                            stt(du[:, n], u[:, n], W("l2_D", lo=n, n=1), yn[:], ALU.mult, ALU.add).then_inc(S["yd"], 1)
                        v.wait_ge(S["w3"], NE * FCH)
                        for n in range(2):
                            v.wait_ge(S["yd"], n + 1)
                            tt(cv[:, n], du[:, n], sg[:, n], ALU.mult).then_inc(S["yg"], 1)
                        v.wait_ge(S["s"], 1)
                        v.wait_ge(S["gate"], 1)
                        tt(sq[:], rs[:], bank[2][:], ALU.mult).then_inc(S["m"], 1)
                        v.wait_ge(S["m"], 1)
                        tt(x[:], x[:], sq[:], ALU.add).then_inc(S["x_new"], 1)

                    @block.gpsimd
                    def _(g):
                        for n in range(NS):
                            g.wait_ge(S["h"], 2 * n + 2)
                            g.wait_ge(S["cn"], n + 1)
                            if n >= 2:
                                g.wait_ge(S["y"], n - 1)
                                g.wait_ge(S["y1"], n - 1)
                            nc.gpsimd.tensor_tensor(hc[n % 2][:], hh[n % 2][:],
                                                    cn[n % 3][:, None, :].to_broadcast([128, 2, T]),
                                                    ALU.mult).then_inc(S["hc"], 1)
                            if n:
                                g.wait_ge(S["hc"], n + 1)
                                if n >= 2:
                                    g.wait_ge(S["y1"], n - 1)
                                nc.gpsimd.tensor_tensor(y1[:], hc[0][:, 1] if n == 1 else y1[:], hc[n % 2][:, 1],
                                                        ALU.add).then_inc(S["y1"], 1)
                S.clear()

        def layer3():
            with ExitStack() as c:
                S = Steps(nc, c, "l3")
                t = lambda n, f=T: sb("l3_" + n, [128, f], c)
                RS, RM = 6, 4
                sc = [t(f"sc{i}") for i in range(RS)]
                sq, rs = sc[4], sc[5]
                lx = Norm(S, "xn", x[:], xn[:], sq[:], rs[:], bank[4:8])
                cp = Coupling(S, "L3", 1, c, (bank[6], bank[7]), xn[:], relieved=True)
                G = 2 * H3
                qk = sb("l3_qk", [128, 2, NT, D], c)
                qk2 = sb("l3_qk2", [128, 2, NT, D], c)
                mu, var, mx = (sb("l3_" + n, [128, NT * G], c) for n in ("mu", "var", "mx"))
                VW = 11
                vt = sb("l3_v", [128, NT, H3 + VW, D3 + 1], c)
                km = sb("l3_km", [128, 4, T], c)
                qm = hold[:, 0:4]
                qft = t("qft")
                kvm = sb("l3_kvm", [128, H3, D3 + 1], c)
                ol = sb("l3_ol", [128, NT, H3, D3 + 1], c)
                wk_, pp, pt = ([t(f"{n}{i}") for i in range(2)] for n in ("wk", "pp", "pt"))
                ex = [t(f"ex{i}") for i in range(RM)]
                m8 = [sb(f"l3_m8{i}", [128, 4, 8], c) for i in range(RM)]
                nmx = [sb(f"l3_nmx{i}", [128, 1], c) for i in range(RM)]
                og = [sb(f"l3_og{i}", [128, H3, D3 + 1], c) for i in range(2)]
                zs = sb("l3_zs", [128, NT, H3], c)
                den = sb("l3_den", [128, 2, H3], c)
                zi = sb("l3_zi", [128, NT, H3], c)
                oo = qk[:, 0]
                o1 = qk2[:, 0, 0].rearrange("p (h d) -> p h d", d=D3)
                of = qft
                SC = D3 ** -0.5
                g8 = "p q (g d) -> p (q g) d"
                GH = NT * H3
                tiles = [(q, h) for q in range(NT) for h in range(H3)]
                N = len(tiles)
                FIRST = 7
                op = Opening(S, [cp.h1, cp.h2, cp.h3, cp.m, cp.o[0], cp.o[1], cp.h1, cp.h2], bank[0], bank[1], bank[2],
                             bank[6], bank[7])
                OPEN = 26
                cycles = [2 * (FIRST + 7 + 5 * k) + 1 for k in range(3)]
                tops = lambda n, k: 8 * (n // 2) + 2 * k + n % 2 + 1
                rests = lambda n, k: 6 * (n // 2) + 2 * k + n % 2 + 1
                with nc.Block(no_gpsimd_drain=True) as block:
                    @block.sync
                    def _(sp):
                        sp.dma_start(x0, x_in[b + 1]).then_inc(S["x0"], 16)

                    @block.tensor
                    def _(pe):
                        lx.pe(pe)
                        pe.wait_ge(S["xn"], 1)
                        for q in range(NT):
                            mm(bank[q][:, 0:384], xn[:, 128 * q:128 * q + 128], W("l3_qkv")).then_inc(S["qkv"], 1)
                        keep_clock(bank[6], 2)
                        for n, part in enumerate((1, 0)):
                            pe.wait_ge(S["qk_n"], n + 1)
                            for q in range(NT):
                                r = nc.tensor.transpose(bank[4 + part][:, 128 * q:128 * q + 128],
                                                        qk[:, part, q], C("ident"))
                            r.then_inc(S["qk_turn"], 1)
                        def linear_kv():
                            pe.wait_ge(S["soft"], 1)
                            pe.wait_ge(S["ones"], 1)
                            for q in range(NT):
                                r = mm(bank[6][:, 0:H3 * 9], qk2[:, 1, q], vt[:, q, 0:H3].rearrange("p h d -> p (h d)"),
                                       q == 0, q == NT - 1)
                            r.then_inc(S["kv"], 1)
                            for q in range(NT):
                                r = nc.tensor.transpose(bank[7][:, 128 * q:128 * q + 128], qk2[:, 0, q], C("ident"))
                            r.then_inc(S["qf_turn"], 1)

                        def linear_out():
                            pe.wait_ge(S["kvm"], 1)
                            pe.wait_ge(S["qft"], 1)
                            for q in range(NT):
                                r = mm(bank[6 + q // 2][:, 256 * (q % 2):256 * (q % 2) + H3 * 9],
                                       qft[:, 128 * q:128 * q + 128], kvm[:].rearrange("p h d -> p (h d)"))
                            r.then_inc(S["lin"], 1)

                        def score(n):
                            q, h = tiles[n]
                            if n >= 3:
                                pe.wait_ge(S["sc"], n - 2)
                            if q == 0:
                                pe.wait_ge(S["qm"], min(h, 3) + 1)
                                pe.wait_ge(S["km"], h // 4 + 1)
                            mm(bank[n % 3][:], qm[:, h % 4, 128 * q:128 * q + 128],
                               km[:, h // 4, :]).then_inc(S["score"], 1)

                        def values(n):
                            q, h = tiles[n]
                            pe.wait_ge(S["pt"], n + 1)
                            if h == 0 and q:
                                pe.wait_ge(S["og"], q)
                            for k in range(NT):
                                r = mm(bank[5][:, 9 * h:9 * (h + VW)], pt[n % 2][:, 128 * k:128 * k + 128],
                                       vt[:, k, h:h + VW].rearrange("p h d -> p (h d)"),
                                       k == 0, k == NT - 1)
                            r.then_inc(S["pv"], 1)

                        pe.wait_ge(S["vt"], NT)
                        pe.wait_ge(S["zeros"], 1)
                        LEAD = 5
                        for n in range(LEAD):
                            score(n)
                        ff = cp.pe(pe)
                        for n in range(N):
                            if n + LEAD < N:
                                score(n + LEAD)
                            pe.wait_ge(S["pp"], n + 1)
                            if n >= 2:
                                pe.wait_ge(S["pt"], n - 1)
                            for k in range(NT):
                                r = nc.tensor.transpose(bank[3 + n % 2][:, 128 * k:128 * k + 128],
                                                        pp[n % 2][:, 128 * k:128 * k + 128], C("ident"))
                            r.then_inc(S["turned"], 1)
                            if n == N - 2:
                                next(opening)
                            if n:
                                values(n - 1)
                            if n == 5:
                                linear_kv()
                            if n == 9:
                                linear_out()
                            if n == 2 * FIRST - 3:
                                pe.wait_ge(S["ol"], 1)
                            if n % 2 and n >= 2 * FIRST - 1:
                                next(ff, None)
                            if n == 2 * OPEN - 1:
                                for _ in ff:
                                    pass
                                opening = op.pe(pe)
                                next(opening)
                            if n == 2 * OPEN + 1:
                                next(opening)
                            if n == N - 5:
                                next(opening)
                            if n == N - 3:
                                pe.wait_ge(S["sc"], N)
                                next(opening)
                            if n == N - 2:
                                next(opening)
                        values(N - 1)
                        for _ in opening:
                            pass
                        pe.wait_ge(S["oo"], NT)
                        for q in range(NT):
                            r = nc.tensor.transpose(bank[3][:, 128 * q:128 * q + 128], oo[:, q], C("ident"))
                        r.then_inc(S["o_turn"], 1)
                        pe.wait_ge(S["of"], 1)
                        mm(bank[4][:], W("l3_proj"), of[:]).then_inc(S["s"], 1)

                    @block.scalar
                    def _(a):
                        def turn_out(a, n):
                            a.wait_ge(S["turned"], n + 1)
                            if n >= 2:
                                a.wait_ge(S["pv"], n - 1)
                            act(pt[n % 2][:], bank[3 + n % 2][:], ACT.Copy).then_inc(S["pt"], 1)

                        nc.scalar.preload_act_table_set("natural_log_exp_and_others")
                        lx.act(a)
                        for q in range(NT):
                            a.wait_ge(S["qk"], q + 1)
                            act(qk2[:, :, q], qk[:, :, q], ACT.Square).then_inc(S["qk_sq"], 1)
                        a.wait_ge(S["qk_ss"], NT)
                        for n, part in enumerate((1, 0)):
                            g0 = slice(GH * part, GH * part + GH)
                            act(var[:, g0], mu[:, g0], ACT.Ln, scale=1.0 / D3, bias=C("eps5")).then_inc(S["qk_ln"], 1)
                            a.wait_ge(S["qk_ln"], n + 1)
                            act(var[:, g0], var[:, g0], ACT.Exp, scale=-0.5).then_inc(S["qk_rs"], 1)

                        def mask_q(r):
                            act(qm[:, r], bank[4][:], ACT.Identity, scale=keep[:, 0, r:r + 1],
                                bias=keep[:, 2, r:r + 1]).then_inc(S["qm"], 1)

                        def mask_k(g):
                            act(km[:, g], bank[5][:], ACT.Identity, scale=keep[:, 1, g:g + 1],
                                bias=keep[:, 3, g:g + 1]).then_inc(S["km"], 1)

                        a.wait_ge(S["qk_turn"], 1)
                        mask_k(0)
                        a.wait_ge(S["qk_turn"], 2)
                        mask_q(0)
                        def fetch(n):
                            a.wait_ge(S["score"], n + 1)
                            if n >= RS:
                                a.wait_ge(S["kept"], n - RS + 1)
                            act(sc[n % RS][:], bank[n % 3][:], ACT.Copy).then_inc(S["sc"], 1)

                        def exponent(n):
                            q, h = tiles[n]
                            a.wait_ge(S["nmx"], n + 1)
                            if n >= RM:
                                a.wait_ge(S["pp"], n - RM + 1)
                            act(ex[n % RM][:], sc[n % RS][:], ACT.Exp, scale=SC, bias=nmx[n % RM][:],
                                accum_out=zs[:, q, h:h + 1]).then_inc(S["ex"], 1)

                        def take_outputs(q):
                            a.wait_ge(S["pv"], H3 * (q + 1))
                            if q >= 2:
                                a.wait_ge(S["os"], q - 1)
                            act(og[q % 2][:], bank[5][:, 0:H3 * 9].rearrange("p (h d) -> p h d", d=9),
                                ACT.Copy).then_inc(S["og"], 1)

                        ff = cp.act(a)
                        for n in range(3):
                            mask_q(n + 1)
                            fetch(n)
                        fetch(3)
                        for g in range(1, 4):
                            mask_k(g)
                        for p in range(N // 2):
                            exponent(2 * p)
                            exponent(2 * p + 1)
                            for e in range(2):
                                if p:
                                    turn_out(a, 2 * p - 2 + e)
                                    if e == 0 and p > 1 and (2 * p - 2) % H3 == 0:
                                        take_outputs((2 * p - 2) // H3 - 1)
                                if 2 * p + 4 + e < N:
                                    fetch(2 * p + 4 + e)
                            if p == 1:
                                a.wait_ge(S["soft_c"], 1)
                                act(qk2[:], qk2[:], ACT.Exp).then_inc(S["soft_e"], 1)
                            if p == 3:
                                a.wait_ge(S["qf_turn"], 1)
                                act(qft[:], bank[7][:], ACT.Copy).then_inc(S["qft"], 1)
                            if p >= FIRST:
                                next(ff, None)
                            if p == OPEN:
                                for _ in ff:
                                    pass
                                cp.act_silu(a)
                                opening = op.act(a)
                                next(opening)
                            if p == OPEN + 1:
                                nc.scalar.preload_act_table_set("natural_log_exp_and_others")
                                next(opening)
                            if p == N // 2 - 2:
                                nc.scalar.preload_act_table_set("exp_and_others")
                                next(opening)
                            if p == N // 2 - 1:
                                next(opening)
                        turn_out(a, N - 2)
                        next(opening)
                        turn_out(a, N - 1)
                        nc.scalar.preload_act_table_set("natural_log_exp_and_others")
                        take_outputs(NT - 1)
                        for _ in opening:
                            pass
                        a.wait_ge(S["o_turn"], 1)
                        act(of[:], bank[3][:], ACT.Copy).then_inc(S["of"], 1)

                    @block.vector
                    def _(v):
                        def outputs(v, q):
                            v.wait_ge(S["og"], q + 1)
                            v.wait_ge(S["ex"], H3 * (q + 1))
                            o9 = og[q % 2][:]
                            stt(den[:, 0, :, None], zs[:, q, :, None], 1e-8, o9[:, :, D3:9], ALU.mult, ALU.add).then_inc(S["den"], 1)
                            v.wait_ge(S["den"], 3 * q + 1)
                            nc.vector.reciprocal(den[:, 1], den[:, 0]).then_inc(S["den"], 1)
                            v.wait_ge(S["den"], 3 * q + 2)
                            tt(den[:, 0], den[:, 1], alpha[:, 0], ALU.mult).then_inc(S["den"], 1)
                            v.wait_ge(S["den"], 3 * q + 3)
                            tt(o1[:], o9[:, :, 0:D3], den[:, 0, :, None].to_broadcast([128, H3, D3]), ALU.mult).then_inc(S["os"], 1)
                            v.wait_ge(S["os"], q + 1)
                            tt(oo[:, q].rearrange("p (h d) -> p h d", d=D3), o1[:], ol[:, q, :, 0:D3], ALU.add).then_inc(S["oo"], 1)

                        nc.vector.memset(vt[:, :, 0:H3, D3:D3 + 1], 1.0).then_inc(S["ones"], 1)
                        lx.dve(v)
                        v.wait_ge(S["xn"], 1)
                        cp.dve_context(v)
                        def square_sums(q):
                            v.wait_ge(S["qk_sq"], q + 1)
                            nc.vector.tensor_reduce(mu[:].rearrange("p (a q g) -> p a q g", a=2, q=NT)[:, :, q],
                                                    qk2[:, :, q].rearrange("p a (g d) -> p a g d", d=D3), AX.X,
                                                    ALU.add).then_inc(S["qk_ss"], 1)

                        for q in range(NT):
                            v.wait_ge(S["qkv"], q + 1)
                            tt(qk[:, :, q], bank[q][:, 0:256].rearrange("p (a c) -> p a c", a=2),
                               W("l3_bqkv", n=256).rearrange("p (a c) -> p a c", a=2), ALU.add).then_inc(S["qk"], 1)
                            if q:
                                square_sums(q - 1)
                        square_sums(NT - 1)
                        for q in range(NT):
                            tt(vt[:, q, 0:H3, 0:D3], bank[q][:, 256:384].rearrange("p (h d) -> p h d", d=D3),
                               W("l3_bqkv", lo=256).rearrange("p (h d) -> p h d", d=D3), ALU.add).then_inc(S["vt"], 1)
                        q3 = qk[:].rearrange("p a q (g d) -> p (a q g) d", d=D3)
                        s3 = qk2[:].rearrange("p a q (g d) -> p (a q g) d", d=D3)
                        wide = lambda z: z[:, :, None].to_broadcast([128, z.shape[1], D3])
                        parts = [(n, part, slice(GH * part, GH * part + GH)) for n, part in enumerate((1, 0))]
                        for n, part, g0 in parts:
                            v.wait_ge(S["qk_rs"], n + 1)
                            tt(q3[:, g0], q3[:, g0], wide(var[:, g0]), ALU.mult).then_inc(S["qk_n"], 1)
                        gain, shift = (W(f"l3_{n}").rearrange("p (a c) -> p a c", a=2) for n in ("gamma", "beta"))
                        for n, part, g0 in parts:
                            v.wait_ge(S["qk_n"], n + 1)
                            tt(qk2[:, part], qk[:, part], gain[:, part:part + 1].to_broadcast([128, NT, D]),
                               ALU.mult).then_inc(S["qk_g"], 1)
                        for n, part, g0 in parts:
                            v.wait_ge(S["qk_g"], n + 1)
                            tt(qk2[:, part], qk2[:, part], shift[:, part:part + 1].to_broadcast([128, NT, D]),
                               ALU.add).then_inc(S["qkn"], 1)
                        v.wait_ge(S["qkn"], 2)

                        def soft_centre():
                            nc.vector.tensor_reduce(mx[:], s3, AX.X, ALU.max).then_inc(S["soft_m"], 1)
                            v.wait_ge(S["soft_m"], 1)
                            tt(s3, s3, wide(mx), ALU.subtract).then_inc(S["soft_c"], 1)

                        def soft_divide():
                            v.wait_ge(S["soft_e"], 1)
                            nc.vector.tensor_reduce(mu[:], s3, AX.X, ALU.add).then_inc(S["soft_s"], 1)
                            v.wait_ge(S["soft_s"], 1)
                            nc.vector.reciprocal(mu[:], mu[:]).then_inc(S["soft_r"], 1)
                            v.wait_ge(S["soft_r"], 1)
                            tt(s3, s3, wide(mu), ALU.mult).then_inc(S["soft"], 1)

                        def mask_kv():
                            v.wait_ge(S["kv"], 1)
                            tt(kvm[:], bank[6][:, 0:H3 * 9].rearrange("p (h d) -> p h d", d=9),
                               C("headcol")[:, :, None].to_broadcast([128, H3, 9]), ALU.mult).then_inc(S["kvm"], 1)

                        def linear_scale():
                            v.wait_ge(S["lin"], 1)
                            for f in range(2):
                                r = nc.vector.tensor_copy(ol[:, 2 * f:2 * f + 2],
                                                          bank[6 + f][:].rearrange("p (q c) -> p q c", q=2)[:, :, 0:H3 * 9]
                                                          .rearrange("p q (h d) -> p q h d", d=9))
                            r.then_inc(S["ol"], 1)
                            v.wait_ge(S["ol"], 1)
                            ts(zi[:], ol[:, :, :, D3], 1e-6, None, ALU.add).then_inc(S["zi"], 1)
                            v.wait_ge(S["zi"], 1)
                            nc.vector.reciprocal(zi[:], zi[:]).then_inc(S["zi"], 1)
                            v.wait_ge(S["zi"], 2)
                            tt(zi[:], zi[:], alpha[:, 1][:, None, :].to_broadcast([128, NT, H3]), ALU.mult).then_inc(S["zi"], 1)
                            v.wait_ge(S["zi"], 3)
                            tt(ol[:, :, :, 0:D3].rearrange("p q h d -> p (q h) d"), ol[:, :, :, 0:D3].rearrange("p q h d -> p (q h) d"),
                               zi[:].rearrange("p q h -> p (q h)")[:, :, None].to_broadcast([128, NT * H3, D3]),
                               ALU.mult).then_inc(S["ol2"], 1)

                        soft_centre()
                        ff = cp.dve(v)
                        for p in range(N // 2):
                            pair = (2 * p, 2 * p + 1)
                            for n in pair:
                                v.wait_ge(S["sc"], n + 1)
                                if n >= RM:
                                    v.wait_ge(S["nmx"], n - RM + 1)
                                    v.wait_ge(S["kept"], n - RM + 1)
                                nc.vector.max(m8[n % RM][:, 0], sc[n % RS][:]).then_inc(S["top"], 1)
                            for k in range(TOPK // 8):
                                for n in pair:
                                    w = wk_[n % 2]
                                    v.wait_ge(S["top"], tops(n, k))
                                    nc.vector.match_replace(w[:], m8[n % RM][:, k], sc[n % RS][:] if k == 0 else w[:],
                                                            -3e38).then_inc(S["rest"], 1)
                                for n in pair:
                                    v.wait_ge(S["rest"], rests(n, k))
                                    nc.vector.max(m8[n % RM][:, k + 1], wk_[n % 2][:]).then_inc(S["top"], 1)
                            if p > 2 and (2 * p - 4) % H3 == 0:
                                outputs(v, (2 * p - 4) // H3 - 1)
                            if p == 2:
                                soft_divide()
                            if p == 4:
                                mask_kv()
                            if p == 6:
                                linear_scale()
                            if p >= FIRST:
                                next(ff, None)
                            if p == OPEN + 2:
                                for _ in ff:
                                    pass
                                opening = op.dve(v)
                                next(opening)
                        for n in (N - 2, N - 1):
                            v.wait_ge(S["top"], tops(n, 3))
                            v.wait_ge(S["ex"], n + 1)
                            v.wait_ge(S["pp"], n)
                            v.wait_ge(S["turned"], n - 1)
                            stt(pp[n % 2][:], sc[n % RS][:], m8[n % RM][:, 3, 0:1], ex[n % RM][:], ALU.is_ge,
                                ALU.mult).then_inc(S["pp"], 1)
                        outputs(v, NT - 1)
                        for _ in opening:
                            pass
                        v.wait_ge(S["s"], 1)
                        v.wait_ge(S["gate"], 1)
                        stt(sq[:], bank[4][:], W("l3_bproj"), cp.th[:], ALU.add, ALU.mult).then_inc(S["m"], 1)
                        v.wait_ge(S["m"], 1)
                        tt(x[:], x[:], sq[:], ALU.add).then_inc(S["x_new"], 1)

                    @block.gpsimd
                    def _(g):
                        def smallest_exponent(n):
                            g.wait_ge(S["top"], tops(n, 0))
                            if n >= RM:
                                g.wait_ge(S["ex"], n - RM + 1)
                            nc.gpsimd.tensor_scalar(nmx[n % RM][:], m8[n % RM][:, 0, 0:1], -SC, None, ALU.mult).then_inc(S["nmx"], 1)

                        nc.gpsimd.memset(vt[:, :, H3:, :], 0.0).then_inc(S["zeros"], 1)
                        smallest_exponent(0)
                        smallest_exponent(1)
                        for n in range(N - 2):
                            g.wait_ge(S["top"], tops(n, 3))
                            if n >= 2:
                                g.wait_ge(S["turned"], n - 1)
                            nc.gpsimd.tensor_scalar(pp[n % 2][:], sc[n % RS][:], m8[n % RM][:, 3, 0:1], None,
                                                    ALU.is_ge).then_inc(S["kept"], 1)
                            if n % 2 == 0 and n + 2 < N:
                                smallest_exponent(n + 2)
                                smallest_exponent(n + 3)
                            g.wait_ge(S["kept"], n + 1)
                            g.wait_ge(S["ex"], n + 1)
                            nc.gpsimd.tensor_tensor(pp[n % 2][:], pp[n % 2][:], ex[n % RM][:], ALU.mult).then_inc(S["pp"], 1)
                            if n in cycles:
                                cp.gpsimd(g, cycles.index(n))
                S.clear()

        class Opening:

            def __init__(self, S, tiles, kb, qb, sums, b2, b3):
                self.S, self.kb, self.qb, self.sums, self.b2, self.b3 = S, kb, qb, sums, b2, b3
                self.sq, self.rs, self.ksq, self.qsq, self.rk, self.rq, self.kn, self.beta = tiles

            def pe(self, pe):
                S = self.S
                pe.wait_ge(S["x0"], 16)
                mm(self.b2[:], C("centre"), x0).then_inc(S["op_xc"], 1)
                yield
                pe.wait_ge(S["op_sq"], 1)
                mm(self.b3[:], C("mean"), self.sq[:]).then_inc(S["op_var"], 1)
                yield
                pe.wait_ge(S["op_xn"], 1)
                mm(self.b2[:], W("l0_Wbeta"), xn0).then_inc(S["op_b"], 1)
                mm(self.b3[:], W("l0_Wg"), xn0).then_inc(S["op_g"], 1)
                yield
                mm(self.kb[:], W("l0_Wk"), xn0).then_inc(S["op_k"], 1)
                yield
                mm(self.qb[:], W("l0_Wq"), xn0).then_inc(S["op_q"], 1)
                yield
                pe.wait_ge(S["op_ksq"], 1)
                mm(self.sums[:], C("head8"), self.ksq[:]).then_inc(S["op_kss"], 1)
                yield
                pe.wait_ge(S["op_qsq"], 1)
                pe.wait_ge(S["op_beta"], 1)
                mm(self.b2[:], C("head8"), self.qsq[:]).then_inc(S["op_qss"], 1)

            def act(self, a):
                S = self.S
                a.wait_ge(S["op_xc"], 1)
                act(self.sq[:], self.b2[:], ACT.Square).then_inc(S["op_sq"], 1)
                yield
                a.wait_ge(S["op_var"], 1)
                act(self.rs[:], self.b3[:], ACT.Ln, bias=C("eps5")).then_inc(S["op_ln"], 1)
                a.wait_ge(S["op_ln"], 1)
                act(self.rs[:], self.rs[:], ACT.Exp, scale=-0.5).then_inc(S["op_rs"], 1)
                yield
                a.wait_ge(S["op_b"], 1)
                act(self.beta[:], self.b2[:], ACT.Tanh, scale=0.5).then_inc(S["op_beta"], 1)
                yield
                a.wait_ge(S["op_g"], 1)
                act(sg, self.b3[:], ACT.Silu).then_inc(S["op_sg"], 1)
                a.wait_ge(S["op_k"], 1)
                act(self.ksq[:], self.kb[:], ACT.Square).then_inc(S["op_ksq"], 1)
                yield
                a.wait_ge(S["op_q"], 1)
                act(self.qsq[:], self.qb[:], ACT.Square).then_inc(S["op_qsq"], 1)
                yield
                a.wait_ge(S["op_kss"], 1)
                act(self.rk[:], self.sums[:], ACT.Ln, scale=NORM_SCALE, bias=C("floor")).then_inc(S["op_rk_ln"], 1)
                a.wait_ge(S["op_qss"], 1)
                act(self.rq[:], self.b2[:], ACT.Ln, scale=NORM_SCALE, bias=C("floor")).then_inc(S["op_rq_ln"], 1)
                a.wait_ge(S["op_rk_ln"], 1)
                act(self.rk[:], self.rk[:], ACT.Exp, scale=-0.5, bias=C("norm_back")).then_inc(S["op_rk"], 1)
                a.wait_ge(S["op_rq_ln"], 1)
                act(self.rq[:], self.rq[:], ACT.Exp, scale=-0.5, bias=C("norm_back")).then_inc(S["op_rq"], 1)

            def dve(self, v):
                S = self.S
                v.wait_ge(S["op_rs"], 1)
                tt(xn0, self.b2[:], self.rs[:], ALU.mult).then_inc(S["op_xn"], 1)
                yield
                v.wait_ge(S["op_rk"], 1)
                ts(self.rk[:], self.rk[:], 1e12, None, ALU.min).then_inc(S["op_rk_c"], 1)
                v.wait_ge(S["op_rk_c"], 1)
                stt(self.kn[:], self.kb[:], 0.5, self.rk[:], ALU.mult, ALU.mult).then_inc(S["op_kn"], 1)
                v.wait_ge(S["op_rq"], 1)
                ts(self.rq[:], self.rq[:], 1e12, None, ALU.min).then_inc(S["op_rq_c"], 1)
                v.wait_ge(S["op_rq_c"], 1)
                tt(qn, self.qb[:], self.rq[:], ALU.mult).then_inc(S["op_qn"], 1)
                yield
                v.wait_ge(S["op_beta"], 1)
                v.wait_ge(S["op_kn"], 1)
                stt(u, self.beta[:], 1.0, self.kn[:], ALU.add, ALU.mult).then_inc(S["op_u"], 1)
                v.wait_ge(S["op_u"], 1)
                tt(wk, u, self.rk[:], ALU.mult).then_inc(S["op_wk"], 1)

        with ExitStack() as c0:
            S = Steps(nc, c0, "first")
            op = Opening(S, [sb(f"first{i}", [128, T], c0) for i in range(8)], *bank[0:5])
            with nc.Block(no_gpsimd_drain=True) as block:
                @block.sync
                def _(sp):
                    sp.dma_start(x0, x_in[0]).then_inc(S["x0"], 16)

                @block.tensor
                def _(pe):
                    for _ in op.pe(pe):
                        pass

                @block.scalar
                def _(a):
                    for _ in op.act(a):
                        pass

                @block.vector
                def _(v):
                    for _ in op.dve(v):
                        pass
            S.clear()

        with nc.Fori(0, B) as b:
            with ExitStack() as c:
                S = Steps(nc, c, "l0")
                t = lambda n: sb("l0_" + n, [128, T], c)
                sq, rs = t("sq"), t("rs")
                pr = [t(f"pr{i}") for i in range(2)]
                dec = [t(f"dec{i}") for i in range(2)]
                src = [t(f"src{i}") for i in range(2)]
                st = [t(f"st{i}") for i in range(2)]
                sq8 = [t(f"sq8{i}") for i in range(2)]
                og, osb = t("og"), t("osb")
                m = t("m")
                lo = Norm(S, "on", osb[:], og[:], sq[:], rs[:], bank[2:6],
                          W("l0_ln_g"), W("l0_ln_b"))
                cp = Coupling(S, "L0", 0, c, (bank[0], bank[1]), xn0)
                with nc.Block(no_gpsimd_drain=True) as block:
                    @block.sync
                    def _(sp):
                        sp.dma_start(out[b], x[:]).then_inc(S["out"], 16)
                        sp.wait_ge(S["out"], 16)

                    @block.tensor
                    def _(pe):
                        def gather(i):
                            pe.wait_ge(S["sq8"], i + 1)
                            mm(bank[6][:], C(f"reduce{i}"), sq8[i % 2][:], i == 0, i == 7).then_inc(S["gathered"], 1)

                        ff = cp.pe(pe)
                        for i in range(9):
                            if i < 8:
                                if i >= 2:
                                    pe.wait_ge(S["pr"], i - 1)
                                    pe.wait_ge(S["src"], i - 1)
                                mm(bank[2 + i % 2][:], W(f"l0_Wkr{i}"), xn0).then_inc(S["kr"], 1)
                                mm(bank[4 + i % 2][:], W(f"l0_Wvr{i}"), xn0).then_inc(S["vr"], 1)
                            if i:
                                next(ff, None)
                            if i >= 2:
                                gather(i - 2)
                            if i:
                                next(ff, None)
                        gather(7)
                        for _ in ff:
                            pass
                        pe.wait_ge(S["osb"], 1)
                        lo.pe(pe)
                        keep_clock(bank[6], 1)
                        pe.wait_ge(S["og2"], 1)
                        mm(bank[7][:], W("l0_Wout"), og[:]).then_inc(S["s"], 1)

                    @block.scalar
                    def _(a):
                        nc.scalar.preload_act_table_set("gelu_and_others")
                        ff = cp.act(a)
                        for i in range(8):
                            next(ff, None)
                            a.wait_ge(S["pr"], i + 1)
                            if i >= 2:
                                a.wait_ge(S["st"], i - 1)
                            act(dec[i % 2][:], pr[i % 2][:], ACT.Identity, scale=-1.0, bias=C("one")).then_inc(S["dec"], 1)
                            next(ff, None)
                        a.wait_ge(S["gathered"], 8)
                        act(osb[:], bank[6][:], ACT.Copy).then_inc(S["osb"], 1)
                        for _ in ff:
                            pass
                        nc.scalar.preload_act_table_set("natural_log_exp_and_others")
                        lo.act(a)
                        cp.act_silu(a)

                    @block.vector
                    def _(v):
                        cp.dve_context(v)

                        def scan(i):
                            v.wait_ge(S["dec"], i + 1)
                            v.wait_ge(S["src"], i + 1)
                            if i >= 2:
                                v.wait_ge(S["sq8"], i - 1)
                            nc.vector.tensor_tensor_scan(st[i % 2][:], dec[i % 2][:], src[i % 2][:], 0.0,
                                                         ALU.mult, ALU.add).then_inc(S["st"], 1)

                        ff = cp.dve(v)
                        for i in range(8):
                            v.wait_ge(S["kr"], i + 1)
                            if i >= 2:
                                v.wait_ge(S["dec"], i - 1)
                            tt(pr[i % 2][:], bank[2 + i % 2][:], wk, ALU.mult).then_inc(S["pr"], 1)
                            if i:
                                scan(i - 1)
                            v.wait_ge(S["vr"], i + 1)
                            if i >= 2:
                                v.wait_ge(S["st"], i - 1)
                            tt(src[i % 2][:], bank[4 + i % 2][:], u, ALU.mult).then_inc(S["src"], 1)
                            next(ff, None)
                            next(ff, None)
                        scan(7)
                        for _ in ff:
                            pass
                        v.wait_ge(S["osb"], 1)
                        lo.dve(v)
                        v.wait_ge(S["on"], 1)
                        tt(og[:], og[:], sg, ALU.mult).then_inc(S["og2"], 1)
                        v.wait_ge(S["gate"], 1)
                        v.wait_ge(S["s"], 1)
                        tt(m[:], bank[7][:], cp.th[:], ALU.mult).then_inc(S["sg_m"], 1)
                        v.wait_ge(S["sg_m"], 1)
                        v.wait_ge(S["out"], 16)
                        tt(x[:], x0, m[:], ALU.add).then_inc(S["x_new"], 1)

                    @block.gpsimd
                    def _(g):
                        for i in range(8):
                            g.wait_ge(S["st"], i + 1)
                            if i >= 2:
                                g.wait_ge(S["gathered"], i - 1)
                            nc.gpsimd.tensor_tensor(sq8[i % 2][:], st[i % 2][:], qn, ALU.mult).then_inc(S["sq8"], 1)
                S.clear()

            if upto >= 1:
                layer1()
            if upto >= 2:
                layer2()
            if upto >= 3:
                layer3()

        with ExitStack() as c:
            S = Steps(nc, c, "store")
            with nc.Block(no_gpsimd_drain=True) as block:
                @block.sync
                def _(sp):
                    sp.dma_start(out[B], x[:]).then_inc(S["out"], 16)
                    sp.wait_ge(S["out"], 16)


def by_channels(x):
    return np.ascontiguousarray(np.concatenate([x, x[:1]]).transpose(0, 2, 1))


def columns(parts):
    at, found = 0, {}
    for k, v in parts.items():
        found[k] = (at, v.shape[0], v.shape[1])
        at += v.shape[1]
    return found


def kernel(**inputs):
    import numpy as _np
    import concourse.bacc as _bacc
    from concourse.bass_utils import run_bass_kernel_spmd as _run

    a = {k: _np.asarray(v) for k, v in inputs.items()}
    w, c = weights(a), constants()
    arrays = {"x": by_channels(a["L0_attn_x"]), "weights": packed(w), "consts": packed(c)}
    nc = _bacc.Bacc("TRN2", target_bir_lowering=False, num_devices=1)
    args = [nc.dram_tensor(n + "_dram", v.shape, F32, kind="ExternalInput").ap() for n, v in arrays.items()]
    out = nc.dram_tensor("out_dram", (B + 1, D, T), F32, kind="ExternalOutput").ap()
    build(nc, *args, out, columns(w), columns(c))
    r = _run(nc, [{n + "_dram": v for n, v in arrays.items()}], core_ids=[0])
    return _np.ascontiguousarray(r.results[0]["out_dram"][1:].transpose(0, 2, 1))
```
